# Optimizing a Trainium2 kernel written in Bass

```python
import numpy as np
import jax
import jax.numpy as jnp

def _softmax(x, axis=-1):
    return jax.nn.softmax(x, axis=axis)

def _gelu(x):
    return jax.nn.gelu(x, approximate=True)

def _silu(x):
    return jax.nn.silu(x)

def _sigmoid(x):
    return jax.nn.sigmoid(x)

def _layernorm(x, axis=-1, eps=1e-05):
    m = jnp.mean(x, axis=axis, keepdims=True)
    v = jnp.var(x, axis=axis, keepdims=True)
    return (x - m) / jnp.sqrt(v + eps)

def _scatter_add(tgt, idx, src, axis=0):
    return tgt.at[idx].add(src)

def _segment_sum(src, seg, n):
    return jax.ops.segment_sum(src, seg, n)
kernel_name = 'mk_vit_tower_postln_d4_tok_img768_r4_bf567a'

def setup_inputs(seed: int=0):
    np.random.seed(seed)
    _w = jnp.asarray

    def _rec_inputs():
        import jax
        import jax.numpy as jnp
        _rk = jax.random.key(seed)
        x = -0.00016672 + 0.999947 * jax.random.normal(jax.random.fold_in(_rk, 1), (16, 3, 96, 96), jnp.float32)
        return x
    x = _rec_inputs()

    def _L0_tok_setup():
        import jax, jax.numpy as jnp
        import numpy as np
        P = 16

        def _patchify(x, p):
            B, C, H, W = x.shape
            gh, gw = (H // p, W // p)
            x = x.reshape(B, C, gh, p, gw, p)
            x = x.transpose(0, 2, 4, 1, 3, 5)
            return x.reshape(B, gh * gw, C * p * p)
        key = jax.random.key(seed)
        k1, k2, k3, k4, k5 = jax.random.split(key, 5)
        B, C, H, Wd = (64, 3, 96, 96)
        emb = 192
        L = H // P * (Wd // P)
        return {'x': jax.random.normal(k1, (B, C, H, Wd), dtype=jnp.float32), 'W': jax.random.normal(k2, (emb, C * P * P), dtype=jnp.float32) * 0.02, 'b': jax.random.normal(k3, (emb,), dtype=jnp.float32) * 0.02, 'cls_tok': jax.random.normal(k4, (1, 1, emb), dtype=jnp.float32), 'pos_emb': jax.random.normal(k5, (1, L + 1, emb), dtype=jnp.float32)}
    _L0_tok_all = _L0_tok_setup()
    _L0_tok_in = {k: v for k, v in _L0_tok_all.items() if k in ('W', 'b', 'cls_tok', 'pos_emb')}
    del _L0_tok_all

    def _L0_attn_setup():
        import jax, jax.numpy as jnp
        import numpy as np
        B, S, D, H = (8, 256, 192, 12)
        HS = D // H
        key = jax.random.key(seed)
        k1, k2, k3 = jax.random.split(key, 3)
        x = jax.random.normal(k1, (B, S, D), dtype=jnp.float32)
        W_attn = jax.random.normal(k2, (D, 3 * H * HS), dtype=jnp.float32) * 0.02
        b_attn = jnp.zeros((3 * H * HS,), dtype=jnp.float32)
        W_proj = jax.random.normal(k3, (H * HS, D), dtype=jnp.float32) * 0.02
        b_proj = jnp.zeros((D,), dtype=jnp.float32)
        return {'x': x, 'W_attn': W_attn, 'b_attn': b_attn, 'W_proj': W_proj, 'b_proj': b_proj}
    _L0_attn_all = _L0_attn_setup()
    _L0_attn_in = {k: v for k, v in _L0_attn_all.items() if k in ('W_attn', 'b_attn', 'W_proj', 'b_proj')}
    del _L0_attn_all

    def _L0_ffn_setup():
        import jax, jax.numpy as jnp
        import numpy as np
        EPS = 1e-06

        def l2_normalize(x, axis):
            norm = jnp.sqrt(jnp.square(x).sum(axis=axis, keepdims=True))
            return x * (1.0 / (norm + EPS))
        key = jax.random.key(seed)
        ks = jax.random.split(key, 8)
        b, m, d = (32, 256, 192)
        n, p = (8, 4)
        h = d // 8
        X = jax.random.normal(ks[0], (b, m, d), dtype=jnp.float32)
        std_slot = float(np.sqrt(2.0 / (d + n * p)))
        slot_params = jax.random.normal(ks[1], (d, n, p), dtype=jnp.float32) * std_slot
        scale = jnp.ones((), dtype=jnp.float32)
        W_down = jax.random.normal(ks[2], (n, d, h), dtype=jnp.float32) * float(np.sqrt(1.0 / d))
        b_down = jnp.zeros((n, h), dtype=jnp.float32)
        W_up = jax.random.normal(ks[3], (n, h, d), dtype=jnp.float32) * float(np.sqrt(1.0 / h))
        b_up = jnp.zeros((n, d), dtype=jnp.float32)
        return {'X': X, 'slot_params': slot_params, 'scale': scale, 'W_down': W_down, 'b_down': b_down, 'W_up': W_up, 'b_up': b_up}
    _L0_ffn_all = _L0_ffn_setup()
    _L0_ffn_in = {k: v for k, v in _L0_ffn_all.items() if k in ('slot_params', 'scale', 'W_down', 'b_down', 'W_up', 'b_up')}
    del _L0_ffn_all

    def _L1_attn_setup():
        import jax, jax.numpy as jnp
        import numpy as np
        import math
        N_EMBD = 192
        N_HEAD = 12
        HEAD_DIM = N_EMBD // N_HEAD

        def rope_cache(T, dim):
            inv_freq = 1.0 / 10000.0 ** (2.0 * jnp.arange(dim // 2, dtype=jnp.float32) / dim)
            angles = jnp.arange(T, dtype=jnp.float32)[:, None] * inv_freq[None, :]
            return jnp.stack((jnp.cos(angles), jnp.sin(angles)), axis=-1)

        def apply_rope(x, rope):
            B, H, T, D = x.shape
            xp = x.reshape(B, H, T, D // 2, 2)
            x1, x2 = (xp[..., 0], xp[..., 1])
            cos = rope[None, None, :, :, 0]
            sin = rope[None, None, :, :, 1]
            out = jnp.stack((x1 * cos - x2 * sin, x1 * sin + x2 * cos), axis=-1)
            return out.reshape(B, H, T, D)
        key = jax.random.key(seed)
        ks = jax.random.split(key, 9)
        s = 0.02
        d = N_EMBD
        return {'x': jax.random.normal(ks[0], (2, 1024, d), dtype=jnp.float32), 'Wq': jax.random.normal(ks[1], (d, d), dtype=jnp.float32) * s, 'bq': jnp.zeros((d,), jnp.float32), 'Wk': jax.random.normal(ks[2], (d, d), dtype=jnp.float32) * s, 'bk': jnp.zeros((d,), jnp.float32), 'Wv': jax.random.normal(ks[3], (d, d), dtype=jnp.float32) * s, 'bv': jnp.zeros((d,), jnp.float32), 'Wp': jax.random.normal(ks[4], (d, d), dtype=jnp.float32) * s, 'bp': jnp.zeros((d,), jnp.float32)}
    _L1_attn_all = _L1_attn_setup()
    _L1_attn_in = {k: v for k, v in _L1_attn_all.items() if k in ('Wq', 'bq', 'Wk', 'bk', 'Wv', 'bv', 'Wp', 'bp')}
    del _L1_attn_all

    def _L1_ffn_setup():
        import math
        import jax, jax.numpy as jnp
        import numpy as np
        NUM_EXPERTS = 8
        TOP_K = 2
        CAPACITY_FACTOR = 1.25
        H = 192
        INNER = 768
        B, S = (2, 512)
        key = jax.random.key(seed)
        ks = jax.random.split(key, 9)
        scale = 0.02
        x = jax.random.normal(ks[0], (B, S, H), dtype=jnp.float32)
        Wr = jax.random.normal(ks[1], (H, NUM_EXPERTS), dtype=jnp.float32) * scale
        w1 = jax.random.normal(ks[2], (NUM_EXPERTS, H, INNER), dtype=jnp.float32) * scale
        w3 = jax.random.normal(ks[3], (NUM_EXPERTS, H, INNER), dtype=jnp.float32) * scale
        w2 = jax.random.normal(ks[4], (NUM_EXPERTS, INNER, H), dtype=jnp.float32) * scale
        s1 = jax.random.normal(ks[5], (H, INNER), dtype=jnp.float32) * scale
        s3 = jax.random.normal(ks[6], (H, INNER), dtype=jnp.float32) * scale
        s2 = jax.random.normal(ks[7], (INNER, H), dtype=jnp.float32) * scale
        return {'x': x, 'Wr': Wr, 'w1': w1, 'w3': w3, 'w2': w2, 's1': s1, 's3': s3, 's2': s2}
    _L1_ffn_all = _L1_ffn_setup()
    _L1_ffn_in = {k: v for k, v in _L1_ffn_all.items() if k in ('Wr', 'w1', 'w3', 'w2', 's1', 's3', 's2')}
    del _L1_ffn_all

    def _L2_attn_setup():
        import jax, jax.numpy as jnp
        import numpy as np
        D_MODEL = 192
        NHEAD = 12
        HEAD_DIM = D_MODEL // NHEAD
        MAX_REL = 16
        B, T = (4, 256)
        key = jax.random.key(seed)
        ks = jax.random.split(key, 6)
        s = 0.02
        return {'x': jax.random.normal(ks[0], (B, T, D_MODEL), dtype=jnp.float32), 'qkv_w': jax.random.normal(ks[1], (3 * D_MODEL, D_MODEL), dtype=jnp.float32) * s, 'qkv_b': jax.random.normal(ks[2], (3 * D_MODEL,), dtype=jnp.float32) * s, 'out_w': jax.random.normal(ks[3], (D_MODEL, D_MODEL), dtype=jnp.float32) * s, 'out_b': jax.random.normal(ks[4], (D_MODEL,), dtype=jnp.float32) * s, 'rel_pos_emb': jax.random.normal(ks[5], (2 * MAX_REL + 1, HEAD_DIM), dtype=jnp.float32)}
    _L2_attn_all = _L2_attn_setup()
    _L2_attn_in = {k: v for k, v in _L2_attn_all.items() if k in ('qkv_w', 'qkv_b', 'out_w', 'out_b', 'rel_pos_emb')}
    del _L2_attn_all

    def _L2_ffn_setup():
        import jax, jax.numpy as jnp
        import numpy as np
        ALPHA = 1.702
        LIMIT = 7.0
        TOP_K = 2
        B, S, H, E, I = (2, 256, 192, 8, 192)
        key = jax.random.key(seed)
        ks = jax.random.split(key, 7)
        scale = 0.02
        return {'hidden_states': jax.random.normal(ks[0], (B, S, H), dtype=jnp.float32), 'Wr': jax.random.normal(ks[1], (H, E), dtype=jnp.float32) * scale, 'br': jax.random.normal(ks[2], (E,), dtype=jnp.float32) * scale, 'Wgu': jax.random.normal(ks[3], (E, H, 2 * I), dtype=jnp.float32) * scale, 'bgu': jax.random.normal(ks[4], (E, 2 * I), dtype=jnp.float32) * scale, 'Wd': jax.random.normal(ks[5], (E, I, H), dtype=jnp.float32) * scale, 'bd': jax.random.normal(ks[6], (E, H), dtype=jnp.float32) * scale}
    _L2_ffn_all = _L2_ffn_setup()
    _L2_ffn_in = {k: v for k, v in _L2_ffn_all.items() if k in ('Wr', 'br', 'Wgu', 'bgu', 'Wd', 'bd')}
    del _L2_ffn_all

    def _L3_attn_setup():
        import jax, jax.numpy as jnp
        import numpy as np
        EPS = 1e-05

        def _ste(y, x):
            return x + jax.lax.stop_gradient(y - x)

        def _absmean_quant(x):
            s = jnp.mean(jnp.abs(x)) + EPS
            u = x / s
            q = _ste(jnp.round(jnp.clip(u, -1.0, 1.0)), u)
            return (q, s)

        def _ternary_weight(w):
            s = jnp.mean(jnp.abs(w)) + EPS
            u = w / s
            return _ste(jnp.round(jnp.clip(u, -1.0, 1.0)), u) * s

        def _l1norm(x):
            return x / (jnp.sum(jnp.abs(x), axis=-1, keepdims=True) + EPS)
        key = jax.random.key(seed)
        k1, k2 = jax.random.split(key)
        B, N, C = (16, 1025, 192)
        x = jax.random.normal(k1, (B, N, C), dtype=jnp.float32)
        w_qkv = jax.random.normal(k2, (3 * C, C), dtype=jnp.float32) * 0.02
        return {'x': x, 'w_qkv': w_qkv}
    _L3_attn_all = _L3_attn_setup()
    _L3_attn_in = {k: v for k, v in _L3_attn_all.items() if k in ('w_qkv',)}
    del _L3_attn_all

    def _L3_ffn_setup():
        import jax, jax.numpy as jnp
        import numpy as np
        DIM = 192
        MOE_INTER = 512
        N_EXPERTS = 16
        TOP_K = 2
        SHARED_INTER = 2 * 512
        ROUTE_SCALE = 1.0
        B, S = (8, 196)
        key = jax.random.key(seed)
        ks = jax.random.split(key, 8)
        sc = 0.02
        return {'x': jax.random.normal(ks[0], (B, S, DIM), jnp.float32), 'gate_w': jax.random.normal(ks[1], (N_EXPERTS, DIM), jnp.float32) * sc, 'w1': jax.random.normal(ks[2], (N_EXPERTS, MOE_INTER, DIM), jnp.float32) * sc, 'w2': jax.random.normal(ks[3], (N_EXPERTS, DIM, MOE_INTER), jnp.float32) * sc, 'w3': jax.random.normal(ks[4], (N_EXPERTS, MOE_INTER, DIM), jnp.float32) * sc, 'sw1': jax.random.normal(ks[5], (SHARED_INTER, DIM), jnp.float32) * sc, 'sw2': jax.random.normal(ks[6], (DIM, SHARED_INTER), jnp.float32) * sc, 'sw3': jax.random.normal(ks[7], (SHARED_INTER, DIM), jnp.float32) * sc}
    _L3_ffn_all = _L3_ffn_setup()
    _L3_ffn_in = {k: v for k, v in _L3_ffn_all.items() if k in ('gate_w', 'w1', 'w2', 'w3', 'sw1', 'sw2', 'sw3')}
    del _L3_ffn_all
    return {'x': x, 'L0_tok_W': _L0_tok_in['W'], 'L0_tok_b': _L0_tok_in['b'], 'L0_tok_cls_tok': _L0_tok_in['cls_tok'], 'L0_tok_pos_emb': _L0_tok_in['pos_emb'], 'L0_attn_W_attn': _L0_attn_in['W_attn'], 'L0_attn_b_attn': _L0_attn_in['b_attn'], 'L0_attn_W_proj': _L0_attn_in['W_proj'], 'L0_attn_b_proj': _L0_attn_in['b_proj'], 'L0_ffn_slot_params': _L0_ffn_in['slot_params'], 'L0_ffn_scale': _L0_ffn_in['scale'], 'L0_ffn_W_down': _L0_ffn_in['W_down'], 'L0_ffn_b_down': _L0_ffn_in['b_down'], 'L0_ffn_W_up': _L0_ffn_in['W_up'], 'L0_ffn_b_up': _L0_ffn_in['b_up'], 'L1_attn_Wq': _L1_attn_in['Wq'], 'L1_attn_bq': _L1_attn_in['bq'], 'L1_attn_Wk': _L1_attn_in['Wk'], 'L1_attn_bk': _L1_attn_in['bk'], 'L1_attn_Wv': _L1_attn_in['Wv'], 'L1_attn_bv': _L1_attn_in['bv'], 'L1_attn_Wp': _L1_attn_in['Wp'], 'L1_attn_bp': _L1_attn_in['bp'], 'L1_ffn_Wr': _L1_ffn_in['Wr'], 'L1_ffn_w1': _L1_ffn_in['w1'], 'L1_ffn_w3': _L1_ffn_in['w3'], 'L1_ffn_w2': _L1_ffn_in['w2'], 'L1_ffn_s1': _L1_ffn_in['s1'], 'L1_ffn_s3': _L1_ffn_in['s3'], 'L1_ffn_s2': _L1_ffn_in['s2'], 'L2_attn_qkv_w': _L2_attn_in['qkv_w'], 'L2_attn_qkv_b': _L2_attn_in['qkv_b'], 'L2_attn_out_w': _L2_attn_in['out_w'], 'L2_attn_out_b': _L2_attn_in['out_b'], 'L2_attn_rel_pos_emb': _L2_attn_in['rel_pos_emb'], 'L2_ffn_Wr': _L2_ffn_in['Wr'], 'L2_ffn_br': _L2_ffn_in['br'], 'L2_ffn_Wgu': _L2_ffn_in['Wgu'], 'L2_ffn_bgu': _L2_ffn_in['bgu'], 'L2_ffn_Wd': _L2_ffn_in['Wd'], 'L2_ffn_bd': _L2_ffn_in['bd'], 'L3_attn_w_qkv': _L3_attn_in['w_qkv'], 'L3_ffn_gate_w': _L3_ffn_in['gate_w'], 'L3_ffn_w1': _L3_ffn_in['w1'], 'L3_ffn_w2': _L3_ffn_in['w2'], 'L3_ffn_w3': _L3_ffn_in['w3'], 'L3_ffn_sw1': _L3_ffn_in['sw1'], 'L3_ffn_sw2': _L3_ffn_in['sw2'], 'L3_ffn_sw3': _L3_ffn_in['sw3']}

def reference(x, L0_tok_W, L0_tok_b, L0_tok_cls_tok, L0_tok_pos_emb, L0_attn_W_attn, L0_attn_b_attn, L0_attn_W_proj, L0_attn_b_proj, L0_ffn_slot_params, L0_ffn_scale, L0_ffn_W_down, L0_ffn_b_down, L0_ffn_W_up, L0_ffn_b_up, L1_attn_Wq, L1_attn_bq, L1_attn_Wk, L1_attn_bk, L1_attn_Wv, L1_attn_bv, L1_attn_Wp, L1_attn_bp, L1_ffn_Wr, L1_ffn_w1, L1_ffn_w3, L1_ffn_w2, L1_ffn_s1, L1_ffn_s3, L1_ffn_s2, L2_attn_qkv_w, L2_attn_qkv_b, L2_attn_out_w, L2_attn_out_b, L2_attn_rel_pos_emb, L2_ffn_Wr, L2_ffn_br, L2_ffn_Wgu, L2_ffn_bgu, L2_ffn_Wd, L2_ffn_bd, L3_attn_w_qkv, L3_ffn_gate_w, L3_ffn_w1, L3_ffn_w2, L3_ffn_w3, L3_ffn_sw1, L3_ffn_sw2, L3_ffn_sw3):
    import jax
    import jax.numpy as jnp

    def _L0_tok_ref(x, W, b, cls_tok, pos_emb):
        import jax, jax.numpy as jnp
        import numpy as np
        P = 16

        def _patchify(x, p):
            B, C, H, W = x.shape
            gh, gw = (H // p, W // p)
            x = x.reshape(B, C, gh, p, gw, p)
            x = x.transpose(0, 2, 4, 1, 3, 5)
            return x.reshape(B, gh * gw, C * p * p)
        B = x.shape[0]
        patches = _patchify(x, P)
        emb = jnp.einsum('blk,ek->ble', patches, W) + b
        cls = jnp.broadcast_to(cls_tok, (B, 1, cls_tok.shape[-1]))
        emb = jnp.concatenate([cls, emb], axis=1)
        return emb + pos_emb

    def _L0_attn_ref(x, W_attn, b_attn, W_proj, b_proj):
        import jax, jax.numpy as jnp
        import numpy as np
        B, S, D, H = (8, 256, 192, 12)
        HS = D // H
        b, s, d = x.shape
        qkv = (x @ W_attn + b_attn).reshape(b, s, 3, H, HS)
        q, k, v = (qkv[:, :, 0], qkv[:, :, 1], qkv[:, :, 2])
        scale = jnp.sqrt(jnp.asarray(HS, dtype=x.dtype))
        scores = jnp.einsum('bqhd,bkhd->bhqk', q, k) / scale
        causal = jnp.tril(jnp.ones((s, s), dtype=bool))
        scores = jnp.where(causal, scores, -jnp.inf)
        attn = jax.nn.softmax(scores, axis=-1)
        out = jnp.einsum('bhqk,bkhd->bqhd', attn, v).reshape(b, s, H * HS)
        return out @ W_proj + b_proj

    def _L0_ffn_ref(X, slot_params, scale, W_down, b_down, W_up, b_up):
        import jax, jax.numpy as jnp
        import numpy as np
        EPS = 1e-06

        def l2_normalize(x, axis):
            norm = jnp.sqrt(jnp.square(x).sum(axis=axis, keepdims=True))
            return x * (1.0 / (norm + EPS))
        b, m, d = X.shape
        _, n, p = slot_params.shape
        Xn = l2_normalize(X, axis=-1)
        sp = l2_normalize(slot_params, axis=1) * scale
        logits = jnp.einsum('bmd,dnp->bmnp', Xn, sp)
        D = jax.nn.softmax(logits, axis=1)
        C = jax.nn.softmax(logits.reshape(b, m, n * p), axis=2).reshape(b, m, n, p)
        X_tilde = jnp.einsum('bmd,bmnp->bnpd', Xn, D)
        H = jax.nn.gelu(jnp.einsum('bnpd,ndh->bnph', X_tilde, W_down) + b_down[None, :, None, :], approximate=False)
        Y_tilde = jnp.einsum('bnph,nhd->bnpd', H, W_up) + b_up[None, :, None, :]
        Y = jnp.einsum('bnpd,bmnp->bmd', Y_tilde, C)
        return Y

    def _L1_attn_ref(x, Wq, bq, Wk, bk, Wv, bv, Wp, bp):
        import jax, jax.numpy as jnp
        import numpy as np
        import math
        N_EMBD = 192
        N_HEAD = 12
        HEAD_DIM = N_EMBD // N_HEAD

        def rope_cache(T, dim):
            inv_freq = 1.0 / 10000.0 ** (2.0 * jnp.arange(dim // 2, dtype=jnp.float32) / dim)
            angles = jnp.arange(T, dtype=jnp.float32)[:, None] * inv_freq[None, :]
            return jnp.stack((jnp.cos(angles), jnp.sin(angles)), axis=-1)

        def apply_rope(x, rope):
            B, H, T, D = x.shape
            xp = x.reshape(B, H, T, D // 2, 2)
            x1, x2 = (xp[..., 0], xp[..., 1])
            cos = rope[None, None, :, :, 0]
            sin = rope[None, None, :, :, 1]
            out = jnp.stack((x1 * cos - x2 * sin, x1 * sin + x2 * cos), axis=-1)
            return out.reshape(B, H, T, D)
        B, T, C = x.shape
        H, D = (N_HEAD, HEAD_DIM)

        def heads(W, b):
            return (x @ W.T + b).reshape(B, T, H, D).transpose(0, 2, 1, 3)
        q = heads(Wq, bq)
        k = heads(Wk, bk)
        v = heads(Wv, bv)
        rope = rope_cache(T, D)
        q = apply_rope(q, rope)
        k = apply_rope(k, rope)
        att = jnp.einsum('bhqd,bhkd->bhqk', q, k) * (1.0 / math.sqrt(D))
        causal = jnp.tril(jnp.ones((T, T), dtype=bool))
        att = jnp.where(causal[None, None], att, -jnp.inf)
        att = jax.nn.softmax(att, axis=-1)
        y = jnp.einsum('bhqk,bhkd->bhqd', att, v)
        y = y.transpose(0, 2, 1, 3).reshape(B, T, C)
        return y @ Wp.T + bp

    def _L1_ffn_ref(x, Wr, w1, w3, w2, s1, s3, s2):
        import math
        import jax, jax.numpy as jnp
        import numpy as np
        NUM_EXPERTS = 8
        TOP_K = 2
        CAPACITY_FACTOR = 1.25
        H = 192
        INNER = 768
        B, S = (2, 512)
        b, s, h = x.shape
        n = b * s
        flat = x.reshape(n, h)
        logits = flat @ Wr
        probs = jax.nn.softmax(logits, axis=-1)
        topk_p, topk_i = jax.lax.top_k(probs, TOP_K)
        topk_p = topk_p / jnp.clip(topk_p.sum(-1, keepdims=True), 1e-09)
        capacity = max(1, math.ceil(n * TOP_K / NUM_EXPERTS * CAPACITY_FACTOR))
        onehot = topk_i[None, :, :] == jnp.arange(NUM_EXPERTS)[:, None, None]
        w_tok = jnp.sum(topk_p[None] * onehot, axis=-1)
        assigned = jnp.any(onehot, axis=-1)
        score = jnp.where(assigned, w_tok, -jnp.inf)
        order = jnp.argsort(-score, axis=1)[:, :capacity]
        score_sel = jnp.take_along_axis(score, order, axis=1)
        valid = jnp.isfinite(score_sel)
        weight_sel = jnp.where(valid, score_sel, 0.0)
        dispatch = flat[order]
        gate = jax.nn.silu(jnp.einsum('ech,ehi->eci', dispatch, w1))
        up = jnp.einsum('ech,ehi->eci', dispatch, w3)
        expert_out = jnp.einsum('eci,eih->ech', gate * up, w2)
        expert_out = expert_out * weight_sel[..., None]
        routed = jnp.zeros((n, h), dtype=flat.dtype)
        routed = routed.at[order.reshape(-1)].add(expert_out.reshape(-1, h))
        shared = jax.nn.silu(flat @ s1) * (flat @ s3) @ s2
        out = routed + shared
        return out.reshape(b, s, h)

    def _L2_attn_ref(x, qkv_w, qkv_b, out_w, out_b, rel_pos_emb):
        import jax, jax.numpy as jnp
        import numpy as np
        D_MODEL = 192
        NHEAD = 12
        HEAD_DIM = D_MODEL // NHEAD
        MAX_REL = 16
        B, T = (4, 256)
        Bx, Tx, _ = x.shape
        scale = HEAD_DIM ** (-0.5)
        qkv = x @ qkv_w.T + qkv_b
        qkv = qkv.reshape(Bx, Tx, 3, NHEAD, HEAD_DIM)
        q = qkv[:, :, 0].transpose(0, 2, 1, 3)
        k = qkv[:, :, 1].transpose(0, 2, 1, 3)
        v = qkv[:, :, 2].transpose(0, 2, 1, 3)
        attn_scores = jnp.einsum('bhtd,bhsd->bhts', q, k)
        rng = jnp.arange(Tx)
        rel_pos = jnp.clip(rng[None, :] - rng[:, None], -MAX_REL, MAX_REL) + MAX_REL
        rel_emb = rel_pos_emb[rel_pos]
        rel_scores = jnp.einsum('bhtd,tsd->bhts', q, rel_emb)
        attn = jax.nn.softmax((attn_scores + rel_scores) * scale, axis=-1)
        out = jnp.einsum('bhts,bhsd->bhtd', attn, v)
        out = out.transpose(0, 2, 1, 3).reshape(Bx, Tx, D_MODEL)
        return out @ out_w.T + out_b

    def _L2_ffn_ref(hidden_states, Wr, br, Wgu, bgu, Wd, bd):
        import jax, jax.numpy as jnp
        import numpy as np
        ALPHA = 1.702
        LIMIT = 7.0
        TOP_K = 2
        B, S, H, E, I = (2, 256, 192, 8, 192)
        logits = jnp.einsum('bsh,he->bse', hidden_states, Wr) + br
        topk_vals, topk_idx = jax.lax.top_k(logits, TOP_K)
        router_scores = jax.nn.softmax(topk_vals, axis=-1)
        gu = jnp.einsum('bsh,ehf->bsef', hidden_states, Wgu) + bgu
        gu = jnp.minimum(gu, LIMIT)
        gate = gu[..., :I]
        up = jnp.maximum(gu[..., I:], -LIMIT)
        glu = gate * jax.nn.sigmoid(gate * ALPHA)
        activated = (up + 1.0) * glu
        down = jnp.einsum('bsei,eih->bseh', activated, Wd) + bd
        sel = jnp.take_along_axis(down, topk_idx[..., None], axis=2)
        output = jnp.sum(sel * router_scores[..., None], axis=2)
        return output

    def _L3_attn_ref(x, w_qkv):
        import jax, jax.numpy as jnp
        import numpy as np
        EPS = 1e-05

        def _ste(y, x):
            return x + jax.lax.stop_gradient(y - x)

        def _absmean_quant(x):
            s = jnp.mean(jnp.abs(x)) + EPS
            u = x / s
            q = _ste(jnp.round(jnp.clip(u, -1.0, 1.0)), u)
            return (q, s)

        def _ternary_weight(w):
            s = jnp.mean(jnp.abs(w)) + EPS
            u = w / s
            return _ste(jnp.round(jnp.clip(u, -1.0, 1.0)), u) * s

        def _l1norm(x):
            return x / (jnp.sum(jnp.abs(x), axis=-1, keepdims=True) + EPS)
        B, N, C = x.shape
        H = 12
        D = C // H
        scale = D ** (-0.5)
        wq = _ternary_weight(w_qkv)
        qkv = jnp.einsum('bnc,oc->bno', x, wq)
        qkv = qkv.reshape(B, N, 3, H, D).transpose(2, 0, 3, 1, 4)
        q, k, v = (qkv[0], qkv[1], qkv[2])
        q_q, q_s = _absmean_quant(_l1norm(q))
        k_q, k_s = _absmean_quant(_l1norm(k))
        v_q, v_s = _absmean_quant(_l1norm(v))
        attn = jnp.einsum('bhnd,bhmd->bhnm', q_q, k_q) * scale
        attn = attn * q_s * k_s
        attn_q, qk_s = _absmean_quant(attn)
        out = jnp.einsum('bhnm,bhmd->bhnd', attn_q, v_q)
        out = out.transpose(0, 2, 1, 3).reshape(B, N, C)
        return out * qk_s * v_s

    def _L3_ffn_ref(x, gate_w, w1, w2, w3, sw1, sw2, sw3):
        import jax, jax.numpy as jnp
        import numpy as np
        DIM = 192
        MOE_INTER = 512
        N_EXPERTS = 16
        TOP_K = 2
        SHARED_INTER = 2 * 512
        ROUTE_SCALE = 1.0
        B, S = (8, 196)
        Bb, Ss, D = x.shape
        xf = x.reshape(-1, D)
        T = xf.shape[0]
        scores = jax.nn.softmax(xf @ gate_w.T, axis=-1)
        topw, topi = jax.lax.top_k(scores, TOP_K)
        topw = topw * ROUTE_SCALE
        comb = jnp.zeros((T, N_EXPERTS), xf.dtype).at[jnp.arange(T)[:, None], topi].set(topw)
        h = jax.nn.silu(jnp.einsum('td,eid->tei', xf, w1)) * jnp.einsum('td,eid->tei', xf, w3)
        h = h * comb[:, :, None]
        y = jnp.einsum('tei,edi->td', h, w2)
        z = jax.nn.silu(xf @ sw1.T) * (xf @ sw3.T) @ sw2.T
        return (y + z).reshape(Bb, Ss, D)
    h = _L0_tok_ref(x, L0_tok_W, L0_tok_b, L0_tok_cls_tok, L0_tok_pos_emb)
    h = _layernorm(h + _L0_attn_ref(h, L0_attn_W_attn, L0_attn_b_attn, L0_attn_W_proj, L0_attn_b_proj), axis=-1)
    h = _layernorm(h + _L0_ffn_ref(h, L0_ffn_slot_params, L0_ffn_scale, L0_ffn_W_down, L0_ffn_b_down, L0_ffn_W_up, L0_ffn_b_up), axis=-1)
    h = _layernorm(h + _L1_attn_ref(h, L1_attn_Wq, L1_attn_bq, L1_attn_Wk, L1_attn_bk, L1_attn_Wv, L1_attn_bv, L1_attn_Wp, L1_attn_bp), axis=-1)
    h = _layernorm(h + _L1_ffn_ref(h, L1_ffn_Wr, L1_ffn_w1, L1_ffn_w3, L1_ffn_w2, L1_ffn_s1, L1_ffn_s3, L1_ffn_s2), axis=-1)
    h = _layernorm(h + _L2_attn_ref(h, L2_attn_qkv_w, L2_attn_qkv_b, L2_attn_out_w, L2_attn_out_b, L2_attn_rel_pos_emb), axis=-1)
    h = _layernorm(h + _L2_ffn_ref(h, L2_ffn_Wr, L2_ffn_br, L2_ffn_Wgu, L2_ffn_bgu, L2_ffn_Wd, L2_ffn_bd), axis=-1)
    h = _layernorm(h + _L3_attn_ref(h, L3_attn_w_qkv), axis=-1)
    h = _layernorm(h + _L3_ffn_ref(h, L3_ffn_gate_w, L3_ffn_w1, L3_ffn_w2, L3_ffn_w3, L3_ffn_sw1, L3_ffn_sw2, L3_ffn_sw3), axis=-1)
    return h

_drawn_inputs = setup_inputs


def setup_inputs(seed=0):
    import zlib

    import numpy as np

    out = dict(_drawn_inputs(seed))
    spreads = {'L0_attn_b_attn': (0.0, 0.306),
     'L0_attn_b_proj': (0.0, 0.1),
     'L0_ffn_b_down': (0.0, 0.403),
     'L0_ffn_b_up': (0.0, 0.1),
     'L1_attn_bq': (0.0, 0.8),
     'L1_attn_bk': (0.0, 0.8),
     'L1_attn_bv': (0.0, 0.295),
     'L1_attn_bp': (0.0, 0.1)}
    factors = {'L0_tok_b': 3.17,
     'L0_ffn_slot_params': 7.623,
     'L0_ffn_W_down': 8.0,
     'L0_ffn_W_up': 2.903,
     'L1_attn_Wq': 8.0,
     'L1_attn_Wk': 8.0,
     'L1_ffn_Wr': 4.145,
     'L1_ffn_w1': 3.596,
     'L1_ffn_w3': 3.595,
     'L1_ffn_w2': 3.566,
     'L2_attn_qkv_w': 3.195,
     'L2_attn_qkv_b': 8.0,
     'L2_attn_out_w': 3.135,
     'L2_attn_out_b': 2.894,
     'L2_attn_rel_pos_emb': 8.0,
     'L2_ffn_br': 8.0,
     'L2_ffn_bgu': 8.0,
     'L2_ffn_bd': 3.95,
     'L3_attn_w_qkv': 64.0,
     'L3_ffn_gate_w': 8.0,
     'L3_ffn_w1': 8.0,
     'L3_ffn_w2': 8.0,
     'L3_ffn_w3': 8.0,
     'L3_ffn_sw1': 8.0,
     'L3_ffn_sw2': 8.0,
     'L3_ffn_sw3': 8.0}
    for name, (base, spread) in spreads.items():
        noise = np.random.default_rng([zlib.crc32(name.encode()), seed]).standard_normal(out[name].shape)
        drawn = base * np.exp(spread * noise) if base else spread * noise
        out[name] = jnp.asarray(drawn.astype(out[name].dtype))
    for name, factor in factors.items():
        out[name] = (out[name] * factor).astype(out[name].dtype)
    return out
```

```python
from contextlib import ExitStack

import numpy as np
import concourse.bass as bass
from concourse import mybir

F32 = mybir.dt.float32
BF16 = mybir.dt.bfloat16
ACT = mybir.ActivationFunctionType
ALU = mybir.AluOpType
AX = mybir.AxisListType

B, T, D, H = 16, 37, 192, 12
HD = D // H
N = B * T
NP, PT = B // 2, 2 * T
C = D // 2
HC = H // 2
HALF = N // 2
G, GH = 4, 3
GK, GD = GH * T, GH * HD
SECOND = 64
SR = SECOND + T
BANK = 512
LN_EPS = 1e-5
L2_EPS = 1e-6
TERNARY_EPS = 1e-5
NEG = -1e30
SCALE = HD ** -0.5
MAX_REL = 16
SHIFTS = 2 * T - 1
SN, SP, SH = 8, 4, 24
SLOTS = SN * SP
CAPACITY = -(-N * 2 * 5 // (8 * 4))

FFN = {1: (6, 8, 6, 128, 1), 2: (0, 8, 2, 96, 2), 3: (8, 16, 4, 128, 1)}


SEMAPHORES = []


def alloc(nc, ctx):
    def sb(name, shape, dt=F32):
        return ctx.enter_context(nc.sbuf_tensor(name, shape, dt))

    def ps(name, shape, dt=F32):
        return ctx.enter_context(nc.psum_tensor(name, shape, dt))

    def sem(name):
        SEMAPHORES.append(nc.alloc_semaphore(name))
        return SEMAPHORES[-1]
    return sb, ps, sem


def reset_semaphores(nc):
    nc.clear_and_free_semaphores(SEMAPHORES)
    nc.all_engine_barrier()
    SEMAPHORES.clear()


def patch_embedding(nc, I, h):
    with ExitStack() as ctx:
        sb, ps, sem = alloc(nc, ctx)
        KC = I["patches"].shape[1]
        x = sb("tok_x", [128, KC, N])
        w = sb("tok_w", [128, KC, D])
        pos = sb("tok_pos", [PT, D])
        first = sb("tok_first", [PT, D])
        acc = ps("tok_acc", [PT, NP, BANK])
        loaded = sem("tok_loaded")
        small = sem("tok_small_loaded")
        summed = sem("tok_const_summed")
        product = sem("tok_product_ready")
        done = sem("tok_done")
        with nc.Block() as block:
            @block.sync
            def _(sp):
                for k in range(KC):
                    sp.dma_start(w[:, k, :], I["tok_w"][:, k, :]).then_inc(loaded, 16)
                    sp.dma_start(x[:, k, :], I["patches"][:, k, :]).then_inc(loaded, 16)
                sp.dma_start(pos[:, :], I["tok_pos"]).then_inc(small, 16)
                sp.dma_start(first[:, :], I["tok_first"]).then_inc(small, 16)

            @block.tensor
            def _(pe):
                pe.wait_ge(loaded, 32 * KC)
                for j in range(NP):
                    for k in range(KC):
                        mm = pe.matmul(acc[:, j, 0:D], lhsT=x[:, k, j * PT:(j + 1) * PT], rhs=w[:, k, :],
                                       start=(k == 0), stop=(k == KC - 1))
                    mm.then_inc(product, 1)

            @block.vector
            def _(dve):
                dve.wait_ge(small, 32)
                dve.tensor_tensor(pos[:, :], pos[:, :], first[:, :], ALU.add).then_inc(summed, 1)
                dve.wait_ge(summed, 1)
                for j in range(NP):
                    dve.wait_ge(product, j + 1)
                    dve.tensor_tensor(h[:, j, :], acc[:, j, 0:D], pos[:, :], ALU.add).then_inc(done, 1)


def to_feature_major(nc, src, dst, ident, tag):
    with ExitStack() as ctx:
        sb, ps, sem = alloc(nc, ctx)
        tp = ps(tag + "_tp", [C, 4, BANK])
        ready = sem(tag + "_tp_ready")
        copied = sem(tag + "_tp_copied")
        with nc.Block() as block:
            @block.tensor
            def _(pe):
                for half in range(2):
                    for c in range(2):
                        for q in range(NP // 2):
                            j = half * (NP // 2) + q
                            mm = pe.transpose(tp[:, 2 * half + c, q * PT:(q + 1) * PT],
                                              src[:, j, c * C:(c + 1) * C], ident[0:PT, 0:PT])
                        mm.then_inc(ready, 1)

            @block.scalar
            def _(act):
                for half in range(2):
                    for c in range(2):
                        act.wait_ge(ready, 2 * half + c + 1)
                        act.activation(dst[:, c, half * HALF:(half + 1) * HALF],
                                       tp[:, 2 * half + c, 0:HALF], ACT.Copy).then_inc(copied, 1)


def layer_norm(nc, h, tag, unit=None, power=None):
    with ExitStack() as ctx:
        sb, ps, sem = alloc(nc, ctx)
        st = sb(tag + "_stats", [PT, NP, 6])
        mv = sb(tag + "_mean_var", [PT, NP, 2])
        rstd = sb(tag + "_rstd", [PT, NP])
        sq = sb(tag + "_squares", [PT, NP, D])
        length = sb(tag + "_length", [PT, NP])
        stats = sem(tag + "_stats_ready")
        aggr = sem(tag + "_aggregated")
        eps = sem(tag + "_eps_added")
        root = sem(tag + "_root_ready")
        norm = sem(tag + "_normalised")
        summed = sem(tag + "_squares_summed")
        rooted = sem(tag + "_length_ready")
        with nc.Block() as block:
            @block.vector
            def _(dve):
                for j in range(NP):
                    dve.bn_stats(st[:, j, :], h[:, j, :]).then_inc(stats, 1)
                for j in range(NP):
                    dve.wait_ge(stats, j + 1)
                    dve.bn_aggr(mv[:, j, :], st[:, j, :]).then_inc(aggr, 1)
                dve.wait_ge(root, 1)
                for j in range(NP):
                    dve.tensor_scalar(h[:, j, :], h[:, j, :], mv[:, j, 0:1], rstd[:, j:j + 1],
                                      ALU.subtract, ALU.mult).then_inc(norm, 1)
                if unit is not None:
                    dve.wait_ge(norm, NP)
                    dve.tensor_tensor(sq[:, :, :], h[:, :, :], h[:, :, :], ALU.mult).then_inc(summed, 1)
                    dve.wait_ge(summed, 1)
                    dve.tensor_reduce(length[:, :], sq[:, :, :], AX.X, ALU.add).then_inc(summed, 1)
                    dve.wait_ge(rooted, 1)
                    dve.tensor_scalar(length[:, :], length[:, :], L2_EPS, None, ALU.add).then_inc(rooted, 1)
                    dve.wait_ge(rooted, 2)
                    dve.reciprocal(length[:, :], length[:, :]).then_inc(rooted, 1)
                    dve.wait_ge(rooted, 3)
                    dve.tensor_tensor(unit[:, :, :], h[:, :, :],
                                      length[:, :].unsqueeze(2).to_broadcast([PT, NP, D]), ALU.mult).then_inc(rooted, 1)

            @block.gpsimd
            def _(pool):
                pool.wait_ge(aggr, NP)
                pool.tensor_scalar(rstd[:, :], mv[:, :, 1], LN_EPS, None, ALU.add).then_inc(eps, 1)
                pool.wait_ge(eps, 1)
                pool.tensor_tensor(rstd[:, :], rstd[:, :], power[:, 0, :], ALU.pow).then_inc(root, 1)
                if unit is not None:
                    pool.wait_ge(summed, 2)
                    pool.tensor_tensor(length[:, :], length[:, :], power[:, 1, :], ALU.pow).then_inc(rooted, 1)


def attention(nc, I, layer, h, hT, const):
    rope, rel = layer == 1, layer == 2
    p = f"att{layer}"
    ident = const["ident"]
    kinds = ["q", "qs", "k", "ks"] if rope else ["q", "k"]
    with ExitStack() as ctx:
        sb, ps, sem = alloc(nc, ctx)
        w = {n: sb(f"{p}_w{n}", [C, 2, D]) for n in kinds + ["v"]}
        wp = sb(p + "_wp", [GD, G, D])
        bias = sb(p + "_bias", [C, 2, len(kinds)])
        bv = sb(p + "_bv", [GD, G, PT])
        bp = sb(p + "_bp", [PT, D])
        qT = sb(p + "_qT", [C, 2, N])
        kT = sb(p + "_kT", [C, 2, N])
        biases = sb(p + "_score_bias", [SR, 2, H * T])
        if rope:
            table = sb(p + "_rope", [C, 2, T])
            turned = sb(p + "_turned", [C, 2, HALF])
            straight = sb(p + "_straight", [C, 2, HALF])
        if rel:
            rbd = sb(p + "_rel", [C, HC * SHIFTS])
            grid = sb(p + "_rel_grid", [PT, 4, 2 * HC * SHIFTS])
            grid_dram = I["rel_scratch"]
        loaded = sem(p + "_loaded")
        biased = sem(p + "_score_bias_ready")
        grid_copied = sem(p + "_grid_copied")
        grid_stored = [sem(f"{p}_grid_stored{i}") for i in range(4)]

        with ExitStack() as pre:
            _, pps, psem = alloc(nc, pre)
            acc = pps(p + "_acc", [128, 8, BANK])
            product = psem(p + "_product_ready")
            taken = psem(p + "_product_taken")
            gridded = psem(p + "_grid_ready")
            kept = psem(p + "_residual_ready")
            KN = len(kinds)
            with nc.Block() as block:
                @block.sync
                def _(sp):
                    for n in kinds + ["v"]:
                        sp.dma_start(w[n][:, :, :], I[f"{p}_w{n}"]).then_inc(loaded, 16)
                    sp.dma_start(bias[:, :, :], I[p + "_bias"]).then_inc(loaded, 16)
                    sp.dma_start(wp[:, :, :], I[p + "_wp"]).then_inc(loaded, 16)
                    sp.dma_start(bv[:, :, :], I[p + "_bv"]).then_inc(loaded, 16)
                    sp.dma_start(bp[:, :], I[p + "_bp"]).then_inc(loaded, 16)
                    if rope:
                        sp.dma_start(table[:, :, :], I["rope"]).then_inc(loaded, 16)
                    if rel:
                        sp.dma_start(rbd[:, :], I["rel_blocks"]).then_inc(loaded, 16)
                    else:
                        sp.dma_start(biases[:, 0, :], I["causal"]).then_inc(biased, 16)
                    if rel:
                        for j in range(NP):
                            sp.wait_ge(grid_copied, 2 * j + 2)
                            sp.dma_start(grid_dram[j * PT:(j + 1) * PT, :], grid[:, j % 4, :]).then_inc(grid_stored[j % 4], 16)

                LOADS = 16 * (KN + 1 + 4 + rope + rel)

                @block.tensor
                def _(pe):
                    pe.wait_ge(loaded, LOADS)
                    for s in range(4):
                        co, half = s // 2, s % 2
                        for m, n in enumerate(kinds):
                            bank = (s * KN + m) % 8
                            if s * KN + m >= 8:
                                pe.wait_ge(taken, s * KN + m - 7)
                            for ci in range(2):
                                mm = pe.matmul(acc[0:C, bank, 0:HALF], lhsT=w[n][:, ci, co * C:(co + 1) * C],
                                               rhs=hT[:, ci, half * HALF:(half + 1) * HALF],
                                               start=(ci == 0), stop=(ci == 1))
                            mm.then_inc(product, 1)
                    n0 = 4 * KN
                    pe.wait_ge(taken, n0 - 7)
                    for g in range(G):
                        mm = pe.matmul(acc[0:PT, n0 % 8, 0:D], lhsT=bv[:, g, :], rhs=wp[:, g, :],
                                       start=(g == 0), stop=(g == G - 1))
                    mm.then_inc(product, 1)
                    if rel:
                        pe.wait_ge(taken, 4 * KN)
                        for j in range(NP):
                            for ci in range(2):
                                s = 2 * j + ci
                                bank = 1 + s % 6
                                if s >= 6:
                                    pe.wait_ge(grid_copied, s - 5)
                                pe.matmul(acc[0:PT, bank, 0:HC * SHIFTS], lhsT=qT[:, ci, j * PT:(j + 1) * PT],
                                          rhs=rbd[:, :], start=True, stop=True).then_inc(gridded, 1)

                @block.scalar
                def _(act):
                    if not rope:
                        act.wait_ge(loaded, LOADS)
                        for s in range(4):
                            co, half = s // 2, s % 2
                            for m, n in enumerate(kinds):
                                act.wait_ge(product, s * KN + m + 1)
                                dst = qT if n == "q" else kT
                                act.activation(dst[:, co, half * HALF:(half + 1) * HALF],
                                               acc[0:C, (s * KN + m) % 8, 0:HALF], ACT.Identity,
                                               bias=bias[:, co, m:m + 1]).then_inc(taken, 1)
                    if rel:
                        for s in range(2 * NP):
                            j, ci = s // 2, s % 2
                            act.wait_ge(gridded, s + 1)
                            if j >= 4:
                                act.wait_ge(grid_stored[j % 4], 16)
                            act.activation(grid[:, j % 4, ci * HC * SHIFTS:(ci + 1) * HC * SHIFTS],
                                           acc[0:PT, 1 + s % 6, 0:HC * SHIFTS], ACT.Copy).then_inc(grid_copied, 1)

                @block.vector
                def _(dve):
                    if rel:
                        dve.memset(biases[:, :, :], 0.0).then_inc(biased, 1)
                    dve.wait_ge(loaded, LOADS)
                    if rope:
                        for s in range(4):
                            co, half = s // 2, s % 2
                            for m in range(2):
                                dst = (qT, kT)[m]
                                for t in range(2):
                                    n = s * KN + 2 * m + t
                                    dve.wait_ge(product, n + 1)
                                    src = acc[0:C, n % 8, 0:HALF].rearrange("p (b t) -> p b t", t=T)
                                    out = (straight, turned)[t][:, m, :].rearrange("p (b t) -> p b t", t=T)
                                    dve.scalar_tensor_tensor(out, src, bias[:, co, 2 * m + t:2 * m + t + 1],
                                                             table[:, t, :].unsqueeze(1).to_broadcast([C, B // 2, T]),
                                                             ALU.add, ALU.mult).then_inc(taken, 1)
                                dve.wait_ge(taken, s * KN + 2 * m + 2)
                                dve.tensor_tensor(dst[:, co, half * HALF:(half + 1) * HALF], straight[:, m, :],
                                                  turned[:, m, :], ALU.add)
                    dve.tensor_tensor(h[:, :, :], h[:, :, :], bp[:, :].unsqueeze(1).to_broadcast([PT, NP, D]),
                                      ALU.add).then_inc(kept, 1)
                    dve.wait_ge(product, 4 * KN + 1)
                    dve.wait_ge(kept, 1)
                    dve.tensor_tensor(h[:, :, :], h[:, :, :],
                                      acc[0:PT, 4 * KN % 8, 0:D].unsqueeze(1).to_broadcast([PT, NP, D]),
                                      ALU.add).then_inc(kept, 1)

        with ExitStack() as main:
            msb, mps, msem = alloc(nc, main)
            q_stage = msb(p + "_q_stage", [C, 2, 2, PT])
            x_stage = msb(p + "_x_stage", [C, 2, 2, 2, GH, T])
            k_blocks = msb(p + "_k_blocks", [C, 2, 2, 2, HC, T])
            probs = msb(p + "_probs", [SR, 2, H * T])
            probsT = msb(p + "_probsT", [GK, 2, G, SR])
            v_blocks = msb(p + "_v_blocks", [GK, 2, 2, D])
            oT = msb(p + "_oT", [GD, 2, G, PT])
            peak = msb(p + "_peak", [SR, 2, H])
            total = msb(p + "_total", [SR, 2, H])
            s_ps = mps(p + "_s", [128, 2, BANK])
            t_ps = mps(p + "_t", [128, 2, BANK])
            v_ps = mps(p + "_v", [128, 2, BANK])
            oy_ps = mps(p + "_oy", [128, 2, BANK])
            staged = msem(p + "_staged")
            values = msem(p + "_values_ready")
            scores = msem(p + "_scores_ready")
            peaked = msem(p + "_peak_ready")
            shifted = msem(p + "_shifted")
            exped = msem(p + "_exponentials_ready")
            totaled = msem(p + "_totals_ready")
            inverted = msem(p + "_inverted")
            weighted = msem(p + "_probs_ready")
            v_ready = msem(p + "_v_blocks_ready")
            turned_s = msem(p + "_probsT_ready")
            pT_copied = msem(p + "_probsT_copied")
            o_ready = msem(p + "_outputs_ready")
            o_copied = msem(p + "_outputs_copied")
            y_ready = msem(p + "_projected")
            added = msem(p + "_added")
            rel_loaded = [msem(f"{p}_rel_loaded{k}") for k in range(2)]

            def y_of(k):
                return oy_ps[0:PT, k, G * PT:G * PT + D]

            with nc.Block() as block:
                @block.sync
                def _(sp):
                    if rel:
                        for i in range(4):
                            sp.wait_ge(grid_stored[i], 32)

                        def rel_pair(i, k, later):
                            if later:
                                sp.wait_ge(scores, 2 * i + k - 1)
                            for img in range(2):
                                src = bass.AP(grid_dram.tensor, (2 * i + k) * (PT * H * SHIFTS) + img * T * H * SHIFTS + T - 1,
                                              [[H * SHIFTS - 1, T], [SHIFTS, H], [1, T]])
                                dst = biases[img * SECOND:img * SECOND + T, k, :].rearrange("p (h t) -> p h t", h=H)
                                sp.dma_start(dst, src).then_inc(rel_loaded[k], 16)
                        for k in range(2):
                            rel_pair(0, k, False)
                        with sp.Fori(1, NP // 2) as i:
                            for k in range(2):
                                rel_pair(i, k, True)

                @block.gpsimd
                def _(pool):
                    def body(i, later):
                        for k in range(2):
                            j = 2 * i + k
                            if later:
                                pool.wait_ge(scores, j - 1)
                            pool.tensor_copy(q_stage[:, k, :, :], qT[:, :, bass.ds(j * PT, PT)]).then_inc(staged, 1)
                            for c in range(2):
                                pool.tensor_copy(x_stage[:, k, c, :, :, :],
                                                 hT[:, c, bass.ds(j * PT, PT)].rearrange("p (b t) -> p b t", b=2)
                                                 .unsqueeze(2).to_broadcast([C, 2, GH, T])).then_inc(staged, 1)
                                pool.tensor_tensor(k_blocks[:, k, c, :, :, :],
                                                   kT[:, c, bass.ds(j * PT, PT)].rearrange("p (b t) -> p b t", b=2)
                                                   .unsqueeze(2).to_broadcast([C, 2, HC, T]),
                                                   const["own_head"][:, :].unsqueeze(1).unsqueeze(3)
                                                   .to_broadcast([C, 2, HC, T]), ALU.mult).then_inc(staged, 1)
                    body(0, False)
                    with pool.Fori(1, NP // 2) as i:
                        body(i, True)

                @block.tensor
                def _(pe):
                    if not rel:
                        pe.wait_ge(biased, 16)

                    def body(i, later):
                        for k in range(2):
                            j = 2 * i + k
                            pe.wait_ge(staged, 5 * j + 5)
                            if later:
                                pe.wait_ge(v_ready, j - 1)
                            for img in range(2):
                                for c in range(2):
                                    mm = pe.matmul(v_ps[0:GK, k, img * D:(img + 1) * D],
                                                   lhsT=x_stage[:, k, c, img, :, :].rearrange("p a t -> p (a t)"),
                                                   rhs=w["v"][:, c, :], start=(c == 0), stop=(c == 1))
                            mm.then_inc(values, 1)
                            if later:
                                pe.wait_ge(shifted, j - 1)
                            if rel:
                                pe.wait_ge(rel_loaded[k], 32 * i + 32)
                            pe.matmul(s_ps[0:SR, k, 0:H * T], lhsT=ident[0:SR, 0:SR],
                                      rhs=biases[:, k if rel else 0, :], start=True, stop=False,
                                      skip_group_check=True)
                            for c in range(2):
                                for img in range(2):
                                    mm = pe.matmul(s_ps[img * SECOND:img * SECOND + T, k, c * HC * T:(c + 1) * HC * T],
                                                   lhsT=q_stage[:, k, c, img * T:(img + 1) * T],
                                                   rhs=k_blocks[:, k, c, img, :, :].rearrange("p a t -> p (a t)"),
                                                   start=False, stop=True, skip_group_check=True)
                            mm.then_inc(scores, 1)
                        for k in range(2):
                            j = 2 * i + k
                            pe.wait_ge(weighted, j + 1)
                            if later:
                                pe.wait_ge(pT_copied, j - 1)
                            for g in range(G):
                                mm = pe.transpose(t_ps[0:GK, k, g * SR:(g + 1) * SR],
                                                  probs[:, k, g * GK:(g + 1) * GK], ident[0:SR, 0:SR])
                            mm.then_inc(turned_s, 1)
                            pe.wait_ge(pT_copied, j + 1)
                            pe.wait_ge(v_ready, j + 1)
                            if later:
                                pe.wait_ge(added, j - 1)
                            for img in range(2):
                                for g in range(G):
                                    mm = pe.matmul(oy_ps[0:GD, k, g * PT + img * T:g * PT + (img + 1) * T],
                                                   lhsT=v_blocks[:, k, img, g * GD:(g + 1) * GD],
                                                   rhs=probsT[:, k, g, img * SECOND:img * SECOND + T],
                                                   start=True, stop=True)
                            mm.then_inc(o_ready, 1)
                            pe.wait_ge(o_copied, j + 1)
                            for g in range(G):
                                mm = pe.matmul(y_of(k), lhsT=oT[:, k, g, :], rhs=wp[:, g, :],
                                               start=(g == 0), stop=(g == G - 1))
                            mm.then_inc(y_ready, 1)
                    body(0, False)
                    with pe.Fori(1, NP // 2) as i:
                        body(i, True)

                @block.scalar
                def _(act):
                    def body(i, later):
                        for k in range(2):
                            act.wait_ge(shifted, 2 * i + k + 1)
                            act.activation(probs[:, k, :], probs[:, k, :], ACT.Exp, scale=SCALE).then_inc(exped, 1)
                        for k in range(2):
                            j = 2 * i + k
                            act.wait_ge(turned_s, j + 1)
                            if later:
                                act.wait_ge(o_ready, j - 1)
                            act.activation(probsT[:, k, :, :].rearrange("p g s -> p (g s)"), t_ps[0:GK, k, 0:G * SR],
                                           ACT.Copy).then_inc(pT_copied, 1)
                            act.wait_ge(o_ready, j + 1)
                            if later:
                                act.wait_ge(y_ready, j - 1)
                            act.activation(oT[:, k, :, :].rearrange("p g s -> p (g s)"), oy_ps[0:GD, k, 0:G * PT],
                                           ACT.Copy).then_inc(o_copied, 1)
                    body(0, False)
                    with act.Fori(1, NP // 2) as i:
                        body(i, True)

                @block.vector
                def _(dve):
                    def heads(t):
                        return t.rearrange("p (h t) -> p h t", h=H)

                    def body(i, later):
                        for k in range(2):
                            j = 2 * i + k
                            dve.wait_ge(scores, j + 1)
                            dve.tensor_reduce(peak[:, k, :], heads(s_ps[0:SR, k, 0:H * T]), AX.X, ALU.max).then_inc(peaked, 1)
                            dve.wait_ge(peaked, j + 1)
                            if later:
                                dve.wait_ge(turned_s, j - 1)
                            dve.tensor_tensor(heads(probs[:, k, :]), heads(s_ps[0:SR, k, 0:H * T]),
                                              peak[:, k, :].unsqueeze(2).to_broadcast([SR, H, T]),
                                              ALU.subtract).then_inc(shifted, 1)
                            dve.wait_ge(values, j + 1)
                            if later:
                                dve.wait_ge(o_ready, j - 1)
                            dve.tensor_tensor(v_blocks[:, k, :, :],
                                              v_ps[0:GK, k, 0:2 * D].rearrange("p (b d) -> p b d", b=2),
                                              const["own_key"][:, :].unsqueeze(1).to_broadcast([GK, 2, D]),
                                              ALU.mult).then_inc(v_ready, 1)
                        for k in range(2):
                            j = 2 * i + k
                            dve.wait_ge(exped, j + 1)
                            dve.tensor_reduce(total[:, k, :], heads(probs[:, k, :]), AX.X, ALU.add).then_inc(totaled, 1)
                            dve.wait_ge(totaled, j + 1)
                            dve.reciprocal(total[:, k, :], total[:, k, :]).then_inc(inverted, 1)
                            dve.wait_ge(inverted, j + 1)
                            dve.tensor_tensor(heads(probs[:, k, :]), heads(probs[:, k, :]),
                                              total[:, k, :].unsqueeze(2).to_broadcast([SR, H, T]),
                                              ALU.mult).then_inc(weighted, 1)
                        for k in range(2):
                            j = 2 * i + k
                            dve.wait_ge(y_ready, j + 1)
                            dve.tensor_tensor(h[:, bass.ds(j, 1), :].rearrange("p a d -> p (a d)"),
                                              h[:, bass.ds(j, 1), :].rearrange("p a d -> p (a d)"),
                                              y_of(k), ALU.add).then_inc(added, 1)
                    body(0, False)
                    with dve.Fori(1, NP // 2) as i:
                        body(i, True)


def soft_mixture(nc, I, h, unit, unitT, const):
    ident = const["ident"]
    with ExitStack() as ctx:
        sb, ps, sem = alloc(nc, ctx)
        slots = sb("sm_slots", [C, 2, SLOTS])
        squares = sb("sm_squares", [C, 2, SLOTS])
        length = sb("sm_length", [C, 2, SP])
        scale = sb("sm_scale", [C, 1])
        down = sb("sm_down", [C, 2, D])
        bdown = sb("sm_bdown", [C, 2])
        up = sb("sm_up", [C, 2, D])
        bup = sb("sm_bup", [128, D])
        own_expert = sb("sm_own_expert", [C, 2, SLOTS])
        own_image = sb("sm_own_image", [PT, 2])
        own_image4 = sb("sm_own_image4", [PT, 2, 4])
        logitsT = sb("sm_logitsT", [SLOTS, N])
        dispT = sb("sm_dispT", [SLOTS, N])
        comb = sb("sm_comb", [PT, NP, SLOTS])
        peak = sb("sm_peak", [SLOTS, B])
        total = sb("sm_total", [SLOTS, B])
        cpeak = sb("sm_cpeak", [PT, NP])
        ctotal = sb("sm_ctotal", [PT, NP])
        dispatch = sb("sm_dispatch", [PT, NP, 2, SLOTS])
        combine = sb("sm_combine", [PT, NP, 4, SLOTS])
        combineT = sb("sm_combineT", [128, NP, PT])
        slotT = sb("sm_slotT", [C, 2, B * SLOTS])
        hidden = sb("sm_hidden", [C, 2, B * SLOTS])
        masked = sb("sm_masked", [C, 2, B * SLOTS])
        out = sb("sm_out", [128, 4, D])
        l_ps = ps("sm_l_ps", [128, 2, BANK])
        t_ps = ps("sm_t_ps", [128, 2, BANK])
        c_ps = ps("sm_c_ps", [128, 2, BANK])
        y_ps = ps("sm_y_ps", [128, 2, BANK])
        loaded = sem("sm_loaded")
        slots_ready = sem("sm_slots_step")
        rooted = sem("sm_slot_lengths_ready")
        logits = sem("sm_logits_ready")
        kept = sem("sm_logits_kept")
        step = sem("sm_vector_step")
        exped = sem("sm_exponentials_ready")
        shifted = sem("sm_shifted")
        turned = sem("sm_transposed")
        disp = sem("sm_dispT_ready")
        dready = sem("sm_dispatch_ready")
        cready = sem("sm_combine_ready")
        slotted = sem("sm_slot_inputs_ready")
        slots_kept = sem("sm_slot_inputs_kept")
        hid = sem("sm_hidden_product_ready")
        gelued = sem("sm_gelu_ready")
        mready = sem("sm_masked_ready")
        oready = sem("sm_out_product_ready")
        okept = sem("sm_out_kept")
        cturned = sem("sm_combine_transposed")
        ckept = sem("sm_combineT_kept")
        yready = sem("sm_result_ready")
        added = sem("sm_added")

        with nc.Block() as block:
            @block.sync
            def _(sp):
                for dst, name in ((slots, "sm_slots"), (scale, "sm_scale"), (down, "sm_down"), (bdown, "sm_bdown"),
                                  (up, "sm_up"), (bup, "sm_bup"), (own_expert, "sm_own_expert"),
                                  (own_image, "sm_own_image"), (own_image4, "sm_own_image4")):
                    src = I[name]
                    sp.dma_start(dst[tuple(slice(None) for _ in dst.shape)], src).then_inc(loaded, 16)

            @block.gpsimd
            def _(pool):
                pool.wait_ge(slots_ready, 2)
                pool.tensor_tensor(length[:, :, :], length[:, :, :],
                                   const["half"][:, :, :], ALU.pow).then_inc(rooted, 1)

            @block.tensor
            def _(pe):
                pe.wait_ge(slots_ready, 6)
                for half in range(2):
                    for c in range(2):
                        mm = pe.matmul(l_ps[0:SLOTS, half, 0:HALF], lhsT=slots[:, c, :],
                                       rhs=unitT[:, c, half * HALF:(half + 1) * HALF], start=(c == 0), stop=(c == 1))
                    mm.then_inc(logits, 1)
                pe.wait_ge(kept, 2)
                for j in range(NP):
                    mm = pe.transpose(t_ps[0:PT, 0, j * SLOTS:(j + 1) * SLOTS], logitsT[:, j * PT:(j + 1) * PT],
                                      ident[0:SLOTS, 0:SLOTS])
                mm.then_inc(turned, 1)
                pe.wait_ge(disp, 1)
                for j in range(NP):
                    mm = pe.transpose(t_ps[0:PT, 1, j * SLOTS:(j + 1) * SLOTS], dispT[:, j * PT:(j + 1) * PT],
                                      ident[0:SLOTS, 0:SLOTS])
                mm.then_inc(turned, 1)
                pe.wait_ge(dready, 1)
                for c in range(2):
                    for j in range(NP):
                        mm = pe.matmul(l_ps[0:C, c, j * 2 * SLOTS:(j + 1) * 2 * SLOTS], lhsT=unit[:, j, c * C:(c + 1) * C],
                                       rhs=dispatch[:, j, :, :].rearrange("p b s -> p (b s)"), start=True, stop=True)
                    mm.then_inc(slotted, 1)
                pe.wait_ge(cready, 2)
                for j in range(NP):
                    mm = pe.transpose(c_ps[:, j // 4, (j % 4) * PT:(j % 4 + 1) * PT],
                                      combine[:, j, :, :].rearrange("p b s -> p (b s)"), ident[0:PT, 0:PT])
                mm.then_inc(cturned, 1)
                pe.wait_ge(slots_kept, 2)
                for e in range(2):
                    for c in range(2):
                        mm = pe.matmul(l_ps[0:C, e, :], lhsT=down[:, c, e * C:(e + 1) * C], rhs=slotT[:, c, :],
                                       start=(c == 0), stop=(c == 1))
                    mm.then_inc(hid, 1)
                pe.wait_ge(mready, 2)
                for q in range(4):
                    for e in range(2):
                        mm = pe.matmul(t_ps[:, q // 2, (q % 2) * D:(q % 2 + 1) * D], lhsT=masked[:, e, q * 128:(q + 1) * 128],
                                       rhs=up[:, e, :], start=(e == 0), stop=(e == 1))
                mm.then_inc(oready, 1)
                pe.wait_ge(okept, 2)
                pe.wait_ge(ckept, 2)
                for j in range(NP):
                    if j >= 2:
                        pe.wait_ge(added, j - 1)
                    pe.matmul(y_ps[0:PT, j % 2, 0:D], lhsT=combineT[:, j, :], rhs=out[:, j // 2, :],
                              start=True, stop=True).then_inc(yready, 1)

            @block.scalar
            def _(act):
                act.wait_ge(shifted, 1)
                act.activation(dispT[:, :], dispT[:, :], ACT.Exp).then_inc(exped, 1)
                act.wait_ge(shifted, 2)
                act.activation(comb[:, :, :], comb[:, :, :], ACT.Exp).then_inc(exped, 1)
                for c in range(2):
                    act.wait_ge(slotted, c + 1)
                    act.activation(slotT[:, c, :], l_ps[0:C, c, :], ACT.Copy).then_inc(slots_kept, 1)
                act.wait_ge(cturned, 1)
                for g in range(2):
                    act.activation(combineT[:, 4 * g:4 * g + 4, :].rearrange("p j t -> p (j t)"), c_ps[:, g, 0:4 * PT],
                                   ACT.Copy).then_inc(ckept, 1)
                for e in range(2):
                    act.wait_ge(hid, e + 1)
                    act.activation(hidden[:, e, :], l_ps[0:C, e, :], ACT.Gelu, bias=bdown[:, e:e + 1]).then_inc(gelued, 1)

            @block.vector
            def _(dve):
                dve.wait_ge(loaded, 16 * 9)
                dve.tensor_tensor(squares[:, :, :], slots[:, :, :], slots[:, :, :], ALU.mult).then_inc(slots_ready, 1)
                dve.wait_ge(slots_ready, 1)
                dve.tensor_reduce(length[:, :, :], squares[:, :, :].rearrange("p c (n s) -> p c s n", n=SN), AX.X,
                                  ALU.add).then_inc(slots_ready, 1)
                dve.wait_ge(rooted, 1)
                dve.tensor_scalar(length[:, :, :], length[:, :, :], L2_EPS, None, ALU.add).then_inc(slots_ready, 1)
                dve.wait_ge(slots_ready, 3)
                dve.reciprocal(length[:, :, :], length[:, :, :]).then_inc(slots_ready, 1)
                dve.wait_ge(slots_ready, 4)
                dve.tensor_scalar(length[:, :, :], length[:, :, :], scale[:, 0:1], None, ALU.mult).then_inc(slots_ready, 1)
                dve.wait_ge(slots_ready, 5)
                dve.tensor_tensor(slots[:, :, :].rearrange("p c (n s) -> p c n s", n=SN),
                                  slots[:, :, :].rearrange("p c (n s) -> p c n s", n=SN),
                                  length[:, :, :].unsqueeze(2).to_broadcast([C, 2, SN, SP]), ALU.mult).then_inc(slots_ready, 1)
                for half in range(2):
                    dve.wait_ge(logits, half + 1)
                    dve.tensor_copy(logitsT[:, half * HALF:(half + 1) * HALF], l_ps[0:SLOTS, half, 0:HALF]).then_inc(kept, 1)
                dve.wait_ge(kept, 2)
                by_image = logitsT[:, :].rearrange("p (b t) -> p b t", t=T)
                disp_by_image = dispT[:, :].rearrange("p (b t) -> p b t", t=T)
                dve.tensor_reduce(peak[:, :], by_image, AX.X, ALU.max).then_inc(step, 1)
                dve.wait_ge(step, 1)
                dve.tensor_tensor(disp_by_image, by_image, peak[:, :].unsqueeze(2).to_broadcast([SLOTS, B, T]),
                                  ALU.subtract).then_inc(shifted, 1)
                dve.wait_ge(turned, 1)
                tok = t_ps[0:PT, 0, 0:NP * SLOTS].rearrange("p (j s) -> p j s", s=SLOTS)
                dve.tensor_reduce(cpeak[:, :], tok, AX.X, ALU.max).then_inc(step, 1)
                dve.wait_ge(step, 2)
                dve.tensor_tensor(comb[:, :, :], tok, cpeak[:, :].unsqueeze(2).to_broadcast([PT, NP, SLOTS]),
                                  ALU.subtract).then_inc(shifted, 1)
                dve.wait_ge(exped, 1)
                dve.tensor_reduce(total[:, :], disp_by_image, AX.X, ALU.add).then_inc(step, 1)
                dve.wait_ge(step, 3)
                dve.reciprocal(total[:, :], total[:, :]).then_inc(step, 1)
                dve.wait_ge(step, 4)
                dve.tensor_tensor(disp_by_image, disp_by_image, total[:, :].unsqueeze(2).to_broadcast([SLOTS, B, T]),
                                  ALU.mult).then_inc(disp, 1)
                dve.wait_ge(exped, 2)
                dve.tensor_reduce(ctotal[:, :], comb[:, :, :], AX.X, ALU.add).then_inc(step, 1)
                dve.wait_ge(step, 5)
                dve.reciprocal(ctotal[:, :], ctotal[:, :]).then_inc(step, 1)
                dve.wait_ge(step, 6)
                dve.tensor_tensor(comb[:, :, :], comb[:, :, :], ctotal[:, :].unsqueeze(2).to_broadcast([PT, NP, SLOTS]),
                                  ALU.mult).then_inc(step, 1)
                dve.wait_ge(turned, 2)
                dve.tensor_tensor(dispatch[:, :, :, :],
                                  t_ps[0:PT, 1, 0:NP * SLOTS].rearrange("p (j s) -> p j s", s=SLOTS)
                                  .unsqueeze(2).to_broadcast([PT, NP, 2, SLOTS]),
                                  own_image[:, :].unsqueeze(1).unsqueeze(3).to_broadcast([PT, NP, 2, SLOTS]),
                                  ALU.mult).then_inc(dready, 1)
                dve.wait_ge(step, 7)
                for par in range(2):
                    dve.tensor_tensor(combine[:, par:NP:2, :, :],
                                      comb[:, par:NP:2, :].unsqueeze(2).to_broadcast([PT, NP // 2, 4, SLOTS]),
                                      own_image4[:, par, :].unsqueeze(1).unsqueeze(3).to_broadcast([PT, NP // 2, 4, SLOTS]),
                                      ALU.mult).then_inc(cready, 1)
                for e in range(2):
                    dve.wait_ge(gelued, e + 1)
                    dve.tensor_tensor(masked[:, e, :].rearrange("p (b s) -> p b s", s=SLOTS),
                                      hidden[:, e, :].rearrange("p (b s) -> p b s", s=SLOTS),
                                      own_expert[:, e, :].unsqueeze(1).to_broadcast([C, B, SLOTS]), ALU.mult).then_inc(mready, 1)
                dve.wait_ge(oready, 1)
                for g in range(2):
                    dve.tensor_tensor(out[:, 2 * g:2 * g + 2, :], t_ps[:, g, 0:2 * D].rearrange("p (q d) -> p q d", q=2),
                                      bup[:, :].unsqueeze(1).to_broadcast([128, 2, D]), ALU.add).then_inc(okept, 1)
                for j in range(NP):
                    dve.wait_ge(yready, j + 1)
                    dve.tensor_tensor(h[:, j, :], h[:, j, :], y_ps[0:PT, j % 2, 0:D], ALU.add).then_inc(added, 1)


def router(nc, I, layer, hT, comb, comb_dram, const):
    shared, E, upe, M, per_body = FFN[layer]
    p = f"rt{layer}"
    ident = const["ident"]
    with ExitStack() as ctx:
        sb, ps, sem = alloc(nc, ctx)
        w = sb(p + "_w", [C, 2, E])
        order = sb(p + "_order", [PT, E])
        score = sb(p + "_score", [PT, NP, E])
        rest = sb(p + "_rest", [PT, NP, E])
        place = sb(p + "_place", [PT, NP, E])
        hot = [sb(f"{p}_hot{r}", [PT, NP, E]) for r in range(2)]
        best = [sb(f"{p}_best{r}", [PT, NP]) for r in range(2)]
        at = sb(p + "_at", [PT, NP])
        total = sb(p + "_total", [PT, NP])
        combT = sb(p + "_combT", [E, N])
        l_ps = ps(p + "_l_ps", [128, BANK])
        t_ps = ps(p + "_t_ps", [128, 2, BANK])
        rb = sb(p + "_rb", [PT, E]) if layer == 2 else None
        loaded = sem(p + "_loaded")
        logits = sem(p + "_logits_ready")
        step = sem(p + "_vector_step")
        for_exp = sem(p + "_exponents_ready")
        exped = sem(p + "_exponentials_ready")
        combined = sem(p + "_comb_ready")
        turned = sem(p + "_combT_ready")
        kept = sem(p + "_combT_kept")
        stored = sem(p + "_comb_stored")
        LOADS = 16 * (2 + (layer == 2))
        wide = [PT, NP, E]
        with nc.Block() as block:
            @block.sync
            def _(sp):
                sp.dma_start(w[:, :, :], I[p + "_w"]).then_inc(loaded, 16)
                sp.dma_start(order[:, :], I[f"order{E}"]).then_inc(loaded, 16)
                if layer == 2:
                    sp.dma_start(rb[:, :], I[p + "_b"]).then_inc(loaded, 16)
                sp.wait_ge(kept, 2)
                sp.dma_start(comb_dram, combT[:, :]).then_inc(stored, 16)
                sp.wait_ge(stored, 16)

            @block.tensor
            def _(pe):
                pe.wait_ge(loaded, LOADS)
                for j in range(NP):
                    for c in range(2):
                        mm = pe.matmul(l_ps[0:PT, j * E:(j + 1) * E], lhsT=hT[:, c, j * PT:(j + 1) * PT], rhs=w[:, c, :],
                                       start=(c == 0), stop=(c == 1))
                mm.then_inc(logits, 1)
                pe.wait_ge(combined, 1)
                for half in range(2):
                    for q in range(NP // 2):
                        mm = pe.transpose(t_ps[0:E, half, q * PT:(q + 1) * PT], comb[:, half * (NP // 2) + q, :], ident[0:PT, 0:PT])
                    mm.then_inc(turned, 1)

            @block.scalar
            def _(act):
                act.wait_ge(for_exp, 1)
                if layer == 2:
                    act.activation(at[:, :], at[:, :], ACT.Exp).then_inc(exped, 1)
                else:
                    act.activation(score[:, :, :], score[:, :, :], ACT.Exp).then_inc(exped, 1)
                for half in range(2):
                    act.wait_ge(turned, half + 1)
                    act.activation(combT[:, half * HALF:(half + 1) * HALF], t_ps[0:E, half, 0:HALF], ACT.Copy).then_inc(kept, 1)

            @block.vector
            def _(dve):
                count = [0]

                def chain(ins):
                    count[0] += 1
                    ins.then_inc(step, 1)
                    dve.wait_ge(step, count[0])

                def over(t):
                    return t[:, :].unsqueeze(2).to_broadcast(wide)

                dve.wait_ge(loaded, LOADS)
                dve.wait_ge(logits, 1)
                l3 = l_ps[0:PT, 0:NP * E].rearrange("p (j e) -> p j e", e=E)
                if layer == 2:
                    chain(dve.tensor_tensor(score[:, :, :], l3, rb[:, :].unsqueeze(1).to_broadcast(wide), ALU.add))
                else:
                    chain(dve.tensor_reduce(total[:, :], l3, AX.X, ALU.max))
                    dve.tensor_tensor(score[:, :, :], l3, over(total), ALU.subtract).then_inc(for_exp, 1)
                    dve.wait_ge(exped, 1)
                    chain(dve.tensor_reduce(total[:, :], score[:, :, :], AX.X, ALU.add))
                    chain(dve.reciprocal(total[:, :], total[:, :]))
                    chain(dve.tensor_tensor(score[:, :, :], score[:, :, :], over(total), ALU.mult))
                for r in range(2):
                    src = score if r == 0 else rest
                    chain(dve.tensor_reduce(best[r][:, :], src[:, :, :], AX.X, ALU.max))
                    chain(dve.tensor_tensor(place[:, :, :], src[:, :, :], over(best[r]), ALU.is_lt))
                    chain(dve.scalar_tensor_tensor(place[:, :, :], place[:, :, :], float(4 * E),
                                                   order[:, :].unsqueeze(1).to_broadcast(wide), ALU.mult, ALU.add))
                    chain(dve.tensor_reduce(at[:, :], place[:, :, :], AX.X, ALU.min))
                    chain(dve.tensor_tensor(hot[r][:, :, :], place[:, :, :], over(at), ALU.is_equal))
                    if r == 0:
                        chain(dve.scalar_tensor_tensor(rest[:, :, :], hot[0][:, :, :], NEG, score[:, :, :], ALU.mult, ALU.add))
                if layer == 1:
                    chain(dve.tensor_tensor(total[:, :], best[0][:, :], best[1][:, :], ALU.add))
                    chain(dve.tensor_scalar(total[:, :], total[:, :], 1e-9, None, ALU.max))
                    chain(dve.reciprocal(total[:, :], total[:, :]))
                    for r in range(2):
                        chain(dve.tensor_tensor(best[r][:, :], best[r][:, :], total[:, :], ALU.mult))
                if layer == 2:
                    chain(dve.tensor_tensor(total[:, :], best[1][:, :], best[0][:, :], ALU.subtract))
                    dve.tensor_copy(at[:, :], total[:, :]).then_inc(for_exp, 1)
                    dve.wait_ge(exped, 1)
                    chain(dve.tensor_scalar(total[:, :], at[:, :], 1.0, None, ALU.add))
                    chain(dve.reciprocal(best[0][:, :], total[:, :]))
                    chain(dve.tensor_tensor(best[1][:, :], best[0][:, :], at[:, :], ALU.mult))
                for r in range(2):
                    chain(dve.tensor_tensor(hot[r][:, :, :], hot[r][:, :, :], over(best[r]), ALU.mult))
                dve.tensor_tensor(comb[:, :, :], hot[0][:, :, :], hot[1][:, :, :], ALU.add).then_inc(combined, 1)


def capacity(nc, I, comb, comb_dram, kept_dram, const):
    E = FFN[1][1]
    with ExitStack() as ctx:
        sb, ps, sem = alloc(nc, ctx)
        row = sb("cap_row", [128, 2, N])
        before = sb("cap_before", [PT, 2, NP, N], BF16)
        tied = sb("cap_tied", [PT, 2, NP, PT], BF16)
        kept = sb("cap_kept", [128, 2, N])
        later = sb("cap_later", [PT, PT])
        ones = sb("cap_ones", [PT, 128], BF16)
        rank = ps("cap_rank", [128, 4, BANK])
        const_loaded = sem("cap_const_loaded")
        ones_ready = sem("cap_ones_ready")
        loaded = [sem(f"cap_row_loaded{k}") for k in range(2)]
        compared = sem("cap_compared")
        ranked = sem("cap_ranked")
        masked = sem("cap_masked")
        stored = [sem(f"cap_stored{k}") for k in range(2)]
        with nc.Block() as block:
            @block.sync
            def _(sp):
                sp.dma_start(later[:, :], I["later"]).then_inc(const_loaded, 16)

                def body(i, again):
                    for k in range(2):
                        if again:
                            sp.wait_ge(masked, 2 * (2 * i + k - 1))
                        src = bass.AP(comb_dram.tensor, (2 * i + k) * N, [[0, 128], [1, N]])
                        sp.dma_start(row[:, k, :], src).then_inc(loaded[k], 16)
                body(0, False)
                with sp.Fori(1, E // 2) as i:
                    body(i, True)

            @block.gpsimd
            def _(pool):
                pool.memset(ones[:, :], 1.0).then_inc(ones_ready, 1)

                def body(i):
                    for k in range(2):
                        pool.wait_ge(masked, 2 * (2 * i + k + 1))
                        pool.dma_start(kept_dram[bass.ds(2 * i + k, 1), :], kept[0:1, k, :]).then_inc(stored[k], 16)
                with pool.Fori(0, E // 2) as i:
                    body(i)
                for k in range(2):
                    pool.wait_ge(stored[k], 16 * (E // 2))

            @block.vector
            def _(dve):
                dve.wait_ge(const_loaded, 16)

                def body(i, again):
                    for k in range(2):
                        e = 2 * i + k
                        dve.wait_ge(loaded[k], 16 * i + 16)
                        if again:
                            dve.wait_ge(ranked, e - 1)
                        for j in range(NP):
                            own = comb[:, j, bass.ds(e, 1)]
                            end = (j + 1) * PT
                            dve.tensor_scalar(before[:, k, j, 0:end], row[0:PT, k, 0:end], own, None, ALU.is_lt).then_inc(compared, 1)
                            if end < N:
                                dve.tensor_scalar(before[:, k, j, end:N], row[0:PT, k, end:N], own, None, ALU.is_le).then_inc(compared, 1)
                            dve.scalar_tensor_tensor(tied[:, k, j, :], row[0:PT, k, end - PT:end], own, later[:, :],
                                                     ALU.is_equal, ALU.mult).then_inc(compared, 1)
                        dve.wait_ge(ranked, e + 1)
                        if again:
                            dve.wait_ge(stored[k], 16 * i)
                        for half in range(2):
                            cols = slice(half * HALF, (half + 1) * HALF)
                            dve.scalar_tensor_tensor(kept[:, k, cols], rank[:, 2 * k + half, 0:HALF], float(CAPACITY),
                                                     row[:, k, cols], ALU.is_lt, ALU.mult).then_inc(masked, 1)
                body(0, False)
                with dve.Fori(1, E // 2) as i:
                    body(i, True)

            @block.tensor
            def _(pe):
                pe.wait_ge(ones_ready, 1)
                PER = 3 * NP - 1

                def body(i, again):
                    for k in range(2):
                        e = 2 * i + k
                        pe.wait_ge(compared, PER * (e + 1))
                        if again:
                            pe.wait_ge(masked, 2 * (e - 1))
                        for half in range(2):
                            for j in range(NP):
                                pe.matmul(rank[:, 2 * k + half, 0:HALF], lhsT=ones[:, :],
                                          rhs=before[:, k, j, half * HALF:(half + 1) * HALF],
                                          start=(j == 0), stop=False, skip_group_check=True)
                            for q in range(NP // 2):
                                mm = pe.matmul(rank[:, 2 * k + half, q * PT:(q + 1) * PT], lhsT=ones[:, :],
                                               rhs=tied[:, k, half * (NP // 2) + q, :],
                                               start=False, stop=True, skip_group_check=True)
                        mm.then_inc(ranked, 1)
                body(0, False)
                with pe.Fori(1, E // 2) as i:
                    body(i, True)


def experts(nc, I, layer, h, hT, weights_dram, const):
    shared, E, upe, M, per_body = FFN[layer]
    p = f"ffn{layer}"
    ring = upe * per_body
    bodies = (shared + E * upe) // ring
    plain = shared // upe
    S = 2 * ring
    ALPHA, LIMIT = 1.702, 7.0
    clamped = layer == 2
    ident = const["ident"]
    with ExitStack() as ctx:
        sb, ps, sem = alloc(nc, ctx)
        wgu = sb(p + "_wgu", [C, ring, 2, 2 * M])
        wd = sb(p + "_wd", [M, ring, D])
        rows = sb(p + "_rows", [128, plain + E, N])
        gate = sb(p + "_gate", [M, 2, HALF])
        silu = sb(p + "_silu", [M, 2, HALF])
        up = sb(p + "_up", [M, 2, HALF])
        inner = sb(p + "_inner", [M, 2, HALF])
        yT = sb(p + "_yT", [C, 2, N])
        gu_ps = ps(p + "_gu_ps", [128, 4, BANK])
        y_ps = ps(p + "_y_ps", [128, 4, BANK])
        unit_loaded = [sem(f"{p}_unit_loaded{k}") for k in range(ring)]
        rows_loaded = sem(p + "_rows_loaded")
        rows_set = sem(p + "_rows_set")
        small = sem(p + "_small_loaded")
        gu = sem(p + "_gate_up_ready")
        gated = sem(p + "_gate_clamped")
        silued = sem(p + "_silu_ready")
        upped = sem(p + "_up_step")
        product = sem(p + "_product_step")
        ready = sem(p + "_inner_ready")
        downed = sem(p + "_down_done")
        kept = sem(p + "_yT_kept")
        turned = sem(p + "_y_ready")
        added = sem(p + "_added")
        if clamped:
            ubias = sb(p + "_ubias", [M, E * upe, 2])
            dbias = sb(p + "_dbias", [E, D])
            combT = sb(p + "_combT", [E, N])
        with nc.Block() as block:
            @block.sync
            def _(sp):
                if clamped:
                    sp.dma_start(ubias[:, :, :], I[p + "_ubias"]).then_inc(small, 16)
                    sp.dma_start(dbias[:, :], I[p + "_dbias"]).then_inc(small, 16)
                    sp.dma_start(combT[:, :], weights_dram).then_inc(small, 16)

                def load(i, k):
                    u = i * ring + k
                    sp.dma_start(wgu[:, k, :, :].rearrange("p c m -> p (c m)"),
                                 I[p + "_wgu"][bass.ds(u, 1), :, :].rearrange("a p m -> p (a m)")).then_inc(unit_loaded[k], 16)
                    sp.dma_start(wd[:, k, :],
                                 I[p + "_wd"][bass.ds(u, 1), :, :].rearrange("a p m -> p (a m)")).then_inc(unit_loaded[k], 16)
                for k in range(ring):
                    load(0, k)
                sp.dma_start(rows[:, plain:, :].rearrange("p e n -> p (e n)"),
                             bass.AP(weights_dram.tensor, 0, [[0, 128], [1, E * N]])).then_inc(rows_loaded, 16)
                with sp.Fori(1, bodies) as i:
                    for k in range(ring):
                        sp.wait_ge(downed, (i - 1) * S + 2 * k + 2)
                        load(i, k)

            @block.gpsimd
            def _(pool):
                if plain:
                    pool.memset(rows[:, 0:plain, :], 1.0).then_inc(rows_set, 1)

            @block.tensor
            def _(pe):
                def down(s, k, half, start, stop):
                    pe.wait_ge(ready, s + 1)
                    for c in range(2):
                        mm = pe.matmul(y_ps[0:C, 2 * half + c, 0:HALF], lhsT=wd[:, k, c * C:(c + 1) * C],
                                       rhs=inner[:, half, :], start=start, stop=stop, skip_group_check=True)
                    mm.then_inc(downed, 1)

                def body(i, again):
                    for k in range(ring):
                        pe.wait_ge(unit_loaded[k], 32 * i + 32)
                        for half in range(2):
                            s = i * S + 2 * k + half
                            if again or 2 * k + half >= 2:
                                pe.wait_ge(ready, s - 1)
                            for m in range(2):
                                for c in range(2):
                                    mm = pe.matmul(gu_ps[0:M, 2 * half + m, 0:HALF], lhsT=wgu[:, k, c, m * M:(m + 1) * M],
                                                   rhs=hT[:, c, half * HALF:(half + 1) * HALF],
                                                   start=(c == 0), stop=(c == 1))
                            mm.then_inc(gu, 1)
                            if again or 2 * k + half >= 1:
                                down(s - 1, (k - 1 + half) % ring, 1 - half,
                                     not again and not clamped and 2 * k + half <= 2, False)
                if clamped:
                    pe.wait_ge(small, 48)
                    for half in range(2):
                        for c in range(2):
                            pe.matmul(y_ps[0:C, 2 * half + c, 0:HALF], lhsT=dbias[:, c * C:(c + 1) * C],
                                      rhs=combT[:, half * HALF:(half + 1) * HALF], start=True, stop=False,
                                      skip_group_check=True)
                body(0, False)
                with pe.Fori(1, bodies) as i:
                    body(i, True)
                down(bodies * S - 1, ring - 1, 1, False, True)
                for j in range(NP):
                    if j % 4 == 0:
                        pe.wait_ge(kept, 2 * (j // 4) + 2)
                    for c in range(2):
                        mm = pe.transpose(gu_ps[0:PT, j // 2, (j % 2) * D + c * C:(j % 2) * D + (c + 1) * C],
                                          yT[:, c, j * PT:(j + 1) * PT], ident[0:C, 0:C])
                    mm.then_inc(turned, 1)

            @block.scalar
            def _(act):
                def body(i):
                    for k in range(ring):
                        for half in range(2):
                            s = i * S + 2 * k + half
                            if clamped:
                                act.wait_ge(gated, s + 1)
                                act.activation(silu[:, half, :], gate[:, half, :], ACT.Silu, scale=ALPHA).then_inc(silued, 1)
                            else:
                                act.wait_ge(gu, s + 1)
                                act.activation(silu[:, half, :], gu_ps[0:M, 2 * half, 0:HALF], ACT.Silu).then_inc(silued, 1)
                with act.Fori(0, bodies) as i:
                    body(i)
                act.wait_ge(downed, bodies * S)
                for half in range(2):
                    for c in range(2):
                        act.activation(yT[:, c, half * HALF:(half + 1) * HALF], y_ps[0:C, 2 * half + c, 0:HALF],
                                       ACT.Copy).then_inc(kept, 1)

            @block.vector
            def _(dve):
                if clamped:
                    dve.wait_ge(small, 48)

                def body(i, again):
                    for k in range(ring):
                        for half in range(2):
                            s = i * S + 2 * k + half
                            cols = slice(half * HALF, (half + 1) * HALF)
                            row = rows[0:M, bass.ds(i * per_body + k // upe, 1), cols].rearrange("p a n -> p (a n)")
                            dve.wait_ge(gu, s + 1)
                            if clamped:
                                u = bass.ds(i * ring + k, 1)
                                if again or 2 * k + half >= 2:
                                    dve.wait_ge(silued, s - 1)
                                dve.tensor_scalar(gate[:, half, :], gu_ps[0:M, 2 * half, 0:HALF], ubias[:, u, 0], LIMIT,
                                                  ALU.add, ALU.min).then_inc(gated, 1)
                                dve.tensor_scalar(up[:, half, :], gu_ps[0:M, 2 * half + 1, 0:HALF], ubias[:, u, 1], LIMIT,
                                                  ALU.add, ALU.min).then_inc(upped, 1)
                                dve.wait_ge(upped, 2 * s + 1)
                                dve.tensor_scalar(up[:, half, :], up[:, half, :], -LIMIT, 1.0, ALU.max, ALU.add).then_inc(upped, 1)
                                dve.wait_ge(silued, s + 1)
                                dve.wait_ge(upped, 2 * s + 2)
                                dve.scalar_tensor_tensor(up[:, half, :], silu[:, half, :], 1.0 / ALPHA, up[:, half, :],
                                                         ALU.mult, ALU.mult).then_inc(product, 1)
                            else:
                                dve.wait_ge(silued, s + 1)
                                dve.tensor_tensor(up[:, half, :], silu[:, half, :], gu_ps[0:M, 2 * half + 1, 0:HALF],
                                                  ALU.mult).then_inc(product, 1)
                            dve.wait_ge(product, s + 1)
                            if again or 2 * k + half >= 2:
                                dve.wait_ge(downed, s - 1)
                            dve.tensor_tensor(inner[:, half, :], up[:, half, :], row, ALU.mult).then_inc(ready, 1)
                if plain:
                    dve.wait_ge(rows_set, 1)
                else:
                    dve.wait_ge(rows_loaded, 16)
                body(0, False)
                dve.wait_ge(rows_loaded, 16)
                with dve.Fori(1, bodies) as i:
                    body(i, True)
                for q in range(NP // 2):
                    dve.wait_ge(turned, 2 * q + 2)
                    dve.tensor_tensor(h[:, 2 * q:2 * q + 2, :], h[:, 2 * q:2 * q + 2, :],
                                      gu_ps[0:PT, q, 0:2 * D].rearrange("p (a d) -> p a d", a=2), ALU.add).then_inc(added, 1)


def ternary_attention(nc, I, h, hT, const):
    identb = const["identb"]
    with ExitStack() as ctx:
        sb, ps, sem = alloc(nc, ctx)
        W3 = 3 * D
        qT = sb("ta_qT", [C, 2, N], BF16)
        kT = sb("ta_kT", [C, 2, N], BF16)
        tern = sb("ta_tern", [PT, NP, W3], BF16)
        means = sb("ta_means", [128, 3])
        limit = sb("ta_limit", [128, 1])
        out_scale = sb("ta_out_scale", [128, 1])
        ones = const["ones"]

        with ExitStack() as pre:
            psb, pps, psem = alloc(nc, pre)
            w = psb("ta_w", [C, 2, W3])
            wt = psb("ta_wt", [C, 2, W3])
            below = psb("ta_w_below", [C, 2, W3])
            wsum = psb("ta_wsum", [C, 1])
            ws = psb("ta_ws", [128, 1])
            wlim = psb("ta_wlim", [128, 2])
            qkv = psb("ta_qkv", [PT, NP, W3])
            lower = psb("ta_lower", [PT, NP, D], BF16)
            norm1 = psb("ta_norm1", [PT, NP, 3 * H])
            sums = psb("ta_sums", [PT, NP, 3])
            lims = psb("ta_lims", [128, 2, 3])
            acc = pps("ta_acc", [128, 4, BANK])
            stat = pps("ta_stat", [128, BANK])
            trans = pps("ta_trans", [128, 2, 2 * BANK], BF16)
            loaded = psem("ta_loaded")
            step = psem("ta_weight_step")
            wsummed = psem("ta_weight_sum_ready")
            projected = psem("ta_projected")
            copied = psem("ta_projection_copied")
            normed = psem("ta_norm_step")
            summed = psem("ta_sums_ready")
            mstep = psem("ta_mean_step")
            tready = psem("ta_ternary_ready")
            turned = psem("ta_transposed")
            tcopied = psem("ta_transposed_copied")
            with nc.Block() as block:
                @block.sync
                def _(sp):
                    sp.dma_start(w[:, :, :], I["ta_w"]).then_inc(loaded, 16)

                @block.tensor
                def _(pe):
                    pe.wait_ge(step, 1)
                    pe.matmul(stat[:, 0:1], lhsT=ones[0:C, :], rhs=wsum[:, :], start=True, stop=True).then_inc(wsummed, 1)
                    pe.wait_ge(step, 5)
                    for j in range(NP):
                        if j >= 2:
                            pe.wait_ge(copied, 2 * (j - 1))
                        for part in range(2):
                            for c in range(2):
                                mm = pe.matmul(acc[0:PT, 2 * (j % 2) + part, 0:W3 // 2], lhsT=hT[:, c, j * PT:(j + 1) * PT],
                                               rhs=wt[:, c, part * (W3 // 2):(part + 1) * (W3 // 2)],
                                               start=(c == 0), stop=(c == 1))
                            mm.then_inc(projected, 1)
                    pe.wait_ge(summed, NP)
                    pe.matmul(stat[:, 0:3 * NP], lhsT=ones[0:PT, :], rhs=sums[:, :, :].rearrange("p j a -> p (j a)"),
                              start=True, stop=True).then_inc(wsummed, 1)
                    for a in range(2):
                        pe.wait_ge(tready, a + 1)
                        for c in range(2):
                            if a:
                                pe.wait_ge(tcopied, c + 1)
                            for j in range(NP):
                                mm = pe.transpose(trans[0:C, c, j * PT:(j + 1) * PT],
                                                  tern[:, j, a * D + c * C:a * D + (c + 1) * C], identb[0:PT, 0:PT])
                            mm.then_inc(turned, 1)

                @block.scalar
                def _(act):
                    act.wait_ge(step, 5)
                    for j in range(NP):
                        for part in range(2):
                            act.wait_ge(projected, 2 * j + part + 1)
                            act.activation(qkv[:, j, part * (W3 // 2):(part + 1) * (W3 // 2)],
                                           acc[0:PT, 2 * (j % 2) + part, 0:W3 // 2], ACT.Copy,
                                           scale=ws[0:PT, 0:1]).then_inc(copied, 1)
                    for a in range(2):
                        for c in range(2):
                            act.wait_ge(turned, 2 * a + c + 1)
                            act.activation((qT, kT)[a][:, c, :], trans[0:C, c, 0:N], ACT.Copy).then_inc(tcopied, 1)

                @block.vector
                def _(dve):
                    flat = lambda t: t[:, :, :].rearrange("p c n -> p (c n)")
                    dve.wait_ge(loaded, 16)
                    dve.tensor_reduce(wsum[:, :], flat(w), AX.X, ALU.add, apply_absolute_value=True).then_inc(step, 1)
                    dve.wait_ge(wsummed, 1)
                    dve.tensor_scalar(ws[:, :], stat[:, 0:1], 1.0 / (D * W3), TERNARY_EPS, ALU.mult, ALU.add).then_inc(step, 1)
                    dve.wait_ge(step, 2)
                    dve.tensor_scalar(wlim[:, 0:1], ws[:, :], 0.5, None, ALU.mult)
                    dve.tensor_scalar(wlim[:, 1:2], ws[:, :], -0.5, None, ALU.mult).then_inc(step, 1)
                    dve.wait_ge(step, 3)
                    dve.tensor_scalar(flat(below), flat(w), wlim[0:C, 1:2], None, ALU.is_lt).then_inc(step, 1)
                    dve.wait_ge(step, 4)
                    dve.scalar_tensor_tensor(flat(wt), flat(w), wlim[0:C, 0:1], flat(below), ALU.is_gt, ALU.subtract).then_inc(step, 1)
                    for j in range(NP):
                        dve.wait_ge(copied, 2 * j + 2)
                        heads = qkv[:, j, :].rearrange("p (h d) -> p h d", d=HD)
                        dve.tensor_reduce(norm1[:, j, :], heads, AX.X, ALU.add, apply_absolute_value=True).then_inc(normed, 1)
                        dve.wait_ge(normed, 4 * j + 1)
                        dve.tensor_scalar(norm1[:, j, :], norm1[:, j, :], TERNARY_EPS, None, ALU.add).then_inc(normed, 1)
                        dve.wait_ge(normed, 4 * j + 2)
                        dve.reciprocal(norm1[:, j, :], norm1[:, j, :]).then_inc(normed, 1)
                        dve.wait_ge(normed, 4 * j + 3)
                        dve.tensor_tensor(heads, heads, norm1[:, j, :].unsqueeze(2).to_broadcast([PT, 3 * H, HD]),
                                          ALU.mult).then_inc(normed, 1)
                        dve.wait_ge(normed, 4 * j + 4)
                        dve.tensor_reduce(sums[:, j, :], qkv[:, j, :].rearrange("p (a d) -> p a d", a=3), AX.X, ALU.add,
                                          apply_absolute_value=True).then_inc(summed, 1)
                    dve.wait_ge(wsummed, 2)
                    dve.tensor_reduce(means[:, :], stat[:, 0:3 * NP].rearrange("p (j a) -> p a j", a=3), AX.X,
                                      ALU.add).then_inc(mstep, 1)
                    dve.wait_ge(mstep, 1)
                    dve.tensor_scalar(means[:, :], means[:, :], 1.0 / (N * D), TERNARY_EPS, ALU.mult, ALU.add).then_inc(mstep, 1)
                    dve.wait_ge(mstep, 2)
                    dve.tensor_scalar(lims[:, 0, :], means[:, :], 0.5, None, ALU.mult).then_inc(mstep, 1)
                    dve.tensor_scalar(lims[:, 1, :], means[:, :], -0.5, None, ALU.mult).then_inc(mstep, 1)
                    dve.wait_ge(mstep, 4)
                    for a in range(3):
                        part = qkv[:, :, a * D:(a + 1) * D]
                        if a:
                            dve.wait_ge(tready, a)
                        dve.tensor_scalar(lower[:, :, :], part, lims[0:PT, 1, a:a + 1], None, ALU.is_lt).then_inc(mstep, 1)
                        dve.wait_ge(mstep, 5 + a)
                        dve.scalar_tensor_tensor(tern[:, :, a * D:(a + 1) * D], part, lims[0:PT, 0, a:a + 1],
                                                 lower[:, :, :], ALU.is_gt, ALU.subtract).then_inc(tready, 1)

        with ExitStack() as main:
            msb, mps, msem = alloc(nc, main)
            q_stage = msb("ta_q_stage", [C, 2, 2, PT], BF16)
            k_blocks = msb("ta_k_blocks", [C, 2, 2, 2, HC, T], BF16)
            dots = msb("ta_dots", [SR, NP, H * T], BF16)
            dsum = msb("ta_dsum", [SR, NP])
            dtot = msb("ta_dtot", [SR, 1])
            mean = msb("ta_mean", [128, 1])
            unit = msb("ta_unit", [128, 1])
            score_s = msb("ta_score_s", [128, 1])
            nlimit = msb("ta_nlimit", [128, 1])
            inv = msb("ta_inv", [128, 1])
            lower = msb("ta_dots_lower", [SR, 2, H * T], BF16)
            probs = msb("ta_probs", [SR, 2, H * T], BF16)
            probsT = msb("ta_probsT", [GK, 2, G, SR], BF16)
            v_blocks = msb("ta_v_blocks", [GK, 2, 2, D], BF16)
            oT = msb("ta_oT", [GD, 2, G, PT], BF16)
            s_ps = mps("ta_s", [128, 2, BANK])
            staged = msem("ta_staged")
            cleared = msem("ta_banks_cleared")
            scores = msem("ta_scores_ready")
            dotted = msem("ta_dots_kept")
            sstep = msem("ta_scalar_step")
            total = msem("ta_total_ready")
            with nc.Block() as block:
                @block.gpsimd
                def _(pool):
                    def body(i, later):
                        for k in range(2):
                            j = 2 * i + k
                            if later:
                                pool.wait_ge(scores, j - 1)
                            pool.tensor_copy(q_stage[:, k, :, :], qT[:, :, bass.ds(j * PT, PT)]).then_inc(staged, 1)
                            for c in range(2):
                                pool.tensor_tensor(k_blocks[:, k, c, :, :, :],
                                                   kT[:, c, bass.ds(j * PT, PT)].rearrange("p (b t) -> p b t", b=2)
                                                   .unsqueeze(2).to_broadcast([C, 2, HC, T]),
                                                   const["own_head"][:, :].unsqueeze(1).unsqueeze(3)
                                                   .to_broadcast([C, 2, HC, T]), ALU.mult).then_inc(staged, 1)
                    body(0, False)
                    with pool.Fori(1, NP // 2) as i:
                        body(i, True)

                @block.tensor
                def _(pe):
                    pe.wait_ge(cleared, 1)

                    def body(i, later):
                        for k in range(2):
                            j = 2 * i + k
                            pe.wait_ge(staged, 3 * j + 3)
                            if later:
                                pe.wait_ge(dotted, j - 1)
                            for c in range(2):
                                for img in range(2):
                                    mm = pe.matmul(s_ps[img * SECOND:img * SECOND + T, k, c * HC * T:(c + 1) * HC * T],
                                                   lhsT=q_stage[:, k, c, img * T:(img + 1) * T],
                                                   rhs=k_blocks[:, k, c, img, :, :].rearrange("p a t -> p (a t)"),
                                                   start=True, stop=True)
                            mm.then_inc(scores, 1)
                    body(0, False)
                    with pe.Fori(1, NP // 2) as i:
                        body(i, True)
                    pe.wait_ge(sstep, 1)
                    pe.matmul(s_ps[:, 0, 0:1], lhsT=ones[0:SR, :], rhs=dtot[:, :], start=True, stop=True).then_inc(total, 1)

                @block.vector
                def _(dve):
                    dve.memset(s_ps[:, :, :], 0.0).then_inc(cleared, 1)

                    def body(i):
                        for k in range(2):
                            j = 2 * i + k
                            dve.wait_ge(scores, j + 1)
                            dve.tensor_reduce(dsum[:, bass.ds(j, 1)], s_ps[0:SR, k, 0:H * T], AX.X, ALU.add,
                                              apply_absolute_value=True)
                            dve.tensor_copy(dots[:, bass.ds(j, 1), :].rearrange("p a n -> p (a n)"),
                                            s_ps[0:SR, k, 0:H * T]).then_inc(dotted, 1)
                    with dve.Fori(0, NP // 2) as i:
                        body(i)
                    dve.wait_ge(dotted, NP)
                    dve.tensor_reduce(dtot[:, :], dsum[:, :], AX.X, ALU.add).then_inc(sstep, 1)
                    dve.wait_ge(total, 1)
                    dve.tensor_scalar(mean[:, :], s_ps[:, 0, 0:1], 1.0 / (B * H * T * T), None, ALU.mult).then_inc(sstep, 1)
                    dve.scalar_tensor_tensor(unit[:, :], means[:, 0:1], SCALE, means[:, 1:2], ALU.mult, ALU.mult).then_inc(sstep, 1)
                    dve.wait_ge(sstep, 3)
                    dve.tensor_tensor(score_s[:, :], mean[:, :], unit[:, :], ALU.mult).then_inc(sstep, 1)
                    dve.wait_ge(sstep, 4)
                    dve.tensor_scalar(score_s[:, :], score_s[:, :], TERNARY_EPS, None, ALU.add).then_inc(sstep, 1)
                    dve.reciprocal(inv[:, :], unit[:, :]).then_inc(sstep, 1)
                    dve.wait_ge(sstep, 6)
                    dve.scalar_tensor_tensor(limit[:, :], score_s[:, :], 0.5, inv[:, :], ALU.mult, ALU.mult).then_inc(sstep, 1)
                    dve.tensor_tensor(out_scale[:, :], score_s[:, :], means[:, 2:3], ALU.mult).then_inc(sstep, 1)
                    dve.wait_ge(sstep, 8)
                    dve.tensor_scalar(nlimit[:, :], limit[:, :], -1.0, None, ALU.mult).then_inc(sstep, 1)

            t_ps = mps("ta_t", [128, 2, 2 * BANK], BF16)
            v_ps = mps("ta_v", [128, 2, BANK])
            oy_ps = mps("ta_oy", [128, 2, BANK])
            under = msem("ta_under")
            rounded = msem("ta_rounded")
            values = msem("ta_values_ready")
            v_ready = msem("ta_v_blocks_ready")
            turned_s = msem("ta_roundedT_ready")
            pT_copied = msem("ta_roundedT_copied")
            o_ready = msem("ta_outputs_ready")
            o_copied = msem("ta_outputs_copied")
            y_ready = msem("ta_token_major_ready")
            added = msem("ta_added")

            def y_of(k):
                return oy_ps[0:PT, k, G * PT:G * PT + D]

            with nc.Block() as block:
                @block.tensor
                def _(pe):
                    def body(i, later):
                        for k in range(2):
                            j = 2 * i + k
                            if later:
                                pe.wait_ge(v_ready, j - 1)
                            for img in range(2):
                                mm = pe.matmul(v_ps[0:GK, k, img * D:(img + 1) * D], lhsT=const["copy_keys"][:, img, :],
                                               rhs=tern[:, bass.ds(j, 1), 2 * D:3 * D].rearrange("p a d -> p (a d)"),
                                               start=True, stop=True)
                            mm.then_inc(values, 1)
                        for k in range(2):
                            j = 2 * i + k
                            pe.wait_ge(rounded, j + 1)
                            if later:
                                pe.wait_ge(pT_copied, j - 1)
                            for g in range(G):
                                mm = pe.transpose(t_ps[0:GK, k, g * 128:g * 128 + SR],
                                                  probs[:, k, g * GK:(g + 1) * GK], identb[0:SR, 0:SR])
                            mm.then_inc(turned_s, 1)
                            pe.wait_ge(pT_copied, j + 1)
                            pe.wait_ge(v_ready, j + 1)
                            if later:
                                pe.wait_ge(added, j - 1)
                            for img in range(2):
                                for g in range(G):
                                    mm = pe.matmul(oy_ps[0:GD, k, g * PT + img * T:g * PT + (img + 1) * T],
                                                   lhsT=v_blocks[:, k, img, g * GD:(g + 1) * GD],
                                                   rhs=probsT[:, k, g, img * SECOND:img * SECOND + T],
                                                   start=True, stop=True)
                            mm.then_inc(o_ready, 1)
                            pe.wait_ge(o_copied, j + 1)
                            for g in range(G):
                                mm = pe.matmul(y_of(k), lhsT=oT[:, k, g, :], rhs=const["place"][:, g, :],
                                               start=(g == 0), stop=(g == G - 1))
                            mm.then_inc(y_ready, 1)
                    body(0, False)
                    with pe.Fori(1, NP // 2) as i:
                        body(i, True)

                @block.scalar
                def _(act):
                    def body(i, later):
                        for k in range(2):
                            j = 2 * i + k
                            act.wait_ge(turned_s, j + 1)
                            if later:
                                act.wait_ge(o_ready, j - 1)
                            act.activation(probsT[:, k, :, :],
                                           t_ps[0:GK, k, 0:G * 128].rearrange("p (g s) -> p g s", g=G)[:, :, 0:SR],
                                           ACT.Copy).then_inc(pT_copied, 1)
                            act.wait_ge(o_ready, j + 1)
                            if later:
                                act.wait_ge(y_ready, j - 1)
                            act.activation(oT[:, k, :, :].rearrange("p g s -> p (g s)"), oy_ps[0:GD, k, 0:G * PT],
                                           ACT.Copy).then_inc(o_copied, 1)
                    body(0, False)
                    with act.Fori(1, NP // 2) as i:
                        body(i, True)

                @block.vector
                def _(dve):
                    def body(i, later):
                        for k in range(2):
                            j = 2 * i + k
                            dj = dots[:, bass.ds(j, 1), :].rearrange("p a n -> p (a n)")
                            if later:
                                dve.wait_ge(rounded, j - 1)
                            dve.tensor_scalar(lower[:, k, :], dj, nlimit[0:SR, 0:1], None, ALU.is_lt).then_inc(under, 1)
                            dve.wait_ge(under, j + 1)
                            if later:
                                dve.wait_ge(turned_s, j - 1)
                            dve.scalar_tensor_tensor(probs[:, k, :], dj, limit[0:SR, 0:1], lower[:, k, :],
                                                     ALU.is_gt, ALU.subtract).then_inc(rounded, 1)
                            dve.wait_ge(values, j + 1)
                            if later:
                                dve.wait_ge(o_ready, j - 1)
                            dve.tensor_tensor(v_blocks[:, k, :, :],
                                              v_ps[0:GK, k, 0:2 * D].rearrange("p (b d) -> p b d", b=2),
                                              const["own_key"][:, :].unsqueeze(1).to_broadcast([GK, 2, D]),
                                              ALU.mult).then_inc(v_ready, 1)
                        for k in range(2):
                            j = 2 * i + k
                            dve.wait_ge(y_ready, j + 1)
                            hj = h[:, bass.ds(j, 1), :].rearrange("p a d -> p (a d)")
                            dve.scalar_tensor_tensor(hj, y_of(k), out_scale[0:PT, 0:1], hj,
                                                     ALU.mult, ALU.add).then_inc(added, 1)
                    body(0, False)
                    with dve.Fori(1, NP // 2) as i:
                        body(i, True)


def tower(nc, I, out, last=8):
    SEMAPHORES.clear()
    with ExitStack() as ctx:
        sb, ps, sem = alloc(nc, ctx)
        h = sb("h", [PT, NP, D])
        hT = sb("hT", [C, 2, N])
        const = {"ident": sb("ident", [128, 128]), "identb": sb("identb", [128, 128], BF16),
                 "ones": sb("ones", [128, 128]), "power": sb("power", [PT, 2, NP]),
                 "half": sb("half", [C, 2, SP]), "own_head": sb("own_head", [C, HC]),
                 "own_key": sb("own_key", [GK, D]), "copy_keys": sb("copy_keys", [PT, 2, GK], BF16),
                 "place": sb("place", [GD, G, D], BF16)}
        raw = {"copy_keys": sb("copy_keys_f", [PT, 2, GK]), "place": sb("place_f", [GD, G, D])}
        loaded = sem("const_loaded")
        made = sem("const_made")
        with nc.Block() as block:
            @block.sync
            def _(sp):
                for name, dst in (("ident", const["ident"]), ("own_head", const["own_head"]), ("own_key", const["own_key"]),
                                  ("copy_keys", raw["copy_keys"]), ("place", raw["place"])):
                    sp.dma_start(dst[tuple(slice(None) for _ in dst.shape)], I[name]).then_inc(loaded, 16)

            @block.gpsimd
            def _(pool):
                pool.memset(const["ones"][:, :], 1.0).then_inc(made, 1)
                pool.memset(const["power"][:, 0, :], -0.5).then_inc(made, 1)
                pool.memset(const["power"][:, 1, :], 0.5).then_inc(made, 1)
                pool.memset(const["half"][:, :, :], 0.5).then_inc(made, 1)
                pool.wait_ge(loaded, 16 * 5)
                pool.tensor_copy(const["identb"][:, :], const["ident"][:, :]).then_inc(made, 1)
                pool.tensor_copy(const["copy_keys"][:, :, :], raw["copy_keys"][:, :, :]).then_inc(made, 1)
                pool.tensor_copy(const["place"][:, :, :], raw["place"][:, :, :]).then_inc(made, 1)

        def store():
            stored = sem("h_stored")
            with nc.Block() as block:
                @block.sync
                def _(sp):
                    sp.dma_start(out.rearrange("(j p) d -> p j d", p=PT), h[:, :, :]).then_inc(stored, 16)
                    sp.wait_ge(stored, 16)

        patch_embedding(nc, I, h)
        if last == 0:
            return store()
        to_feature_major(nc, h, hT, const["ident"], "tr0")
        n = 0
        for layer in range(4):
            reset_semaphores(nc)
            if layer < 3:
                attention(nc, I, layer, h, hT, const)
            else:
                ternary_attention(nc, I, h, hT, const)
            n += 1
            if layer == 0:
                with nc.sbuf_tensor("unit", [PT, NP, D], F32) as unit:
                    layer_norm(nc, h, f"ln{n}", unit, const["power"])
                    if last == n:
                        return store()
                    to_feature_major(nc, unit, hT, const["ident"], f"tr{n}")
                    soft_mixture(nc, I, h, unit, hT, const)
            else:
                layer_norm(nc, h, f"ln{n}", None, const["power"])
                if last == n:
                    return store()
                to_feature_major(nc, h, hT, const["ident"], f"tr{n}")
                with nc.sbuf_tensor(f"comb{layer}", [PT, NP, FFN[layer][1]], F32) as comb:
                    router(nc, I, layer, hT, comb, I[f"comb_scratch{layer}"], const)
                    if layer == 1:
                        capacity(nc, I, comb, I["comb_scratch1"], I["kept_scratch"], const)
                experts(nc, I, layer, h, hT, I["kept_scratch" if layer == 1 else f"comb_scratch{layer}"], const)
            n += 1
            layer_norm(nc, h, f"ln{n}", None, const["power"])
            if last == n:
                return store()
            to_feature_major(nc, h, hT, const["ident"], f"tr{n}")


def shape_constants():
    f = lambda *s: np.zeros(s, np.float32)
    k = {}
    k["ident"] = np.eye(128, dtype=np.float32)
    own_head = f(C, HC)
    own_head[np.arange(C), np.arange(C) // HD] = 1
    k["own_head"] = own_head
    row, col = np.arange(GK)[:, None] // T, (np.arange(D)[None, :] // HD) % GH
    k["own_key"] = (row == col).astype(np.float32)
    rep = f(PT, 2, GK)
    for img in range(2):
        for a in range(GH):
            rep[img * T + np.arange(T), img, a * T + np.arange(T)] = 1
    k["copy_keys"] = rep
    place = f(GD, G, D)
    for g in range(G):
        place[np.arange(GD), g, g * GD + np.arange(GD)] = 1
    k["place"] = place
    causal = f(SR, H, T)
    for img in range(2):
        causal[img * SECOND:img * SECOND + T] = np.where(np.arange(T)[None, :] > np.arange(T)[:, None], NEG, 0)[:, None, :]
    k["causal"] = causal.reshape(SR, H * T)
    angle = (np.arange(T, dtype=np.float32)[None, :] *
             (1.0 / 10000.0 ** (2.0 * np.arange(HD // 2, dtype=np.float32) / HD)).astype(np.float32)[:, None])
    rope = f(C, 2, T)
    d = np.arange(C) % HD
    rope[:, 0] = np.cos(angle)[d // 2]
    rope[:, 1] = np.sin(angle)[d // 2] * np.where(d % 2, 1, -1)[:, None]
    k["rope"] = rope
    own = f(C, 2, SN, SP)
    for e in range(2):
        own[np.arange(C), e, e * 4 + np.arange(C) // SH] = 1
    k["sm_own_expert"] = own.reshape(C, 2, SLOTS)
    k["sm_own_image"] = (np.arange(PT)[:, None] // T == np.arange(2)).astype(np.float32)
    k["sm_own_image4"] = (2 * np.arange(2)[None, :, None] + (np.arange(PT) // T)[:, None, None] ==
                          np.arange(4)).astype(np.float32)
    for E in (8, 16):
        k[f"order{E}"] = np.tile(np.arange(E, dtype=np.float32), (PT, 1))
    k["later"] = (np.arange(PT)[None, :] > np.arange(PT)[:, None]).astype(np.float32)
    return k


def chunks(a, n=2):
    return a.reshape(n, a.shape[0] // n, a.shape[1]).transpose(1, 0, 2)


def swapped(a):
    return a.reshape(a.shape[:-1] + (-1, 2))[..., ::-1].reshape(a.shape)


def layouts(x):
    P = 16
    k = {}
    gh = 96 // P
    pt = x["x"].reshape(B, 3, gh, P, gh, P).transpose(0, 2, 4, 1, 3, 5).reshape(B, gh * gh, 3 * P * P)
    pt = np.concatenate([np.zeros((B, 1, 3 * P * P), np.float32), pt], 1).reshape(N, -1)
    k["patches"] = chunks(pt.T, 6)
    k["tok_w"] = chunks(x["L0_tok_W"].T, 6)
    k["tok_pos"] = np.tile(x["L0_tok_pos_emb"][0], (2, 1))
    first = np.concatenate([x["L0_tok_cls_tok"][0], np.broadcast_to(x["L0_tok_b"], (T - 1, D))], 0)
    k["tok_first"] = np.tile(first, (2, 1))

    def att(p, wq, wk, wv, wp, bq, bk, bv, bp, rope=False):
        k[p + "_wq"], k[p + "_wk"], k[p + "_wv"] = chunks(wq), chunks(wk), chunks(wv)
        bs = [bq, bk]
        if rope:
            k[p + "_wqs"], k[p + "_wks"] = chunks(swapped(wq)), chunks(swapped(wk))
            bs = [bq, swapped(bq), bk, swapped(bk)]
        k[p + "_bias"] = np.stack([b.reshape(2, C).T for b in bs], 2)
        k[p + "_wp"] = chunks(wp, G)
        k[p + "_bv"] = np.broadcast_to(bv.reshape(G, GD).T[:, :, None], (GD, G, PT))
        k[p + "_bp"] = np.tile(bp, (PT, 1))
    w, b = x["L0_attn_W_attn"], x["L0_attn_b_attn"]
    att("att0", w[:, :D], w[:, D:2 * D], w[:, 2 * D:], x["L0_attn_W_proj"], b[:D], b[D:2 * D], b[2 * D:], x["L0_attn_b_proj"])
    att("att1", x["L1_attn_Wq"].T, x["L1_attn_Wk"].T, x["L1_attn_Wv"].T, x["L1_attn_Wp"].T,
        x["L1_attn_bq"], x["L1_attn_bk"], x["L1_attn_bv"], x["L1_attn_bp"], rope=True)
    w, b = x["L2_attn_qkv_w"].T, x["L2_attn_qkv_b"]
    att("att2", w[:, :D], w[:, D:2 * D], w[:, 2 * D:], x["L2_attn_out_w"].T, b[:D], b[D:2 * D], b[2 * D:], x["L2_attn_out_b"])
    rel = x["L2_attn_rel_pos_emb"][np.clip(np.arange(SHIFTS) - (T - 1), -MAX_REL, MAX_REL) + MAX_REL]
    blocks = np.zeros((C, HC, SHIFTS), np.float32)
    for i in range(HC):
        blocks[i * HD:(i + 1) * HD, i] = rel.T
    k["rel_blocks"] = blocks.reshape(C, -1)
    k["ta_w"] = chunks(x["L3_attn_w_qkv"].T)

    k["sm_slots"] = chunks(x["L0_ffn_slot_params"].reshape(D, SLOTS))
    k["sm_scale"] = np.broadcast_to(x["L0_ffn_scale"].reshape(1, 1), (C, 1))
    k["sm_down"] = chunks(x["L0_ffn_W_down"].transpose(1, 0, 2).reshape(D, SN * SH))
    k["sm_bdown"] = x["L0_ffn_b_down"].reshape(2, C).T
    k["sm_up"] = chunks(x["L0_ffn_W_up"].reshape(SN * SH, D))
    k["sm_bup"] = np.tile(np.repeat(x["L0_ffn_b_up"], SP, 0), (4, 1))

    def units(gate, up, down, M):
        e, inner = gate.shape[0], gate.shape[2]
        n = inner // M
        gu = np.stack([gate.reshape(e, 2, C, n, M), up.reshape(e, 2, C, n, M)], 4)
        return (gu.transpose(0, 3, 2, 1, 4, 5).reshape(e * n, C, 4 * M), down.reshape(e * n, M, D))

    def ffn(layer, parts):
        parts = [units(*q, FFN[layer][3]) for q in parts]
        k[f"ffn{layer}_wgu"] = np.concatenate([q[0] for q in parts], 0)
        k[f"ffn{layer}_wd"] = np.concatenate([q[1] for q in parts], 0)
    ffn(1, [(x["L1_ffn_s1"][None], x["L1_ffn_s3"][None], x["L1_ffn_s2"][None]),
            (x["L1_ffn_w1"], x["L1_ffn_w3"], x["L1_ffn_w2"])])
    gu = x["L2_ffn_Wgu"]
    I2 = gu.shape[2] // 2
    ffn(2, [(gu[:, :, :I2], gu[:, :, I2:], x["L2_ffn_Wd"])])
    k["ffn2_ubias"] = x["L2_ffn_bgu"].reshape(8, 2, 2, C).transpose(3, 0, 2, 1).reshape(C, 16, 2)
    k["ffn2_dbias"] = x["L2_ffn_bd"]
    t = lambda a: a.transpose(0, 2, 1)
    ffn(3, [(x["L3_ffn_sw1"].T[None], x["L3_ffn_sw3"].T[None], x["L3_ffn_sw2"].T[None]),
            (t(x["L3_ffn_w1"]), t(x["L3_ffn_w3"]), t(x["L3_ffn_w2"]))])
    k["rt1_w"], k["rt2_w"], k["rt3_w"] = chunks(x["L1_ffn_Wr"]), chunks(x["L2_ffn_Wr"]), chunks(x["L3_ffn_gate_w"].T)
    k["rt2_b"] = np.tile(x["L2_ffn_br"], (PT, 1))
    return k


LAST = 8


def kernel(**inputs):
    import concourse.bacc as _bacc
    from concourse.bass_utils import run_bass_kernel_spmd as _run
    nc = _bacc.Bacc("TRN2", target_bir_lowering=False, num_devices=1)
    arrays = {**layouts({n: np.asarray(a) for n, a in inputs.items()}), **shape_constants()}
    arrays = {f"in_{n}": np.ascontiguousarray(a) for n, a in arrays.items()}
    I = {n[3:]: nc.dram_tensor(n, a.shape, F32, kind="ExternalInput").ap() for n, a in arrays.items()}
    I["rel_scratch"] = nc.dram_tensor("rel_scratch", (N, H * SHIFTS), F32, kind="Internal").ap()
    for layer in (1, 2, 3):
        I[f"comb_scratch{layer}"] = nc.dram_tensor(f"comb_scratch{layer}", (FFN[layer][1], N), F32, kind="Internal").ap()
    I["kept_scratch"] = nc.dram_tensor("kept_scratch", (FFN[1][1], N), F32, kind="Internal").ap()
    out = nc.dram_tensor("out", (N, D), F32, kind="ExternalOutput").ap()
    tower(nc, I, out, LAST)
    got = _run(nc, [arrays], core_ids=[0]).results[0]["out"]
    return got.reshape(B, T, D)
```

```python
from contextlib import ExitStack

import numpy as np
import concourse.bass as bass
from concourse import mybir

F32 = mybir.dt.float32
BF16 = mybir.dt.bfloat16
F16 = mybir.dt.float16
ACT = mybir.ActivationFunctionType
ALU = mybir.AluOpType
AX = mybir.AxisListType

B, T, D, H = 16, 37, 192, 12
HD = D // H
N = B * T
NP, PT = B // 2, 2 * T
C = D // 2
HC = H // 2
HALF = N // 2
G, GH = 4, 3
GK, GD = GH * T, GH * HD
SECOND = 64
SR = SECOND + T
BANK = 512
SPLIT = 256.0
LN_EPS = 1e-5
L2_EPS = 1e-6
TERNARY_EPS = 1e-5
NEG = -1e30
SCALE = HD ** -0.5
MAX_REL = 16
SHIFTS = 2 * T - 1
SN, SP, SH = 8, 4, 24
SLOTS = SN * SP
CAPACITY = -(-N * 2 * 5 // (8 * 4))

FFN = {1: (6, 8, 6, 128, 1), 2: (0, 8, 2, 96, 2), 3: (8, 16, 4, 128, 1)}


SEMAPHORES = []


def alloc(nc, ctx):
    def sb(name, shape, dt=F32):
        return ctx.enter_context(nc.sbuf_tensor(name, shape, dt))

    def ps(name, shape, dt=F32):
        return ctx.enter_context(nc.psum_tensor(name, shape, dt))

    def sem(name):
        SEMAPHORES.append(nc.alloc_semaphore(name))
        return SEMAPHORES[-1]
    return sb, ps, sem


def reset_semaphores(nc):
    nc.clear_and_free_semaphores(SEMAPHORES)
    nc.all_engine_barrier()
    SEMAPHORES.clear()


def patch_embedding(nc, I, h):
    with ExitStack() as ctx:
        sb, ps, sem = alloc(nc, ctx)
        KC = I["patches"].shape[1]
        x = sb("tok_x", [128, KC, N])
        w = sb("tok_w", [128, KC, D])
        pos = sb("tok_pos", [PT, D])
        first = sb("tok_first", [PT, D])
        acc = ps("tok_acc", [PT, NP, BANK])
        loaded = [sem(f"tok_loaded{k}") for k in range(KC)]
        small = sem("tok_small_loaded")
        summed = sem("tok_const_summed")
        product = sem("tok_product_ready")
        done = sem("tok_done")
        with nc.Block() as block:
            @block.sync
            def _(sp):
                for k in range(KC):
                    sp.dma_start(w[:, k, :], I["tok_w"][:, k, :]).then_inc(loaded[k], 16)
                    sp.dma_start(x[:, k, :], I["patches"][:, k, :]).then_inc(loaded[k], 16)
                sp.dma_start(pos[:, :], I["tok_pos"]).then_inc(small, 16)
                sp.dma_start(first[:, :], I["tok_first"]).then_inc(small, 16)

            @block.tensor
            def _(pe):
                for k in range(KC):
                    pe.wait_ge(loaded[k], 32)
                    for j in range(NP):
                        mm = pe.matmul(acc[:, j, 0:D], lhsT=x[:, k, j * PT:(j + 1) * PT], rhs=w[:, k, :],
                                       start=(k == 0), stop=(k == KC - 1))
                        if k == KC - 1:
                            mm.then_inc(product, 1)

            @block.vector
            def _(dve):
                dve.wait_ge(small, 32)
                dve.tensor_tensor(pos[:, :], pos[:, :], first[:, :], ALU.add).then_inc(summed, 1)
                dve.wait_ge(summed, 1)
                for j in range(NP):
                    dve.wait_ge(product, j + 1)
                    dve.tensor_tensor(h[:, j, :], acc[:, j, 0:D], pos[:, :], ALU.add).then_inc(done, 1)


def to_feature_major(nc, src, dst, ident, tag, split=None):
    with ExitStack() as ctx:
        sb, ps, sem = alloc(nc, ctx)
        tp = ps(tag + "_tp", [C, 4, BANK])
        ready = sem(tag + "_tp_ready")
        copied = sem(tag + "_tp_copied")
        rest = D - 128
        if split:
            wide = ps(tag + "_wide", [128, 4, BANK])
            high = sb(tag + "_high", [128, 2, HALF], F16)
            twice = sb(tag + "_twice", [PT, NP, 2, rest])
            doubled = sem(tag + "_doubled")
            w_ready = sem(tag + "_wide_ready")
            w_high = sem(tag + "_high_ready")
            w_low = sem(tag + "_low_ready")
        with nc.Block() as block:
            @block.tensor
            def _(pe):
                for half in range(2):
                    for c in range(2):
                        for q in range(NP // 2):
                            j = half * (NP // 2) + q
                            mm = pe.transpose(tp[:, 2 * half + c, q * PT:(q + 1) * PT],
                                              src[:, j, c * C:(c + 1) * C], ident[0:PT, 0:PT])
                        mm.then_inc(ready, 1)
                if split:
                    pe.wait_ge(doubled, 1)
                    for half in range(2):
                        for q in range(NP // 2):
                            j = half * (NP // 2) + q
                            pe.transpose(wide[:, 2 * half, q * PT:(q + 1) * PT], src[:, j, 0:128], ident[0:PT, 0:PT])
                        for q in range(NP // 2):
                            j = half * (NP // 2) + q
                            mm = pe.transpose(wide[:, 2 * half + 1, q * PT:(q + 1) * PT],
                                              twice[:, j, :, :].rearrange("p a f -> p (a f)"), ident[0:PT, 0:PT])
                        mm.then_inc(w_ready, 1)

            @block.scalar
            def _(act):
                if split:
                    act.activation(twice[:, :, :, :], src[:, :, 128:D].unsqueeze(2).to_broadcast([PT, NP, 2, rest]),
                                   ACT.Copy).then_inc(doubled, 1)
                for half in range(2):
                    cols = slice(half * HALF, (half + 1) * HALF)
                    for c in range(2):
                        act.wait_ge(ready, 2 * half + c + 1)
                        act.activation(dst[:, c, cols], tp[:, 2 * half + c, 0:HALF], ACT.Copy).then_inc(copied, 1)
                if split:
                    for half in range(2):
                        cols = slice(half * HALF, (half + 1) * HALF)
                        act.wait_ge(w_ready, half + 1)
                        act.activation(split[0][:, cols], wide[:, 2 * half, 0:HALF], ACT.Copy, scale=SPLIT).then_inc(w_high, 1)
                        act.activation(split[1][0:rest, cols], wide[0:rest, 2 * half + 1, 0:HALF], ACT.Copy,
                                       scale=SPLIT).then_inc(w_high, 1)
                        act.activation(high[rest:128, half, :], wide[rest:128, 2 * half + 1, 0:HALF], ACT.Copy,
                                       scale=SPLIT).then_inc(w_high, 1)

            @block.vector
            def _(dve):
                if split:
                    for half in range(2):
                        cols = slice(half * HALF, (half + 1) * HALF)
                        dve.wait_ge(w_high, 3 * half + 3)
                        dve.scalar_tensor_tensor(split[2][:, cols], wide[:, 2 * half, 0:HALF], SPLIT, split[0][:, cols],
                                                 ALU.mult, ALU.subtract).then_inc(w_low, 1)
                        dve.scalar_tensor_tensor(split[1][rest:128, cols], wide[rest:128, 2 * half + 1, 0:HALF], SPLIT,
                                                 high[rest:128, half, :], ALU.mult, ALU.subtract).then_inc(w_low, 1)


def layer_norm(nc, h, tag, unit=None, power=None):
    with ExitStack() as ctx:
        sb, ps, sem = alloc(nc, ctx)
        st = sb(tag + "_stats", [PT, NP, 6])
        mv = sb(tag + "_mean_var", [PT, NP, 2])
        rstd = sb(tag + "_rstd", [PT, NP])
        sq = sb(tag + "_squares", [PT, NP, D])
        length = sb(tag + "_length", [PT, NP])
        stats = sem(tag + "_stats_ready")
        aggr = sem(tag + "_aggregated")
        eps = sem(tag + "_eps_added")
        root = sem(tag + "_root_ready")
        norm = sem(tag + "_normalised")
        summed = sem(tag + "_squares_summed")
        rooted = sem(tag + "_length_ready")
        with nc.Block() as block:
            @block.vector
            def _(dve):
                for j in range(NP):
                    dve.bn_stats(st[:, j, :], h[:, j, :]).then_inc(stats, 1)
                for j in range(NP):
                    dve.wait_ge(stats, j + 1)
                    dve.bn_aggr(mv[:, j, :], st[:, j, :]).then_inc(aggr, 1)
                dve.wait_ge(root, 1)
                for j in range(NP):
                    dve.tensor_scalar(h[:, j, :], h[:, j, :], mv[:, j, 0:1], rstd[:, j:j + 1],
                                      ALU.subtract, ALU.mult).then_inc(norm, 1)
                if unit is not None:
                    dve.wait_ge(norm, NP)
                    dve.tensor_tensor(sq[:, :, :], h[:, :, :], h[:, :, :], ALU.mult).then_inc(summed, 1)
                    dve.wait_ge(summed, 1)
                    dve.tensor_reduce(length[:, :], sq[:, :, :], AX.X, ALU.add).then_inc(summed, 1)
                    dve.wait_ge(rooted, 1)
                    dve.tensor_scalar(length[:, :], length[:, :], L2_EPS, None, ALU.add).then_inc(rooted, 1)
                    dve.wait_ge(rooted, 2)
                    dve.reciprocal(length[:, :], length[:, :]).then_inc(rooted, 1)
                    dve.wait_ge(rooted, 3)
                    dve.tensor_tensor(unit[:, :, :], h[:, :, :],
                                      length[:, :].unsqueeze(2).to_broadcast([PT, NP, D]), ALU.mult).then_inc(rooted, 1)

            @block.gpsimd
            def _(pool):
                pool.wait_ge(aggr, NP)
                pool.tensor_scalar(rstd[:, :], mv[:, :, 1], LN_EPS, None, ALU.add).then_inc(eps, 1)
                pool.wait_ge(eps, 1)
                pool.tensor_tensor(rstd[:, :], rstd[:, :], power[:, 0, :], ALU.pow).then_inc(root, 1)
                if unit is not None:
                    pool.wait_ge(summed, 2)
                    pool.tensor_tensor(length[:, :], length[:, :], power[:, 1, :], ALU.pow).then_inc(rooted, 1)


def attention(nc, I, layer, h, hT, const):
    rope, rel = layer == 1, layer == 2
    p = f"att{layer}"
    ident = const["ident"]
    kinds = ["q", "qs", "k", "ks"] if rope else ["q", "k"]
    with ExitStack() as ctx:
        sb, ps, sem = alloc(nc, ctx)
        w = {n: sb(f"{p}_w{n}", [C, 2, D]) for n in kinds + ["v"]}
        wp = sb(p + "_wp", [GD, G, D])
        bias = sb(p + "_bias", [C, 2, len(kinds)])
        bv = sb(p + "_bv", [GD, G, PT])
        bp = sb(p + "_bp", [PT, D])
        qT = sb(p + "_qT", [C, 2, N])
        kT = sb(p + "_kT", [C, 2, N])
        biases = sb(p + "_score_bias", [SR, 2, H * T])
        causal = None if rel else sb(p + "_causal", [SR, H * T], BF16)
        if rope:
            table = sb(p + "_rope", [C, 2, T])
            turned = sb(p + "_turned", [C, 2, HALF])
            straight = sb(p + "_straight", [C, 2, HALF])
        if rel:
            rbd = sb(p + "_rel", [C, HC * SHIFTS])
            grid = sb(p + "_rel_grid", [PT, 4, 2 * HC * SHIFTS])
            grid_dram = I["rel_scratch"]
        loaded = sem(p + "_loaded")
        biased = sem(p + "_score_bias_ready")
        grid_copied = sem(p + "_grid_copied")
        grid_stored = [sem(f"{p}_grid_stored{i}") for i in range(4)]

        with ExitStack() as pre:
            _, pps, psem = alloc(nc, pre)
            acc = pps(p + "_acc", [128, 8, BANK])
            product = psem(p + "_product_ready")
            taken = psem(p + "_product_taken")
            gridded = psem(p + "_grid_ready")
            mask_loaded = psem(p + "_mask_loaded")
            kept = psem(p + "_residual_ready")
            KN = len(kinds)
            with nc.Block() as block:
                @block.sync
                def _(sp):
                    for n in kinds + ["v"]:
                        sp.dma_start(w[n][:, :, :], I[f"{p}_w{n}"]).then_inc(loaded, 16)
                    sp.dma_start(bias[:, :, :], I[p + "_bias"]).then_inc(loaded, 16)
                    sp.dma_start(wp[:, :, :], I[p + "_wp"]).then_inc(loaded, 16)
                    sp.dma_start(bv[:, :, :], I[p + "_bv"]).then_inc(loaded, 16)
                    sp.dma_start(bp[:, :], I[p + "_bp"]).then_inc(loaded, 16)
                    if rope:
                        sp.dma_start(table[:, :, :], I["rope"]).then_inc(loaded, 16)
                    if rel:
                        sp.dma_start(rbd[:, :], I["rel_blocks"]).then_inc(loaded, 16)
                    else:
                        sp.dma_start(biases[:, 0, :], I["causal"]).then_inc(mask_loaded, 16)
                    if rel:
                        for j in range(NP):
                            sp.wait_ge(grid_copied, 2 * j + 2)
                            sp.dma_start(grid_dram[j * PT:(j + 1) * PT, :], grid[:, j % 4, :]).then_inc(grid_stored[j % 4], 16)

                LOADS = 16 * (KN + 1 + 4 + rope + rel)

                @block.gpsimd
                def _(pool):
                    if rel:
                        pool.memset(biases[:, :, :], 0.0).then_inc(biased, 1)
                    else:
                        pool.wait_ge(mask_loaded, 16)
                        pool.tensor_copy(causal[:, :], biases[:, 0, :]).then_inc(biased, 1)

                @block.tensor
                def _(pe):
                    pe.wait_ge(loaded, LOADS)
                    for s in range(4):
                        co, half = s // 2, s % 2
                        for m, n in enumerate(kinds):
                            bank = (s * KN + m) % 8
                            if s * KN + m >= 8:
                                pe.wait_ge(taken, s * KN + m - 7)
                            for ci in range(2):
                                mm = pe.matmul(acc[0:C, bank, 0:HALF], lhsT=w[n][:, ci, co * C:(co + 1) * C],
                                               rhs=hT[:, ci, half * HALF:(half + 1) * HALF],
                                               start=(ci == 0), stop=(ci == 1))
                            mm.then_inc(product, 1)
                    n0 = 4 * KN
                    pe.wait_ge(taken, n0 - 7)
                    for g in range(G):
                        mm = pe.matmul(acc[0:PT, n0 % 8, 0:D], lhsT=bv[:, g, :], rhs=wp[:, g, :],
                                       start=(g == 0), stop=(g == G - 1))
                    mm.then_inc(product, 1)
                    if rel:
                        pe.wait_ge(taken, 4 * KN)
                        for j in range(NP):
                            for ci in range(2):
                                s = 2 * j + ci
                                bank = 1 + s % 6
                                if s >= 6:
                                    pe.wait_ge(grid_copied, s - 5)
                                pe.matmul(acc[0:PT, bank, 0:HC * SHIFTS], lhsT=qT[:, ci, j * PT:(j + 1) * PT],
                                          rhs=rbd[:, :], start=True, stop=True).then_inc(gridded, 1)

                @block.scalar
                def _(act):
                    if not rope:
                        act.wait_ge(loaded, LOADS)
                        for s in range(4):
                            co, half = s // 2, s % 2
                            for m, n in enumerate(kinds):
                                act.wait_ge(product, s * KN + m + 1)
                                dst = qT if n == "q" else kT
                                act.activation(dst[:, co, half * HALF:(half + 1) * HALF],
                                               acc[0:C, (s * KN + m) % 8, 0:HALF], ACT.Identity,
                                               bias=bias[:, co, m:m + 1]).then_inc(taken, 1)
                    if rel:
                        for s in range(2 * NP):
                            j, ci = s // 2, s % 2
                            act.wait_ge(gridded, s + 1)
                            if j >= 4:
                                act.wait_ge(grid_stored[j % 4], 16)
                            act.activation(grid[:, j % 4, ci * HC * SHIFTS:(ci + 1) * HC * SHIFTS],
                                           acc[0:PT, 1 + s % 6, 0:HC * SHIFTS], ACT.Copy).then_inc(grid_copied, 1)

                @block.vector
                def _(dve):
                    dve.wait_ge(loaded, LOADS)
                    if rope:
                        for s in range(4):
                            co, half = s // 2, s % 2
                            for m in range(2):
                                dst = (qT, kT)[m]
                                for t in range(2):
                                    n = s * KN + 2 * m + t
                                    dve.wait_ge(product, n + 1)
                                    src = acc[0:C, n % 8, 0:HALF].rearrange("p (b t) -> p b t", t=T)
                                    out = (straight, turned)[t][:, m, :].rearrange("p (b t) -> p b t", t=T)
                                    dve.scalar_tensor_tensor(out, src, bias[:, co, 2 * m + t:2 * m + t + 1],
                                                             table[:, t, :].unsqueeze(1).to_broadcast([C, B // 2, T]),
                                                             ALU.add, ALU.mult).then_inc(taken, 1)
                                dve.wait_ge(taken, s * KN + 2 * m + 2)
                                dve.tensor_tensor(dst[:, co, half * HALF:(half + 1) * HALF], straight[:, m, :],
                                                  turned[:, m, :], ALU.add)
                    dve.tensor_tensor(h[:, :, :], h[:, :, :], bp[:, :].unsqueeze(1).to_broadcast([PT, NP, D]),
                                      ALU.add).then_inc(kept, 1)
                    dve.wait_ge(product, 4 * KN + 1)
                    dve.wait_ge(kept, 1)
                    dve.tensor_tensor(h[:, :, :], h[:, :, :],
                                      acc[0:PT, 4 * KN % 8, 0:D].unsqueeze(1).to_broadcast([PT, NP, D]),
                                      ALU.add).then_inc(kept, 1)

        with ExitStack() as main:
            msb, mps, msem = alloc(nc, main)
            q_stage = msb(p + "_q_stage", [C, 2, 2, PT])
            x_stage = msb(p + "_x_stage", [C, 2, 2, 2, GH, T])
            k_blocks = msb(p + "_k_blocks", [C, 2, 2, 2, HC, T])
            probs = msb(p + "_probs", [SR, 2, H * T])
            probsT = msb(p + "_probsT", [GK, 2, G, SR])
            v_blocks = msb(p + "_v_blocks", [GK, 2, 2, D])
            oT = msb(p + "_oT", [GD, 2, G, PT])
            peak = msb(p + "_peak", [SR, 2, H])
            total = msb(p + "_total", [SR, 2, H])
            s_ps = mps(p + "_s", [128, 2, BANK])
            t_ps = mps(p + "_t", [128, 2, BANK])
            v_ps = mps(p + "_v", [128, 2, BANK])
            oy_ps = mps(p + "_oy", [128, 2, BANK])
            staged = msem(p + "_staged")
            x_staged = msem(p + "_x_staged")
            values = msem(p + "_values_ready")
            scores = msem(p + "_scores_ready")
            peaked = msem(p + "_peak_ready")
            shifted = msem(p + "_shifted")
            exped = msem(p + "_exponentials_ready")
            totaled = msem(p + "_totals_ready")
            inverted = msem(p + "_inverted")
            weighted = msem(p + "_probs_ready")
            v_ready = msem(p + "_v_blocks_ready")
            turned_s = msem(p + "_probsT_ready")
            pT_copied = msem(p + "_probsT_copied")
            o_ready = msem(p + "_outputs_ready")
            o_copied = msem(p + "_outputs_copied")
            y_ready = msem(p + "_projected")
            added = msem(p + "_added")
            rel_loaded = [msem(f"{p}_rel_loaded{k}") for k in range(2)]

            def y_of(k):
                return oy_ps[0:PT, k, G * PT:G * PT + D]

            with nc.Block() as block:
                @block.sync
                def _(sp):
                    if rel:
                        for i in range(4):
                            sp.wait_ge(grid_stored[i], 32)

                        def rel_pair(i, k, later):
                            if later:
                                sp.wait_ge(scores, 2 * i + k - 1)
                            for img in range(2):
                                src = bass.AP(grid_dram.tensor, (2 * i + k) * (PT * H * SHIFTS) + img * T * H * SHIFTS + T - 1,
                                              [[H * SHIFTS - 1, T], [SHIFTS, H], [1, T]])
                                dst = biases[img * SECOND:img * SECOND + T, k, :].rearrange("p (h t) -> p h t", h=H)
                                sp.dma_start(dst, src).then_inc(rel_loaded[k], 16)
                        for k in range(2):
                            rel_pair(0, k, False)
                        with sp.Fori(1, NP // 2) as i:
                            for k in range(2):
                                rel_pair(i, k, True)

                @block.gpsimd
                def _(pool):
                    def body(i, later):
                        for k in range(2):
                            j = 2 * i + k
                            if later:
                                pool.wait_ge(scores, j - 1)
                            pool.tensor_copy(q_stage[:, k, :, :], qT[:, :, bass.ds(j * PT, PT)]).then_inc(staged, 1)
                            for c in range(2):
                                pool.tensor_tensor(k_blocks[:, k, c, :, :, :],
                                                   kT[:, c, bass.ds(j * PT, PT)].rearrange("p (b t) -> p b t", b=2)
                                                   .unsqueeze(2).to_broadcast([C, 2, HC, T]),
                                                   const["own_head"][:, :].unsqueeze(1).unsqueeze(3)
                                                   .to_broadcast([C, 2, HC, T]), ALU.mult).then_inc(staged, 1)
                    body(0, False)
                    with pool.Fori(1, NP // 2) as i:
                        body(i, True)

                @block.tensor
                def _(pe):
                    if not rel:
                        pe.wait_ge(biased, 1)

                    def value(i, k, later):
                        j = 2 * i + k
                        pe.wait_ge(x_staged, 2 * j + 2)
                        if later:
                            pe.wait_ge(v_ready, j - 1)
                        for img in range(2):
                            for c in range(2):
                                mm = pe.matmul(v_ps[0:GK, k, img * D:(img + 1) * D],
                                               lhsT=x_stage[:, k, c, img, :, :].rearrange("p a t -> p (a t)"),
                                               rhs=w["v"][:, c, :], start=(c == 0), stop=(c == 1))
                        mm.then_inc(values, 1)

                    def score(i, k, later):
                        j = 2 * i + k
                        pe.wait_ge(staged, 3 * j + 3)
                        if later:
                            pe.wait_ge(shifted, j - 1)
                        if rel:
                            pe.wait_ge(rel_loaded[k], 32 * i + 32)
                            pe.matmul(s_ps[0:SR, k, 0:H * T], lhsT=ident[0:SR, 0:SR], rhs=biases[:, k, :],
                                      start=True, stop=False, skip_group_check=True)
                        else:
                            pe.matmul(s_ps[0:SR, k, 0:H * T], lhsT=const["identb"][0:SR, 0:SR], rhs=causal[:, :],
                                      start=True, stop=False, skip_group_check=True)
                        for c in range(2):
                            for img in range(2):
                                mm = pe.matmul(s_ps[img * SECOND:img * SECOND + T, k, c * HC * T:(c + 1) * HC * T],
                                               lhsT=q_stage[:, k, c, img * T:(img + 1) * T],
                                               rhs=k_blocks[:, k, c, img, :, :].rearrange("p a t -> p (a t)"),
                                               start=False, stop=True, skip_group_check=True)
                        mm.then_inc(scores, 1)

                    def body(i, later, more):
                        for k in range(2):
                            t = 2 * i + k
                            pe.wait_ge(weighted, t + 1)
                            if later:
                                pe.wait_ge(pT_copied, t - 1)
                            for g in range(G):
                                mm = pe.transpose(t_ps[0:GK, k, g * SR:(g + 1) * SR],
                                                  probs[:, k, g * GK:(g + 1) * GK], ident[0:SR, 0:SR])
                            mm.then_inc(turned_s, 1)
                            if more:
                                value(i + 1, k, True)
                            pe.wait_ge(pT_copied, t + 1)
                            pe.wait_ge(v_ready, t + 1)
                            if later:
                                pe.wait_ge(added, t - 1)
                            for img in range(2):
                                for g in range(G):
                                    mm = pe.matmul(oy_ps[0:GD, k, g * PT + img * T:g * PT + (img + 1) * T],
                                                   lhsT=v_blocks[:, k, img, g * GD:(g + 1) * GD],
                                                   rhs=probsT[:, k, g, img * SECOND:img * SECOND + T],
                                                   start=True, stop=True)
                            mm.then_inc(o_ready, 1)
                            if more:
                                score(i + 1, k, True)
                            pe.wait_ge(o_copied, t + 1)
                            for g in range(G):
                                mm = pe.matmul(y_of(k), lhsT=oT[:, k, g, :], rhs=wp[:, g, :],
                                               start=(g == 0), stop=(g == G - 1))
                            mm.then_inc(y_ready, 1)
                    for k in range(2):
                        value(0, k, False)
                        score(0, k, False)
                    body(0, False, True)
                    with pe.Fori(1, NP // 2 - 1) as i:
                        body(i, True, True)
                    body(NP // 2 - 1, True, False)

                @block.scalar
                def _(act):
                    def stage_x(j, k, later):
                        if later:
                            act.wait_ge(values, j - 1)
                        for c in range(2):
                            act.activation(x_stage[:, k, c, :, :, :],
                                           hT[:, c, bass.ds(j * PT, PT)].rearrange("p (b t) -> p b t", b=2)
                                           .unsqueeze(2).to_broadcast([C, 2, GH, T]), ACT.Copy).then_inc(x_staged, 1)

                    def exponentials(t, k):
                        act.wait_ge(shifted, t + 1)
                        act.activation(probs[:, k, :], probs[:, k, :], ACT.Exp, scale=SCALE).then_inc(exped, 1)

                    def body(i, later, left):
                        for k in range(2):
                            t = 2 * i + k
                            act.wait_ge(turned_s, t + 1)
                            if later:
                                act.wait_ge(o_ready, t - 1)
                            act.activation(probsT[:, k, :, :].rearrange("p g s -> p (g s)"), t_ps[0:GK, k, 0:G * SR],
                                           ACT.Copy).then_inc(pT_copied, 1)
                            if left or k == 0:
                                exponentials(t + 1, 1 - k)
                            act.wait_ge(o_ready, t + 1)
                            if later:
                                act.wait_ge(y_ready, t - 1)
                            act.activation(oT[:, k, :, :].rearrange("p g s -> p (g s)"), oy_ps[0:GD, k, 0:G * PT],
                                           ACT.Copy).then_inc(o_copied, 1)
                            if left >= 2 + k:
                                stage_x(t + 3, 1 - k, True)
                    stage_x(0, 0, False)
                    stage_x(1, 1, False)
                    exponentials(0, 0)
                    stage_x(2, 0, True)
                    body(0, False, NP - 2)
                    with act.Fori(1, NP // 2 - 2) as i:
                        body(i, True, 4)
                    body(NP // 2 - 2, True, 2)
                    body(NP // 2 - 1, True, 0)

                @block.vector
                def _(dve):
                    def heads(t):
                        return t.rearrange("p (h t) -> p h t", h=H)

                    def shift(n, k, later):
                        dve.wait_ge(scores, n + 1)
                        dve.tensor_reduce(peak[:, k, :], heads(s_ps[0:SR, k, 0:H * T]), AX.X, ALU.max).then_inc(peaked, 1)
                        dve.wait_ge(peaked, n + 1)
                        if later:
                            dve.wait_ge(turned_s, n - 1)
                        dve.tensor_tensor(heads(probs[:, k, :]), heads(s_ps[0:SR, k, 0:H * T]),
                                          peak[:, k, :].unsqueeze(2).to_broadcast([SR, H, T]),
                                          ALU.subtract).then_inc(shifted, 1)

                    def value_blocks(n, k, later):
                        dve.wait_ge(values, n + 1)
                        if later:
                            dve.wait_ge(o_ready, n - 1)
                        dve.tensor_tensor(v_blocks[:, k, :, :],
                                          v_ps[0:GK, k, 0:2 * D].rearrange("p (b f) -> p b f", b=2),
                                          const["own_key"][:, :].unsqueeze(1).to_broadcast([GK, 2, D]),
                                          ALU.mult).then_inc(v_ready, 1)

                    def add(t, k):
                        dve.wait_ge(y_ready, t + 1)
                        hj = h[:, bass.ds(t, 1), :].rearrange("p a d -> p (a d)")
                        dve.tensor_tensor(hj, hj, y_of(k), ALU.add).then_inc(added, 1)

                    def body(i, later, more):
                        for k in range(2):
                            t = 2 * i + k
                            dve.wait_ge(exped, t + 1)
                            dve.tensor_reduce(total[:, k, :], heads(probs[:, k, :]), AX.X, ALU.add).then_inc(totaled, 1)
                            dve.wait_ge(totaled, t + 1)
                            dve.reciprocal(total[:, k, :], total[:, k, :]).then_inc(inverted, 1)
                            dve.wait_ge(inverted, t + 1)
                            dve.tensor_tensor(heads(probs[:, k, :]), heads(probs[:, k, :]),
                                              total[:, k, :].unsqueeze(2).to_broadcast([SR, H, T]),
                                              ALU.mult).then_inc(weighted, 1)
                            if more or k == 0:
                                shift(t + 1, 1 - k, later or k == 1)
                                value_blocks(t + 1, 1 - k, later or k == 1)
                            if later or k == 1:
                                add(t - 1, 1 - k)
                    shift(0, 0, False)
                    value_blocks(0, 0, False)
                    body(0, False, True)
                    with dve.Fori(1, NP // 2 - 1) as i:
                        body(i, True, True)
                    body(NP // 2 - 1, True, False)
                    add(NP - 1, 1)


def soft_mixture(nc, I, h, unit, unitT, const):
    ident = const["ident"]
    with ExitStack() as ctx:
        sb, ps, sem = alloc(nc, ctx)
        slots = sb("sm_slots", [C, 2, SLOTS])
        squares = sb("sm_squares", [C, 2, SLOTS])
        length = sb("sm_length", [C, 2, SP])
        scale = sb("sm_scale", [C, 1])
        down = sb("sm_down", [C, 2, D])
        bdown = sb("sm_bdown", [C, 2])
        up = sb("sm_up", [C, 2, D])
        bup = sb("sm_bup", [128, D])
        own_expert = sb("sm_own_expert", [C, 2, SLOTS])
        own_image = sb("sm_own_image", [PT, 2])
        own_image4 = sb("sm_own_image4", [PT, 2, 4])
        logitsT = sb("sm_logitsT", [SLOTS, N])
        dispT = sb("sm_dispT", [SLOTS, N])
        comb = sb("sm_comb", [PT, NP, SLOTS])
        peak = sb("sm_peak", [SLOTS, B])
        total = sb("sm_total", [SLOTS, B])
        cpeak = sb("sm_cpeak", [PT, NP])
        ctotal = sb("sm_ctotal", [PT, NP])
        dispatch = sb("sm_dispatch", [PT, NP, 2, SLOTS])
        combine = sb("sm_combine", [PT, NP, 4, SLOTS])
        combineT = sb("sm_combineT", [128, NP, PT])
        slotT = sb("sm_slotT", [C, 2, B * SLOTS])
        hidden = sb("sm_hidden", [C, 2, B * SLOTS])
        masked = sb("sm_masked", [C, 2, B * SLOTS])
        out = sb("sm_out", [128, 4, D])
        l_ps = ps("sm_l_ps", [128, 2, BANK])
        t_ps = ps("sm_t_ps", [128, 2, BANK])
        c_ps = ps("sm_c_ps", [128, 2, BANK])
        y_ps = ps("sm_y_ps", [128, 2, BANK])
        loaded = sem("sm_loaded")
        slots_ready = sem("sm_slots_step")
        rooted = sem("sm_slot_lengths_ready")
        logits = sem("sm_logits_ready")
        kept = sem("sm_logits_kept")
        step = sem("sm_vector_step")
        exped = sem("sm_exponentials_ready")
        shifted = sem("sm_shifted")
        turned = sem("sm_transposed")
        disp = sem("sm_dispT_ready")
        dready = sem("sm_dispatch_ready")
        cready = sem("sm_combine_ready")
        slotted = sem("sm_slot_inputs_ready")
        slots_kept = sem("sm_slot_inputs_kept")
        hid = sem("sm_hidden_product_ready")
        gelued = sem("sm_gelu_ready")
        mready = sem("sm_masked_ready")
        oready = sem("sm_out_product_ready")
        okept = sem("sm_out_kept")
        cturned = sem("sm_combine_transposed")
        ckept = sem("sm_combineT_kept")
        yready = sem("sm_result_ready")
        added = sem("sm_added")

        with nc.Block() as block:
            @block.sync
            def _(sp):
                for dst, name in ((slots, "sm_slots"), (scale, "sm_scale"), (down, "sm_down"), (bdown, "sm_bdown"),
                                  (up, "sm_up"), (bup, "sm_bup"), (own_expert, "sm_own_expert"),
                                  (own_image, "sm_own_image"), (own_image4, "sm_own_image4")):
                    src = I[name]
                    sp.dma_start(dst[tuple(slice(None) for _ in dst.shape)], src).then_inc(loaded, 16)

            @block.gpsimd
            def _(pool):
                pool.wait_ge(slots_ready, 2)
                pool.tensor_tensor(length[:, :, :], length[:, :, :],
                                   const["half"][:, :, :], ALU.pow).then_inc(rooted, 1)

            @block.tensor
            def _(pe):
                pe.wait_ge(slots_ready, 6)
                for half in range(2):
                    for c in range(2):
                        mm = pe.matmul(l_ps[0:SLOTS, half, 0:HALF], lhsT=slots[:, c, :],
                                       rhs=unitT[:, c, half * HALF:(half + 1) * HALF], start=(c == 0), stop=(c == 1))
                    mm.then_inc(logits, 1)
                pe.wait_ge(kept, 2)
                for j in range(NP):
                    mm = pe.transpose(t_ps[0:PT, 0, j * SLOTS:(j + 1) * SLOTS], logitsT[:, j * PT:(j + 1) * PT],
                                      ident[0:SLOTS, 0:SLOTS])
                mm.then_inc(turned, 1)
                pe.wait_ge(disp, 1)
                for j in range(NP):
                    mm = pe.transpose(t_ps[0:PT, 1, j * SLOTS:(j + 1) * SLOTS], dispT[:, j * PT:(j + 1) * PT],
                                      ident[0:SLOTS, 0:SLOTS])
                mm.then_inc(turned, 1)
                pe.wait_ge(dready, 1)
                for c in range(2):
                    for j in range(NP):
                        mm = pe.matmul(l_ps[0:C, c, j * 2 * SLOTS:(j + 1) * 2 * SLOTS], lhsT=unit[:, j, c * C:(c + 1) * C],
                                       rhs=dispatch[:, j, :, :].rearrange("p b s -> p (b s)"), start=True, stop=True)
                    mm.then_inc(slotted, 1)
                pe.wait_ge(cready, 2)
                for j in range(NP):
                    mm = pe.transpose(c_ps[:, j // 4, (j % 4) * PT:(j % 4 + 1) * PT],
                                      combine[:, j, :, :].rearrange("p b s -> p (b s)"), ident[0:PT, 0:PT])
                mm.then_inc(cturned, 1)
                pe.wait_ge(slots_kept, 2)
                for e in range(2):
                    for c in range(2):
                        mm = pe.matmul(l_ps[0:C, e, :], lhsT=down[:, c, e * C:(e + 1) * C], rhs=slotT[:, c, :],
                                       start=(c == 0), stop=(c == 1))
                    mm.then_inc(hid, 1)
                pe.wait_ge(mready, 2)
                for q in range(4):
                    for e in range(2):
                        mm = pe.matmul(t_ps[:, q // 2, (q % 2) * D:(q % 2 + 1) * D], lhsT=masked[:, e, q * 128:(q + 1) * 128],
                                       rhs=up[:, e, :], start=(e == 0), stop=(e == 1))
                mm.then_inc(oready, 1)
                pe.wait_ge(okept, 2)
                pe.wait_ge(ckept, 2)
                for j in range(NP):
                    if j >= 2:
                        pe.wait_ge(added, j - 1)
                    pe.matmul(y_ps[0:PT, j % 2, 0:D], lhsT=combineT[:, j, :], rhs=out[:, j // 2, :],
                              start=True, stop=True).then_inc(yready, 1)

            @block.scalar
            def _(act):
                act.wait_ge(shifted, 1)
                act.activation(dispT[:, :], dispT[:, :], ACT.Exp).then_inc(exped, 1)
                act.wait_ge(shifted, 2)
                act.activation(comb[:, :, :], comb[:, :, :], ACT.Exp).then_inc(exped, 1)
                for c in range(2):
                    act.wait_ge(slotted, c + 1)
                    act.activation(slotT[:, c, :], l_ps[0:C, c, :], ACT.Copy).then_inc(slots_kept, 1)
                act.wait_ge(cturned, 1)
                for g in range(2):
                    act.activation(combineT[:, 4 * g:4 * g + 4, :].rearrange("p j t -> p (j t)"), c_ps[:, g, 0:4 * PT],
                                   ACT.Copy).then_inc(ckept, 1)
                for e in range(2):
                    act.wait_ge(hid, e + 1)
                    act.activation(hidden[:, e, :], l_ps[0:C, e, :], ACT.Gelu, bias=bdown[:, e:e + 1]).then_inc(gelued, 1)

            @block.vector
            def _(dve):
                dve.wait_ge(loaded, 16 * 9)
                dve.tensor_tensor(squares[:, :, :], slots[:, :, :], slots[:, :, :], ALU.mult).then_inc(slots_ready, 1)
                dve.wait_ge(slots_ready, 1)
                dve.tensor_reduce(length[:, :, :], squares[:, :, :].rearrange("p c (n s) -> p c s n", n=SN), AX.X,
                                  ALU.add).then_inc(slots_ready, 1)
                dve.wait_ge(rooted, 1)
                dve.tensor_scalar(length[:, :, :], length[:, :, :], L2_EPS, None, ALU.add).then_inc(slots_ready, 1)
                dve.wait_ge(slots_ready, 3)
                dve.reciprocal(length[:, :, :], length[:, :, :]).then_inc(slots_ready, 1)
                dve.wait_ge(slots_ready, 4)
                dve.tensor_scalar(length[:, :, :], length[:, :, :], scale[:, 0:1], None, ALU.mult).then_inc(slots_ready, 1)
                dve.wait_ge(slots_ready, 5)
                dve.tensor_tensor(slots[:, :, :].rearrange("p c (n s) -> p c n s", n=SN),
                                  slots[:, :, :].rearrange("p c (n s) -> p c n s", n=SN),
                                  length[:, :, :].unsqueeze(2).to_broadcast([C, 2, SN, SP]), ALU.mult).then_inc(slots_ready, 1)
                for half in range(2):
                    dve.wait_ge(logits, half + 1)
                    dve.tensor_copy(logitsT[:, half * HALF:(half + 1) * HALF], l_ps[0:SLOTS, half, 0:HALF]).then_inc(kept, 1)
                dve.wait_ge(kept, 2)
                by_image = logitsT[:, :].rearrange("p (b t) -> p b t", t=T)
                disp_by_image = dispT[:, :].rearrange("p (b t) -> p b t", t=T)
                dve.tensor_reduce(peak[:, :], by_image, AX.X, ALU.max).then_inc(step, 1)
                dve.wait_ge(step, 1)
                dve.tensor_tensor(disp_by_image, by_image, peak[:, :].unsqueeze(2).to_broadcast([SLOTS, B, T]),
                                  ALU.subtract).then_inc(shifted, 1)
                dve.wait_ge(turned, 1)
                tok = t_ps[0:PT, 0, 0:NP * SLOTS].rearrange("p (j s) -> p j s", s=SLOTS)
                dve.tensor_reduce(cpeak[:, :], tok, AX.X, ALU.max).then_inc(step, 1)
                dve.wait_ge(step, 2)
                dve.tensor_tensor(comb[:, :, :], tok, cpeak[:, :].unsqueeze(2).to_broadcast([PT, NP, SLOTS]),
                                  ALU.subtract).then_inc(shifted, 1)
                dve.wait_ge(exped, 1)
                dve.tensor_reduce(total[:, :], disp_by_image, AX.X, ALU.add).then_inc(step, 1)
                dve.wait_ge(step, 3)
                dve.reciprocal(total[:, :], total[:, :]).then_inc(step, 1)
                dve.wait_ge(step, 4)
                dve.tensor_tensor(disp_by_image, disp_by_image, total[:, :].unsqueeze(2).to_broadcast([SLOTS, B, T]),
                                  ALU.mult).then_inc(disp, 1)
                dve.wait_ge(exped, 2)
                dve.tensor_reduce(ctotal[:, :], comb[:, :, :], AX.X, ALU.add).then_inc(step, 1)
                dve.wait_ge(step, 5)
                dve.reciprocal(ctotal[:, :], ctotal[:, :]).then_inc(step, 1)
                dve.wait_ge(step, 6)
                dve.tensor_tensor(comb[:, :, :], comb[:, :, :], ctotal[:, :].unsqueeze(2).to_broadcast([PT, NP, SLOTS]),
                                  ALU.mult).then_inc(step, 1)
                dve.wait_ge(turned, 2)
                dve.tensor_tensor(dispatch[:, :, :, :],
                                  t_ps[0:PT, 1, 0:NP * SLOTS].rearrange("p (j s) -> p j s", s=SLOTS)
                                  .unsqueeze(2).to_broadcast([PT, NP, 2, SLOTS]),
                                  own_image[:, :].unsqueeze(1).unsqueeze(3).to_broadcast([PT, NP, 2, SLOTS]),
                                  ALU.mult).then_inc(dready, 1)
                dve.wait_ge(step, 7)
                for par in range(2):
                    dve.tensor_tensor(combine[:, par:NP:2, :, :],
                                      comb[:, par:NP:2, :].unsqueeze(2).to_broadcast([PT, NP // 2, 4, SLOTS]),
                                      own_image4[:, par, :].unsqueeze(1).unsqueeze(3).to_broadcast([PT, NP // 2, 4, SLOTS]),
                                      ALU.mult).then_inc(cready, 1)
                for e in range(2):
                    dve.wait_ge(gelued, e + 1)
                    dve.tensor_tensor(masked[:, e, :].rearrange("p (b s) -> p b s", s=SLOTS),
                                      hidden[:, e, :].rearrange("p (b s) -> p b s", s=SLOTS),
                                      own_expert[:, e, :].unsqueeze(1).to_broadcast([C, B, SLOTS]), ALU.mult).then_inc(mready, 1)
                dve.wait_ge(oready, 1)
                for g in range(2):
                    dve.tensor_tensor(out[:, 2 * g:2 * g + 2, :], t_ps[:, g, 0:2 * D].rearrange("p (q d) -> p q d", q=2),
                                      bup[:, :].unsqueeze(1).to_broadcast([128, 2, D]), ALU.add).then_inc(okept, 1)
                for j in range(NP):
                    dve.wait_ge(yready, j + 1)
                    dve.tensor_tensor(h[:, j, :], h[:, j, :], y_ps[0:PT, j % 2, 0:D], ALU.add).then_inc(added, 1)


def router(nc, I, layer, hT, comb, comb_dram, const):
    shared, E, upe, M, per_body = FFN[layer]
    p = f"rt{layer}"
    ident = const["ident"]
    with ExitStack() as ctx:
        sb, ps, sem = alloc(nc, ctx)
        w = sb(p + "_w", [C, 2, E])
        order = sb(p + "_order", [PT, E])
        score = sb(p + "_score", [PT, NP, E])
        rest = sb(p + "_rest", [PT, NP, E])
        place = sb(p + "_place", [PT, NP, E])
        hot = [sb(f"{p}_hot{r}", [PT, NP, E]) for r in range(2)]
        best = [sb(f"{p}_best{r}", [PT, NP]) for r in range(2)]
        at = sb(p + "_at", [PT, NP])
        total = sb(p + "_total", [PT, NP])
        combT = sb(p + "_combT", [E, N])
        l_ps = ps(p + "_l_ps", [128, BANK])
        t_ps = ps(p + "_t_ps", [128, 2, BANK])
        rb = sb(p + "_rb", [PT, E]) if layer == 2 else None
        loaded = sem(p + "_loaded")
        logits = sem(p + "_logits_ready")
        step = sem(p + "_vector_step")
        for_exp = sem(p + "_exponents_ready")
        exped = sem(p + "_exponentials_ready")
        combined = sem(p + "_comb_ready")
        turned = sem(p + "_combT_ready")
        kept = sem(p + "_combT_kept")
        stored = sem(p + "_comb_stored")
        LOADS = 16 * (2 + (layer == 2))
        wide = [PT, NP, E]
        with nc.Block() as block:
            @block.sync
            def _(sp):
                sp.dma_start(w[:, :, :], I[p + "_w"]).then_inc(loaded, 16)
                sp.dma_start(order[:, :], I[f"order{E}"]).then_inc(loaded, 16)
                if layer == 2:
                    sp.dma_start(rb[:, :], I[p + "_b"]).then_inc(loaded, 16)
                sp.wait_ge(kept, 2)
                sp.dma_start(comb_dram, combT[:, :]).then_inc(stored, 16)
                sp.wait_ge(stored, 16)

            @block.tensor
            def _(pe):
                pe.wait_ge(loaded, LOADS)
                for j in range(NP):
                    for c in range(2):
                        mm = pe.matmul(l_ps[0:PT, j * E:(j + 1) * E], lhsT=hT[:, c, j * PT:(j + 1) * PT], rhs=w[:, c, :],
                                       start=(c == 0), stop=(c == 1))
                mm.then_inc(logits, 1)
                pe.wait_ge(combined, 1)
                for half in range(2):
                    for q in range(NP // 2):
                        mm = pe.transpose(t_ps[0:E, half, q * PT:(q + 1) * PT], comb[:, half * (NP // 2) + q, :], ident[0:PT, 0:PT])
                    mm.then_inc(turned, 1)

            @block.scalar
            def _(act):
                act.wait_ge(for_exp, 1)
                if layer == 2:
                    act.activation(at[:, :], at[:, :], ACT.Exp).then_inc(exped, 1)
                else:
                    act.activation(score[:, :, :], score[:, :, :], ACT.Exp).then_inc(exped, 1)
                for half in range(2):
                    act.wait_ge(turned, half + 1)
                    act.activation(combT[:, half * HALF:(half + 1) * HALF], t_ps[0:E, half, 0:HALF], ACT.Copy).then_inc(kept, 1)

            @block.vector
            def _(dve):
                count = [0]

                def chain(ins):
                    count[0] += 1
                    ins.then_inc(step, 1)
                    dve.wait_ge(step, count[0])

                def over(t):
                    return t[:, :].unsqueeze(2).to_broadcast(wide)

                dve.wait_ge(loaded, LOADS)
                dve.wait_ge(logits, 1)
                l3 = l_ps[0:PT, 0:NP * E].rearrange("p (j e) -> p j e", e=E)
                if layer == 2:
                    chain(dve.tensor_tensor(score[:, :, :], l3, rb[:, :].unsqueeze(1).to_broadcast(wide), ALU.add))
                else:
                    chain(dve.tensor_reduce(total[:, :], l3, AX.X, ALU.max))
                    dve.tensor_tensor(score[:, :, :], l3, over(total), ALU.subtract).then_inc(for_exp, 1)
                    dve.wait_ge(exped, 1)
                    chain(dve.tensor_reduce(total[:, :], score[:, :, :], AX.X, ALU.add))
                    chain(dve.reciprocal(total[:, :], total[:, :]))
                    chain(dve.tensor_tensor(score[:, :, :], score[:, :, :], over(total), ALU.mult))
                for r in range(2):
                    src = score if r == 0 else rest
                    chain(dve.tensor_reduce(best[r][:, :], src[:, :, :], AX.X, ALU.max))
                    chain(dve.tensor_tensor(place[:, :, :], src[:, :, :], over(best[r]), ALU.is_lt))
                    chain(dve.scalar_tensor_tensor(place[:, :, :], place[:, :, :], float(4 * E),
                                                   order[:, :].unsqueeze(1).to_broadcast(wide), ALU.mult, ALU.add))
                    chain(dve.tensor_reduce(at[:, :], place[:, :, :], AX.X, ALU.min))
                    chain(dve.tensor_tensor(hot[r][:, :, :], place[:, :, :], over(at), ALU.is_equal))
                    if r == 0:
                        chain(dve.scalar_tensor_tensor(rest[:, :, :], hot[0][:, :, :], NEG, score[:, :, :], ALU.mult, ALU.add))
                if layer == 1:
                    chain(dve.tensor_tensor(total[:, :], best[0][:, :], best[1][:, :], ALU.add))
                    chain(dve.tensor_scalar(total[:, :], total[:, :], 1e-9, None, ALU.max))
                    chain(dve.reciprocal(total[:, :], total[:, :]))
                    for r in range(2):
                        chain(dve.tensor_tensor(best[r][:, :], best[r][:, :], total[:, :], ALU.mult))
                if layer == 2:
                    chain(dve.tensor_tensor(total[:, :], best[1][:, :], best[0][:, :], ALU.subtract))
                    dve.tensor_copy(at[:, :], total[:, :]).then_inc(for_exp, 1)
                    dve.wait_ge(exped, 1)
                    chain(dve.tensor_scalar(total[:, :], at[:, :], 1.0, None, ALU.add))
                    chain(dve.reciprocal(best[0][:, :], total[:, :]))
                    chain(dve.tensor_tensor(best[1][:, :], best[0][:, :], at[:, :], ALU.mult))
                for r in range(2):
                    chain(dve.tensor_tensor(hot[r][:, :, :], hot[r][:, :, :], over(best[r]), ALU.mult))
                dve.tensor_tensor(comb[:, :, :], hot[0][:, :, :], hot[1][:, :, :], ALU.add).then_inc(combined, 1)


def capacity(nc, I, comb, comb_dram, rows, const):
    E = FFN[1][1]
    PER = 3 * NP - 1
    with ExitStack() as ctx:
        sb, ps, sem = alloc(nc, ctx)
        before = sb("cap_before", [PT, 2, NP, N], BF16)
        tied = sb("cap_tied", [PT, 2, NP, PT], BF16)
        later = sb("cap_later", [PT, PT])
        ones = sb("cap_ones", [PT, 128], BF16)
        rank = ps("cap_rank", [128, 4, BANK])
        const_loaded = sem("cap_const_loaded")
        ones_ready = sem("cap_ones_ready")
        loaded = [sem(f"cap_row_loaded{k}") for k in range(2)]
        compared = sem("cap_compared")
        ranked = sem("cap_ranked")
        masked = sem("cap_masked")

        with nc.Block() as block:
            @block.sync
            def _(sp):
                sp.dma_start(later[:, :], I["later"]).then_inc(const_loaded, 16)

                def body(i, again):
                    for k in range(2):
                        if again:
                            sp.wait_ge(loaded[k], 16 * i)
                        src = bass.AP(comb_dram.tensor, (2 * i + k) * N, [[0, 128], [1, N]])
                        sp.dma_start(rows[:, bass.ds(1 + 2 * i + k, 1), :].rearrange("p a n -> p (a n)"),
                                     src).then_inc(loaded[k], 16)
                body(0, False)
                with sp.Fori(1, E // 2) as i:
                    body(i, True)

            @block.gpsimd
            def _(pool):
                pool.memset(ones[:, :], 1.0).then_inc(ones_ready, 1)
                pool.memset(rows[:, 0:1, :], 1.0).then_inc(ones_ready, 1)

            @block.vector
            def _(dve):
                dve.wait_ge(const_loaded, 16)

                def mask(e, k):
                    row = rows[:, bass.ds(1 + e, 1), :].rearrange("p a n -> p (a n)")
                    dve.wait_ge(ranked, e + 1)
                    for half in range(2):
                        cols = slice(half * HALF, (half + 1) * HALF)
                        dve.scalar_tensor_tensor(row[:, cols], rank[:, 2 * k + half, 0:HALF], float(CAPACITY),
                                                 row[:, cols], ALU.is_lt, ALU.mult).then_inc(masked, 1)

                def body(i, again):
                    for k in range(2):
                        e = 2 * i + k
                        row = rows[0:PT, bass.ds(1 + e, 1), :].rearrange("p a n -> p (a n)")
                        dve.wait_ge(loaded[k], 16 * i + 16)
                        if again:
                            dve.wait_ge(ranked, e - 1)
                        for j in range(NP):
                            own = comb[:, j, bass.ds(e, 1)]
                            end = (j + 1) * PT
                            dve.tensor_scalar(before[:, k, j, 0:end], row[:, 0:end], own, None, ALU.is_lt).then_inc(compared, 1)
                            if end < N:
                                dve.tensor_scalar(before[:, k, j, end:N], row[:, end:N], own, None, ALU.is_le).then_inc(compared, 1)
                            dve.scalar_tensor_tensor(tied[:, k, j, :], row[:, end - PT:end], own, later[:, :],
                                                     ALU.is_equal, ALU.mult).then_inc(compared, 1)
                        if again or k == 1:
                            mask(2 * i + k - 1, 1 - k)
                body(0, False)
                with dve.Fori(1, E // 2) as i:
                    body(i, True)
                mask(E - 1, 1)

            @block.tensor
            def _(pe):
                pe.wait_ge(ones_ready, 1)

                def body(i, again):
                    for k in range(2):
                        e = 2 * i + k
                        if again:
                            pe.wait_ge(masked, 2 * (e - 1))
                        for half in range(2):
                            for j in range(NP):
                                if half == 0:
                                    pe.wait_ge(compared, PER * e + min(3 * j + 3, PER))
                                pe.matmul(rank[:, 2 * k + half, 0:HALF], lhsT=ones[:, :],
                                          rhs=before[:, k, j, half * HALF:(half + 1) * HALF],
                                          start=(j == 0), stop=False, skip_group_check=True)
                            for q in range(NP // 2):
                                mm = pe.matmul(rank[:, 2 * k + half, q * PT:(q + 1) * PT], lhsT=ones[:, :],
                                               rhs=tied[:, k, half * (NP // 2) + q, :],
                                               start=False, stop=True, skip_group_check=True)
                        mm.then_inc(ranked, 1)
                body(0, False)
                with pe.Fori(1, E // 2) as i:
                    body(i, True)


def experts(nc, I, layer, h, split, weights_dram, const, rows=None):
    shared, E, upe, M, per_body = FFN[layer]
    p = f"ffn{layer}"
    ring = upe * per_body
    units = shared + E * upe
    bodies = units // ring
    plain = shared // upe
    S = 2 * ring
    rest = D - 128
    WG, WR, WD = 0, 2 * M, 4 * M
    WEND = WD + D
    ALPHA, LIMIT = 1.702, 7.0
    GU = SPLIT * SPLIT
    clamped = layer == 2
    ident = const["ident"]
    with ExitStack() as ctx:
        sb, ps, sem = alloc(nc, ctx)
        w = sb(p + "_w", [128, ring, WEND])
        w_high = sb(p + "_w_high", [128, ring, WEND], F16)
        w_low = sb(p + "_w_low", [128, ring, WEND], F16)
        given = rows is not None
        if not given:
            rows = sb(p + "_rows", [128, plain + E, N])
        silu = sb(p + "_silu", [M, 2, HALF])
        up = sb(p + "_up", [M, 2, HALF])
        inner = sb(p + "_inner", [M, 4, HALF])
        high = sb(p + "_inner_high", [M, 4, HALF], F16)
        low = sb(p + "_inner_low", [M, 4, HALF], F16)
        yT = sb(p + "_yT", [C, 2, N])
        gu_ps = ps(p + "_gu_ps", [128, 4, BANK])
        y_ps = ps(p + "_y_ps", [128, 4, BANK])
        loaded = [sem(f"{p}_unit_loaded{k}") for k in range(ring)]
        rows_loaded = sem(p + "_rows_loaded")
        rows_set = sem(p + "_rows_set")
        w_high_ready = sem(p + "_w_high_ready")
        w_low_ready = sem(p + "_w_low_ready")
        gu = sem(p + "_gate_up_ready")
        taken = sem(p + "_gate_up_taken")
        silued = sem(p + "_silu_ready")
        product = sem(p + "_product_ready")
        ready = sem(p + "_inner_ready")
        high_ready = sem(p + "_inner_high_ready")
        low_ready = sem(p + "_inner_low_ready")
        downed = sem(p + "_down_done")
        kept = sem(p + "_yT_kept")
        turned = sem(p + "_y_ready")
        added = sem(p + "_added")
        if clamped:
            gate = sb(p + "_gate", [M, 2, HALF])
            ubias = sb(p + "_ubias", [M, E * upe, 2])
            dbias = sb(p + "_dbias", [E, D])
            combT = sb(p + "_combT", [E, N])
            small = sem(p + "_small_loaded")
            scaled = sem(p + "_biases_scaled")
            gated = sem(p + "_gate_clamped")
            upped = sem(p + "_up_clamped")
        with nc.Block() as block:
            @block.sync
            def _(sp):
                def load(i, k):
                    sp.dma_start(w[:, k, :], I[p + "_w"][bass.ds(i * ring + k, 1), :, :].rearrange("a p m -> p (a m)")
                                 ).then_inc(loaded[k], 16)
                load(0, 0)
                load(0, 1)
                if clamped:
                    sp.dma_start(ubias[:, :, :], I[p + "_ubias"]).then_inc(small, 16)
                    sp.dma_start(dbias[:, :], I[p + "_dbias"]).then_inc(small, 16)
                    sp.dma_start(combT[:, :], weights_dram).then_inc(small, 16)
                    sp.dma_start(rows[:, plain:, :].rearrange("p e n -> p (e n)"),
                                 bass.AP(weights_dram.tensor, 0, [[0, 128], [1, E * N]])).then_inc(rows_loaded, 16)
                for k in range(2, ring):
                    load(0, k)
                if not clamped and not given:
                    sp.dma_start(rows[:, plain:, :].rearrange("p e n -> p (e n)"),
                                 bass.AP(weights_dram.tensor, 0, [[0, 128], [1, E * N]])).then_inc(rows_loaded, 16)
                with sp.Fori(1, bodies) as i:
                    for k in range(ring):
                        sp.wait_ge(w_low_ready, (i - 1) * ring + k + 1)
                        load(i, k)

            @block.gpsimd
            def _(pool):
                if plain and not given:
                    pool.memset(rows[:, 0:plain, :], 1.0).then_inc(rows_set, 1)
                if clamped:
                    pool.wait_ge(small, 48)
                    pool.tensor_scalar(ubias[:, :, :], ubias[:, :, :], GU, None, ALU.mult).then_inc(scaled, 1)
                    pool.tensor_scalar(dbias[:, :], dbias[:, :], SPLIT, None, ALU.mult).then_inc(scaled, 1)
                with pool.Fori(0, bodies) as i:
                    for n in range(S):
                        pool.wait_ge(high_ready, i * S + n + 1)
                        pool.tensor_tensor(low[:, n % 4, :], inner[:, n % 4, :], high[:, n % 4, :],
                                           ALU.subtract).then_inc(low_ready, 1)

            @block.tensor
            def _(pe):
                def gate_up(i, n):
                    k, half = n // 2, n % 2
                    cols = slice(half * HALF, (half + 1) * HALF)
                    for m in range(2):
                        out = gu_ps[0:M, 2 * half + m, 0:HALF]
                        first, second = slice(WG + m * M, WG + (m + 1) * M), slice(WR + m * M, WR + (m + 1) * M)
                        pe.matmul(out, lhsT=w_high[:, k, first], rhs=split[0][:, cols], start=True, stop=False)
                        pe.matmul(out, lhsT=w_high[:, k, first], rhs=split[2][:, cols], start=False, stop=False)
                        pe.matmul(out, lhsT=w_low[:, k, first], rhs=split[0][:, cols], start=False, stop=False)
                        pe.matmul(out, lhsT=w_high[:, k, second], rhs=split[1][:, cols], start=False, stop=False)
                        mm = pe.matmul(out, lhsT=w_low[0:rest, k, second], rhs=split[1][0:rest, cols], start=False, stop=True)
                    mm.then_inc(gu, 1)

                def down(i, n, start=False, stop=False):
                    k, half = n // 2, n % 2
                    pe.wait_ge(low_ready, i * S + n + 1)
                    for c in range(2):
                        out = y_ps[0:C, 2 * half + c, 0:HALF]
                        cols = slice(WD + c * C, WD + (c + 1) * C)
                        pe.matmul(out, lhsT=w_high[0:M, k, cols], rhs=high[:, n % 4, :], start=start, stop=False, skip_group_check=True)
                        pe.matmul(out, lhsT=w_high[0:M, k, cols], rhs=low[:, n % 4, :], start=False, stop=False, skip_group_check=True)
                        mm = pe.matmul(out, lhsT=w_low[0:M, k, cols], rhs=high[:, n % 4, :], start=False, stop=stop, skip_group_check=True)
                    mm.then_inc(downed, 1)

                def body(i, again):
                    for n in range(S):
                        if n % 2 == 0:
                            pe.wait_ge(w_low_ready, i * ring + n // 2 + 1)
                        if again or n >= 2:
                            pe.wait_ge(taken, i * S + n - 1)
                        gate_up(i, n)
                        if n >= 2:
                            down(i, n - 2, start=not again and not clamped and n < 4)
                        elif again:
                            down(i - 1, S + n - 2)
                if clamped:
                    pe.wait_ge(scaled, 2)
                    for half in range(2):
                        for c in range(2):
                            pe.matmul(y_ps[0:C, 2 * half + c, 0:HALF], lhsT=dbias[:, c * C:(c + 1) * C],
                                      rhs=combT[:, half * HALF:(half + 1) * HALF], start=True, stop=False,
                                      skip_group_check=True)
                body(0, False)
                with pe.Fori(1, bodies) as i:
                    body(i, True)
                for n in (S - 2, S - 1):
                    down(bodies - 1, n, stop=True)
                for j in range(NP):
                    if j % 4 == 0:
                        pe.wait_ge(kept, 2 * (j // 4) + 2)
                    for c in range(2):
                        mm = pe.transpose(gu_ps[0:PT, j // 2, (j % 2) * D + c * C:(j % 2) * D + (c + 1) * C],
                                          yT[:, c, j * PT:(j + 1) * PT], ident[0:C, 0:C])
                    mm.then_inc(turned, 1)

            @block.scalar
            def _(act):
                def split_unit(i, k, again):
                    act.wait_ge(loaded[k], 16 * i + 16)
                    if again:
                        act.wait_ge(downed, (i - 1) * S + 2 * k + 2)
                    act.activation(w_high[:, k, :], w[:, k, :], ACT.Copy, scale=SPLIT).then_inc(w_high_ready, 1)

                def keep_high(i, n, again):
                    act.wait_ge(ready, i * S + n + 1)
                    if again or n >= 4:
                        act.wait_ge(downed, i * S + n - 3)
                    act.activation(high[:, n % 4, :], inner[:, n % 4, :], ACT.Copy).then_inc(high_ready, 1)

                def body(i, again, more):
                    for n in range(S):
                        k, half = n // 2, n % 2
                        s = i * S + n
                        if clamped:
                            act.wait_ge(gated, s + 1)
                            act.activation(silu[:, half, :], gate[:, half, :], ACT.Silu, scale=ALPHA / GU).then_inc(silued, 1)
                        else:
                            act.wait_ge(gu, s + 1)
                            act.activation(silu[:, half, :], gu_ps[0:M, 2 * half, 0:HALF], ACT.Silu,
                                           scale=1.0 / GU).then_inc(silued, 1)
                        if n:
                            keep_high(i, n - 1, again)
                        elif again:
                            keep_high(i - 1, S - 1, True)
                        if half == 0:
                            if k + 2 < ring:
                                split_unit(i, k + 2, again)
                            elif more:
                                split_unit(i + 1, k + 2 - ring, True)
                for k in range(2):
                    split_unit(0, k, False)
                body(0, False, True)
                with act.Fori(1, bodies - 1) as i:
                    body(i, True, True)
                body(bodies - 1, True, False)
                keep_high(bodies - 1, S - 1, True)
                act.wait_ge(downed, bodies * S)
                for half in range(2):
                    for c in range(2):
                        act.activation(yT[:, c, half * HALF:(half + 1) * HALF], y_ps[0:C, 2 * half + c, 0:HALF],
                                       ACT.Copy, scale=1.0 / SPLIT).then_inc(kept, 1)

            @block.vector
            def _(dve):
                def split_unit(i, k, again):
                    dve.wait_ge(w_high_ready, i * ring + k + 1)
                    dve.scalar_tensor_tensor(w_low[:, k, :], w[:, k, :], SPLIT, w_high[:, k, :],
                                             ALU.mult, ALU.subtract).then_inc(w_low_ready, 1)

                def body(i, again, more):
                    for n in range(S):
                        k, half = n // 2, n % 2
                        s = i * S + n
                        cols = slice(half * HALF, (half + 1) * HALF)
                        row = rows[0:M, bass.ds(i * per_body + k // upe, 1), cols].rearrange("p a n -> p (a n)")
                        dve.wait_ge(gu, s + 1)
                        if clamped:
                            u = bass.ds(i * ring + k, 1)
                            if again or n >= 2:
                                dve.wait_ge(silued, s - 1)
                            dve.tensor_scalar(gate[:, half, :], gu_ps[0:M, 2 * half, 0:HALF], ubias[:, u, 0], LIMIT * GU,
                                              ALU.add, ALU.min).then_inc(gated, 1)
                            dve.tensor_scalar(up[:, half, :], gu_ps[0:M, 2 * half + 1, 0:HALF], ubias[:, u, 1], LIMIT * GU,
                                              ALU.add, ALU.min).then_inc(taken, 1)
                            dve.wait_ge(taken, s + 1)
                            dve.tensor_scalar(up[:, half, :], up[:, half, :], -LIMIT * GU, GU, ALU.max, ALU.add).then_inc(upped, 1)
                            dve.wait_ge(silued, s + 1)
                            dve.wait_ge(upped, s + 1)
                            dve.scalar_tensor_tensor(up[:, half, :], silu[:, half, :], 1.0 / (ALPHA * GU), up[:, half, :],
                                                     ALU.mult, ALU.mult).then_inc(product, 1)
                            dve.wait_ge(product, s + 1)
                        else:
                            dve.wait_ge(silued, s + 1)
                            dve.scalar_tensor_tensor(up[:, half, :], gu_ps[0:M, 2 * half + 1, 0:HALF], 1.0 / GU, silu[:, half, :],
                                                     ALU.mult, ALU.mult).then_inc(taken, 1)
                            dve.wait_ge(taken, s + 1)
                        if again or n >= 4:
                            dve.wait_ge(low_ready, s - 3)
                        dve.tensor_tensor(inner[:, n % 4, :], up[:, half, :], row, ALU.mult).then_inc(ready, 1)
                        if half == 0:
                            if k + 2 < ring:
                                split_unit(i, k + 2, again)
                            elif more:
                                split_unit(i + 1, k + 2 - ring, True)
                for k in range(2):
                    split_unit(0, k, False)
                if plain and not given:
                    dve.wait_ge(rows_set, 1)
                elif not plain:
                    dve.wait_ge(rows_loaded, 16)
                if clamped:
                    dve.wait_ge(scaled, 2)
                body(0, False, True)
                if not given:
                    dve.wait_ge(rows_loaded, 16)
                with dve.Fori(1, bodies - 1) as i:
                    body(i, True, True)
                body(bodies - 1, True, False)
                for q in range(NP // 2):
                    dve.wait_ge(turned, 2 * q + 2)
                    dve.tensor_tensor(h[:, 2 * q:2 * q + 2, :], h[:, 2 * q:2 * q + 2, :],
                                      gu_ps[0:PT, q, 0:2 * D].rearrange("p (a d) -> p a d", a=2), ALU.add).then_inc(added, 1)


def ternary_attention(nc, I, h, hT, const):
    identb = const["identb"]
    with ExitStack() as ctx:
        sb, ps, sem = alloc(nc, ctx)
        W3 = 3 * D
        qT = sb("ta_qT", [C, 2, N], BF16)
        kT = sb("ta_kT", [C, 2, N], BF16)
        tern = sb("ta_tern", [PT, NP, W3], BF16)
        means = sb("ta_means", [128, 3])
        limit = sb("ta_limit", [128, 1])
        out_scale = sb("ta_out_scale", [128, 1])
        ones = const["ones"]

        with ExitStack() as pre:
            psb, pps, psem = alloc(nc, pre)
            w = psb("ta_w", [C, 2, W3])
            wt = psb("ta_wt", [C, 2, W3])
            below = psb("ta_w_below", [C, 2, W3])
            wsum = psb("ta_wsum", [C, 1])
            ws = psb("ta_ws", [128, 1])
            wlim = psb("ta_wlim", [128, 2])
            qkv = psb("ta_qkv", [PT, NP, W3])
            lower = psb("ta_lower", [PT, NP, D], BF16)
            norm1 = psb("ta_norm1", [PT, NP, 3 * H])
            sums = psb("ta_sums", [PT, NP, 3])
            lims = psb("ta_lims", [128, 2, 3])
            acc = pps("ta_acc", [128, 4, BANK])
            stat = pps("ta_stat", [128, BANK])
            trans = pps("ta_trans", [128, 2, 2 * BANK], BF16)
            loaded = psem("ta_loaded")
            step = psem("ta_weight_step")
            wsummed = psem("ta_weight_sum_ready")
            projected = psem("ta_projected")
            copied = psem("ta_projection_copied")
            normed = psem("ta_norm_step")
            summed = psem("ta_sums_ready")
            mstep = psem("ta_mean_step")
            tready = psem("ta_ternary_ready")
            turned = psem("ta_transposed")
            tcopied = psem("ta_transposed_copied")
            with nc.Block() as block:
                @block.sync
                def _(sp):
                    sp.dma_start(w[:, :, :], I["ta_w"]).then_inc(loaded, 16)

                @block.tensor
                def _(pe):
                    pe.wait_ge(step, 1)
                    pe.matmul(stat[:, 0:1], lhsT=ones[0:C, :], rhs=wsum[:, :], start=True, stop=True).then_inc(wsummed, 1)
                    pe.wait_ge(step, 5)
                    for j in range(NP):
                        if j >= 2:
                            pe.wait_ge(copied, 2 * (j - 1))
                        for part in range(2):
                            for c in range(2):
                                mm = pe.matmul(acc[0:PT, 2 * (j % 2) + part, 0:W3 // 2], lhsT=hT[:, c, j * PT:(j + 1) * PT],
                                               rhs=wt[:, c, part * (W3 // 2):(part + 1) * (W3 // 2)],
                                               start=(c == 0), stop=(c == 1))
                            mm.then_inc(projected, 1)
                    pe.wait_ge(summed, NP)
                    pe.matmul(stat[:, 0:3 * NP], lhsT=ones[0:PT, :], rhs=sums[:, :, :].rearrange("p j a -> p (j a)"),
                              start=True, stop=True).then_inc(wsummed, 1)
                    for a in range(2):
                        pe.wait_ge(tready, a + 1)
                        for c in range(2):
                            if a:
                                pe.wait_ge(tcopied, c + 1)
                            for j in range(NP):
                                mm = pe.transpose(trans[0:C, c, j * PT:(j + 1) * PT],
                                                  tern[:, j, a * D + c * C:a * D + (c + 1) * C], identb[0:PT, 0:PT])
                            mm.then_inc(turned, 1)

                @block.scalar
                def _(act):
                    act.wait_ge(step, 5)
                    for j in range(NP):
                        for part in range(2):
                            act.wait_ge(projected, 2 * j + part + 1)
                            act.activation(qkv[:, j, part * (W3 // 2):(part + 1) * (W3 // 2)],
                                           acc[0:PT, 2 * (j % 2) + part, 0:W3 // 2], ACT.Copy,
                                           scale=ws[0:PT, 0:1]).then_inc(copied, 1)
                    for a in range(2):
                        for c in range(2):
                            act.wait_ge(turned, 2 * a + c + 1)
                            act.activation((qT, kT)[a][:, c, :], trans[0:C, c, 0:N], ACT.Copy).then_inc(tcopied, 1)

                @block.vector
                def _(dve):
                    flat = lambda t: t[:, :, :].rearrange("p c n -> p (c n)")
                    dve.wait_ge(loaded, 16)
                    dve.tensor_reduce(wsum[:, :], flat(w), AX.X, ALU.add, apply_absolute_value=True).then_inc(step, 1)
                    dve.wait_ge(wsummed, 1)
                    dve.tensor_scalar(ws[:, :], stat[:, 0:1], 1.0 / (D * W3), TERNARY_EPS, ALU.mult, ALU.add).then_inc(step, 1)
                    dve.wait_ge(step, 2)
                    dve.tensor_scalar(wlim[:, 0:1], ws[:, :], 0.5, None, ALU.mult)
                    dve.tensor_scalar(wlim[:, 1:2], ws[:, :], -0.5, None, ALU.mult).then_inc(step, 1)
                    dve.wait_ge(step, 3)
                    dve.tensor_scalar(flat(below), flat(w), wlim[0:C, 1:2], None, ALU.is_lt).then_inc(step, 1)
                    dve.wait_ge(step, 4)
                    dve.scalar_tensor_tensor(flat(wt), flat(w), wlim[0:C, 0:1], flat(below), ALU.is_gt, ALU.subtract).then_inc(step, 1)
                    for j in range(NP):
                        dve.wait_ge(copied, 2 * j + 2)
                        heads = qkv[:, j, :].rearrange("p (h d) -> p h d", d=HD)
                        dve.tensor_reduce(norm1[:, j, :], heads, AX.X, ALU.add, apply_absolute_value=True).then_inc(normed, 1)
                        dve.wait_ge(normed, 4 * j + 1)
                        dve.tensor_scalar(norm1[:, j, :], norm1[:, j, :], TERNARY_EPS, None, ALU.add).then_inc(normed, 1)
                        dve.wait_ge(normed, 4 * j + 2)
                        dve.reciprocal(norm1[:, j, :], norm1[:, j, :]).then_inc(normed, 1)
                        dve.wait_ge(normed, 4 * j + 3)
                        dve.tensor_tensor(heads, heads, norm1[:, j, :].unsqueeze(2).to_broadcast([PT, 3 * H, HD]),
                                          ALU.mult).then_inc(normed, 1)
                        dve.wait_ge(normed, 4 * j + 4)
                        dve.tensor_reduce(sums[:, j, :], qkv[:, j, :].rearrange("p (a d) -> p a d", a=3), AX.X, ALU.add,
                                          apply_absolute_value=True).then_inc(summed, 1)
                    dve.wait_ge(wsummed, 2)
                    dve.tensor_reduce(means[:, :], stat[:, 0:3 * NP].rearrange("p (j a) -> p a j", a=3), AX.X,
                                      ALU.add).then_inc(mstep, 1)
                    dve.wait_ge(mstep, 1)
                    dve.tensor_scalar(means[:, :], means[:, :], 1.0 / (N * D), TERNARY_EPS, ALU.mult, ALU.add).then_inc(mstep, 1)
                    dve.wait_ge(mstep, 2)
                    dve.tensor_scalar(lims[:, 0, :], means[:, :], 0.5, None, ALU.mult).then_inc(mstep, 1)
                    dve.tensor_scalar(lims[:, 1, :], means[:, :], -0.5, None, ALU.mult).then_inc(mstep, 1)
                    dve.wait_ge(mstep, 4)
                    for a in range(3):
                        part = qkv[:, :, a * D:(a + 1) * D]
                        if a:
                            dve.wait_ge(tready, a)
                        dve.tensor_scalar(lower[:, :, :], part, lims[0:PT, 1, a:a + 1], None, ALU.is_lt).then_inc(mstep, 1)
                        dve.wait_ge(mstep, 5 + a)
                        dve.scalar_tensor_tensor(tern[:, :, a * D:(a + 1) * D], part, lims[0:PT, 0, a:a + 1],
                                                 lower[:, :, :], ALU.is_gt, ALU.subtract).then_inc(tready, 1)

        with ExitStack() as main:
            msb, mps, msem = alloc(nc, main)
            q_stage = msb("ta_q_stage", [C, 2, 2, PT], BF16)
            k_blocks = msb("ta_k_blocks", [C, 2, 2, 2, HC, T], BF16)
            dots = msb("ta_dots", [SR, NP, H * T], BF16)
            dsum = msb("ta_dsum", [SR, NP])
            dtot = msb("ta_dtot", [SR, 1])
            mean = msb("ta_mean", [128, 1])
            unit = msb("ta_unit", [128, 1])
            score_s = msb("ta_score_s", [128, 1])
            nlimit = msb("ta_nlimit", [128, 1])
            inv = msb("ta_inv", [128, 1])
            lower = msb("ta_dots_lower", [SR, 2, H * T], BF16)
            probs = msb("ta_probs", [SR, 2, H * T], BF16)
            probsT = msb("ta_probsT", [GK, 2, G, SR], BF16)
            v_blocks = msb("ta_v_blocks", [GK, 2, 2, D], BF16)
            oT = msb("ta_oT", [GD, 2, G, PT], BF16)
            s_ps = mps("ta_s", [128, 2, BANK])
            staged = msem("ta_staged")
            cleared = msem("ta_banks_cleared")
            scores = msem("ta_scores_ready")
            dotted = msem("ta_dots_kept")
            sstep = msem("ta_scalar_step")
            total = msem("ta_total_ready")
            with nc.Block() as block:
                @block.gpsimd
                def _(pool):
                    def body(i, later):
                        for k in range(2):
                            j = 2 * i + k
                            if later:
                                pool.wait_ge(scores, j - 1)
                            pool.tensor_copy(q_stage[:, k, :, :], qT[:, :, bass.ds(j * PT, PT)]).then_inc(staged, 1)
                            for c in range(2):
                                pool.tensor_tensor(k_blocks[:, k, c, :, :, :],
                                                   kT[:, c, bass.ds(j * PT, PT)].rearrange("p (b t) -> p b t", b=2)
                                                   .unsqueeze(2).to_broadcast([C, 2, HC, T]),
                                                   const["own_head"][:, :].unsqueeze(1).unsqueeze(3)
                                                   .to_broadcast([C, 2, HC, T]), ALU.mult).then_inc(staged, 1)
                    body(0, False)
                    with pool.Fori(1, NP // 2) as i:
                        body(i, True)

                @block.tensor
                def _(pe):
                    pe.wait_ge(cleared, 1)

                    def body(i, later):
                        for k in range(2):
                            j = 2 * i + k
                            pe.wait_ge(staged, 3 * j + 3)
                            if later:
                                pe.wait_ge(dotted, j - 1)
                            for c in range(2):
                                for img in range(2):
                                    mm = pe.matmul(s_ps[img * SECOND:img * SECOND + T, k, c * HC * T:(c + 1) * HC * T],
                                                   lhsT=q_stage[:, k, c, img * T:(img + 1) * T],
                                                   rhs=k_blocks[:, k, c, img, :, :].rearrange("p a t -> p (a t)"),
                                                   start=True, stop=True)
                            mm.then_inc(scores, 1)
                    body(0, False)
                    with pe.Fori(1, NP // 2) as i:
                        body(i, True)
                    pe.wait_ge(sstep, 1)
                    pe.matmul(s_ps[:, 0, 0:1], lhsT=ones[0:SR, :], rhs=dtot[:, :], start=True, stop=True).then_inc(total, 1)

                @block.vector
                def _(dve):
                    dve.memset(s_ps[:, :, :], 0.0).then_inc(cleared, 1)

                    def body(i):
                        for k in range(2):
                            j = 2 * i + k
                            dve.wait_ge(scores, j + 1)
                            dve.tensor_reduce(dsum[:, bass.ds(j, 1)], s_ps[0:SR, k, 0:H * T], AX.X, ALU.add,
                                              apply_absolute_value=True)
                            dve.tensor_copy(dots[:, bass.ds(j, 1), :].rearrange("p a n -> p (a n)"),
                                            s_ps[0:SR, k, 0:H * T]).then_inc(dotted, 1)
                    with dve.Fori(0, NP // 2) as i:
                        body(i)
                    dve.wait_ge(dotted, NP)
                    dve.tensor_reduce(dtot[:, :], dsum[:, :], AX.X, ALU.add).then_inc(sstep, 1)
                    dve.wait_ge(total, 1)
                    dve.tensor_scalar(mean[:, :], s_ps[:, 0, 0:1], 1.0 / (B * H * T * T), None, ALU.mult).then_inc(sstep, 1)
                    dve.scalar_tensor_tensor(unit[:, :], means[:, 0:1], SCALE, means[:, 1:2], ALU.mult, ALU.mult).then_inc(sstep, 1)
                    dve.wait_ge(sstep, 3)
                    dve.tensor_tensor(score_s[:, :], mean[:, :], unit[:, :], ALU.mult).then_inc(sstep, 1)
                    dve.wait_ge(sstep, 4)
                    dve.tensor_scalar(score_s[:, :], score_s[:, :], TERNARY_EPS, None, ALU.add).then_inc(sstep, 1)
                    dve.reciprocal(inv[:, :], unit[:, :]).then_inc(sstep, 1)
                    dve.wait_ge(sstep, 6)
                    dve.scalar_tensor_tensor(limit[:, :], score_s[:, :], 0.5, inv[:, :], ALU.mult, ALU.mult).then_inc(sstep, 1)
                    dve.tensor_tensor(out_scale[:, :], score_s[:, :], means[:, 2:3], ALU.mult).then_inc(sstep, 1)
                    dve.wait_ge(sstep, 8)
                    dve.tensor_scalar(nlimit[:, :], limit[:, :], -1.0, None, ALU.mult).then_inc(sstep, 1)

            t_ps = mps("ta_t", [128, 2, 2 * BANK], BF16)
            v_ps = mps("ta_v", [128, 2, BANK])
            oy_ps = mps("ta_oy", [128, 2, BANK])
            under = msem("ta_under")
            rounded = msem("ta_rounded")
            values = msem("ta_values_ready")
            v_ready = msem("ta_v_blocks_ready")
            turned_s = msem("ta_roundedT_ready")
            pT_copied = msem("ta_roundedT_copied")
            o_ready = msem("ta_outputs_ready")
            o_copied = msem("ta_outputs_copied")
            y_ready = msem("ta_token_major_ready")
            added = msem("ta_added")

            def y_of(k):
                return oy_ps[0:PT, k, G * PT:G * PT + D]

            with nc.Block() as block:
                @block.tensor
                def _(pe):
                    def value(i, k, later):
                        j = 2 * i + k
                        if later:
                            pe.wait_ge(v_ready, j - 1)
                        for img in range(2):
                            mm = pe.matmul(v_ps[0:GK, k, img * D:(img + 1) * D], lhsT=const["copy_keys"][:, img, :],
                                           rhs=tern[:, bass.ds(j, 1), 2 * D:3 * D].rearrange("p a d -> p (a d)"),
                                           start=True, stop=True)
                        mm.then_inc(values, 1)

                    def body(i, later, more):
                        for k in range(2):
                            t = 2 * i + k
                            pe.wait_ge(rounded, t + 1)
                            if later:
                                pe.wait_ge(pT_copied, t - 1)
                            for g in range(G):
                                mm = pe.transpose(t_ps[0:GK, k, g * 128:g * 128 + SR],
                                                  probs[:, k, g * GK:(g + 1) * GK], identb[0:SR, 0:SR])
                            mm.then_inc(turned_s, 1)
                            if more:
                                value(i + 1, k, True)
                            pe.wait_ge(pT_copied, t + 1)
                            pe.wait_ge(v_ready, t + 1)
                            if later:
                                pe.wait_ge(added, t - 1)
                            for img in range(2):
                                for g in range(G):
                                    mm = pe.matmul(oy_ps[0:GD, k, g * PT + img * T:g * PT + (img + 1) * T],
                                                   lhsT=v_blocks[:, k, img, g * GD:(g + 1) * GD],
                                                   rhs=probsT[:, k, g, img * SECOND:img * SECOND + T],
                                                   start=True, stop=True)
                            mm.then_inc(o_ready, 1)
                            pe.wait_ge(o_copied, t + 1)
                            for g in range(G):
                                mm = pe.matmul(y_of(k), lhsT=oT[:, k, g, :], rhs=const["place"][:, g, :],
                                               start=(g == 0), stop=(g == G - 1))
                            mm.then_inc(y_ready, 1)
                    for k in range(2):
                        value(0, k, False)
                    body(0, False, True)
                    with pe.Fori(1, NP // 2 - 1) as i:
                        body(i, True, True)
                    body(NP // 2 - 1, True, False)

                @block.scalar
                def _(act):
                    def body(i, later):
                        for k in range(2):
                            t = 2 * i + k
                            act.wait_ge(turned_s, t + 1)
                            if later:
                                act.wait_ge(o_ready, t - 1)
                            act.activation(probsT[:, k, :, :],
                                           t_ps[0:GK, k, 0:G * 128].rearrange("p (g s) -> p g s", g=G)[:, :, 0:SR],
                                           ACT.Copy).then_inc(pT_copied, 1)
                            act.wait_ge(o_ready, t + 1)
                            if later:
                                act.wait_ge(y_ready, t - 1)
                            act.activation(oT[:, k, :, :].rearrange("p g s -> p (g s)"), oy_ps[0:GD, k, 0:G * PT],
                                           ACT.Copy).then_inc(o_copied, 1)
                    body(0, False)
                    with act.Fori(1, NP // 2) as i:
                        body(i, True)

                @block.vector
                def _(dve):
                    def round_scores(n, k, later):
                        dn = dots[:, bass.ds(n, 1), :].rearrange("p a n -> p (a n)")
                        if later:
                            dve.wait_ge(rounded, n - 1)
                        dve.tensor_scalar(lower[:, k, :], dn, nlimit[0:SR, 0:1], None, ALU.is_lt).then_inc(under, 1)
                        dve.wait_ge(under, n + 1)
                        if later:
                            dve.wait_ge(turned_s, n - 1)
                        dve.scalar_tensor_tensor(probs[:, k, :], dn, limit[0:SR, 0:1], lower[:, k, :],
                                                 ALU.is_gt, ALU.subtract).then_inc(rounded, 1)

                    def value_blocks(n, k, later):
                        dve.wait_ge(values, n + 1)
                        if later:
                            dve.wait_ge(o_ready, n - 1)
                        dve.tensor_tensor(v_blocks[:, k, :, :],
                                          v_ps[0:GK, k, 0:2 * D].rearrange("p (b f) -> p b f", b=2),
                                          const["own_key"][:, :].unsqueeze(1).to_broadcast([GK, 2, D]),
                                          ALU.mult).then_inc(v_ready, 1)

                    def add(t, k):
                        dve.wait_ge(y_ready, t + 1)
                        hj = h[:, bass.ds(t, 1), :].rearrange("p a d -> p (a d)")
                        dve.scalar_tensor_tensor(hj, y_of(k), out_scale[0:PT, 0:1], hj,
                                                 ALU.mult, ALU.add).then_inc(added, 1)

                    def body(i, later, more):
                        for k in range(2):
                            t = 2 * i + k
                            if more or k == 0:
                                round_scores(t + 1, 1 - k, later or k == 1)
                                value_blocks(t + 1, 1 - k, later or k == 1)
                            if later or k == 1:
                                add(t - 1, 1 - k)
                    round_scores(0, 0, False)
                    value_blocks(0, 0, False)
                    body(0, False, True)
                    with dve.Fori(1, NP // 2 - 1) as i:
                        body(i, True, True)
                    body(NP // 2 - 1, True, False)
                    add(NP - 1, 1)


def tower(nc, I, out, last=8):
    SEMAPHORES.clear()
    with ExitStack() as ctx:
        sb, ps, sem = alloc(nc, ctx)
        h = sb("h", [PT, NP, D])
        hT = sb("hT", [C, 2, N])
        split = [sb(f"split{i}", [128, N], F16) for i in range(3)]
        const = {"ident": sb("ident", [128, 128]), "identb": sb("identb", [128, 128], BF16),
                 "ones": sb("ones", [128, 128]), "power": sb("power", [PT, 2, NP]),
                 "half": sb("half", [C, 2, SP]), "own_head": sb("own_head", [C, HC]),
                 "own_key": sb("own_key", [GK, D]), "copy_keys": sb("copy_keys", [PT, 2, GK], BF16),
                 "place": sb("place", [GD, G, D], BF16)}
        raw = {"copy_keys": sb("copy_keys_f", [PT, 2, GK]), "place": sb("place_f", [GD, G, D])}
        loaded = sem("const_loaded")
        made = sem("const_made")
        with nc.Block() as block:
            @block.sync
            def _(sp):
                for name, dst in (("ident", const["ident"]), ("own_head", const["own_head"]), ("own_key", const["own_key"]),
                                  ("copy_keys", raw["copy_keys"]), ("place", raw["place"])):
                    sp.dma_start(dst[tuple(slice(None) for _ in dst.shape)], I[name]).then_inc(loaded, 16)

            @block.gpsimd
            def _(pool):
                pool.memset(const["ones"][:, :], 1.0).then_inc(made, 1)
                pool.memset(const["power"][:, 0, :], -0.5).then_inc(made, 1)
                pool.memset(const["power"][:, 1, :], 0.5).then_inc(made, 1)
                pool.memset(const["half"][:, :, :], 0.5).then_inc(made, 1)
                pool.wait_ge(loaded, 16 * 5)
                pool.tensor_copy(const["identb"][:, :], const["ident"][:, :]).then_inc(made, 1)
                pool.tensor_copy(const["copy_keys"][:, :, :], raw["copy_keys"][:, :, :]).then_inc(made, 1)
                pool.tensor_copy(const["place"][:, :, :], raw["place"][:, :, :]).then_inc(made, 1)

        def store():
            stored = sem("h_stored")
            with nc.Block() as block:
                @block.sync
                def _(sp):
                    sp.dma_start(out.rearrange("(j p) d -> p j d", p=PT), h[:, :, :]).then_inc(stored, 16)
                    sp.wait_ge(stored, 16)

        patch_embedding(nc, I, h)
        if last == 0:
            return store()
        to_feature_major(nc, h, hT, const["ident"], "tr0")
        n = 0
        for layer in range(4):
            reset_semaphores(nc)
            if layer < 3:
                attention(nc, I, layer, h, hT, const)
            else:
                ternary_attention(nc, I, h, hT, const)
            n += 1
            if layer == 0:
                with nc.sbuf_tensor("unit", [PT, NP, D], F32) as unit:
                    layer_norm(nc, h, f"ln{n}", unit, const["power"])
                    if last == n:
                        return store()
                    to_feature_major(nc, unit, hT, const["ident"], f"tr{n}")
                    soft_mixture(nc, I, h, unit, hT, const)
            else:
                layer_norm(nc, h, f"ln{n}", None, const["power"])
                if last == n:
                    return store()
                to_feature_major(nc, h, hT, const["ident"], f"tr{n}", split)
                with ExitStack() as weighing:
                    wsb, _, _ = alloc(nc, weighing)
                    rows = wsb("cap_rows", [128, 1 + FFN[1][1], N]) if layer == 1 else None
                    with nc.sbuf_tensor(f"comb{layer}", [PT, NP, FFN[layer][1]], F32) as comb:
                        router(nc, I, layer, hT, comb, I[f"comb_scratch{layer}"], const)
                        if layer == 1:
                            capacity(nc, I, comb, I["comb_scratch1"], rows, const)
                    experts(nc, I, layer, h, split, I[f"comb_scratch{layer}"], const, rows)
            n += 1
            layer_norm(nc, h, f"ln{n}", None, const["power"])
            if last == n:
                return store()
            to_feature_major(nc, h, hT, const["ident"], f"tr{n}")


def shape_constants():
    f = lambda *s: np.zeros(s, np.float32)
    k = {}
    k["ident"] = np.eye(128, dtype=np.float32)
    own_head = f(C, HC)
    own_head[np.arange(C), np.arange(C) // HD] = 1
    k["own_head"] = own_head
    row, col = np.arange(GK)[:, None] // T, (np.arange(D)[None, :] // HD) % GH
    k["own_key"] = (row == col).astype(np.float32)
    rep = f(PT, 2, GK)
    for img in range(2):
        for a in range(GH):
            rep[img * T + np.arange(T), img, a * T + np.arange(T)] = 1
    k["copy_keys"] = rep
    place = f(GD, G, D)
    for g in range(G):
        place[np.arange(GD), g, g * GD + np.arange(GD)] = 1
    k["place"] = place
    causal = f(SR, H, T)
    for img in range(2):
        causal[img * SECOND:img * SECOND + T] = np.where(np.arange(T)[None, :] > np.arange(T)[:, None], NEG, 0)[:, None, :]
    k["causal"] = causal.reshape(SR, H * T)
    angle = (np.arange(T, dtype=np.float32)[None, :] *
             (1.0 / 10000.0 ** (2.0 * np.arange(HD // 2, dtype=np.float32) / HD)).astype(np.float32)[:, None])
    rope = f(C, 2, T)
    d = np.arange(C) % HD
    rope[:, 0] = np.cos(angle)[d // 2]
    rope[:, 1] = np.sin(angle)[d // 2] * np.where(d % 2, 1, -1)[:, None]
    k["rope"] = rope
    own = f(C, 2, SN, SP)
    for e in range(2):
        own[np.arange(C), e, e * 4 + np.arange(C) // SH] = 1
    k["sm_own_expert"] = own.reshape(C, 2, SLOTS)
    k["sm_own_image"] = (np.arange(PT)[:, None] // T == np.arange(2)).astype(np.float32)
    k["sm_own_image4"] = (2 * np.arange(2)[None, :, None] + (np.arange(PT) // T)[:, None, None] ==
                          np.arange(4)).astype(np.float32)
    for E in (8, 16):
        k[f"order{E}"] = np.tile(np.arange(E, dtype=np.float32), (PT, 1))
    k["later"] = (np.arange(PT)[None, :] > np.arange(PT)[:, None]).astype(np.float32)
    return k


def chunks(a, n=2):
    return a.reshape(n, a.shape[0] // n, a.shape[1]).transpose(1, 0, 2)


def swapped(a):
    return a.reshape(a.shape[:-1] + (-1, 2))[..., ::-1].reshape(a.shape)


def layouts(x):
    P = 16
    k = {}
    gh = 96 // P
    pt = x["x"].reshape(B, 3, gh, P, gh, P).transpose(0, 2, 4, 1, 3, 5).reshape(B, gh * gh, 3 * P * P)
    pt = np.concatenate([np.zeros((B, 1, 3 * P * P), np.float32), pt], 1).reshape(N, -1)
    k["patches"] = chunks(pt.T, 6)
    k["tok_w"] = chunks(x["L0_tok_W"].T, 6)
    k["tok_pos"] = np.tile(x["L0_tok_pos_emb"][0], (2, 1))
    first = np.concatenate([x["L0_tok_cls_tok"][0], np.broadcast_to(x["L0_tok_b"], (T - 1, D))], 0)
    k["tok_first"] = np.tile(first, (2, 1))

    def att(p, wq, wk, wv, wp, bq, bk, bv, bp, rope=False):
        k[p + "_wq"], k[p + "_wk"], k[p + "_wv"] = chunks(wq), chunks(wk), chunks(wv)
        bs = [bq, bk]
        if rope:
            k[p + "_wqs"], k[p + "_wks"] = chunks(swapped(wq)), chunks(swapped(wk))
            bs = [bq, swapped(bq), bk, swapped(bk)]
        k[p + "_bias"] = np.stack([b.reshape(2, C).T for b in bs], 2)
        k[p + "_wp"] = chunks(wp, G)
        k[p + "_bv"] = np.broadcast_to(bv.reshape(G, GD).T[:, :, None], (GD, G, PT))
        k[p + "_bp"] = np.tile(bp, (PT, 1))
    w, b = x["L0_attn_W_attn"], x["L0_attn_b_attn"]
    att("att0", w[:, :D], w[:, D:2 * D], w[:, 2 * D:], x["L0_attn_W_proj"], b[:D], b[D:2 * D], b[2 * D:], x["L0_attn_b_proj"])
    att("att1", x["L1_attn_Wq"].T, x["L1_attn_Wk"].T, x["L1_attn_Wv"].T, x["L1_attn_Wp"].T,
        x["L1_attn_bq"], x["L1_attn_bk"], x["L1_attn_bv"], x["L1_attn_bp"], rope=True)
    w, b = x["L2_attn_qkv_w"].T, x["L2_attn_qkv_b"]
    att("att2", w[:, :D], w[:, D:2 * D], w[:, 2 * D:], x["L2_attn_out_w"].T, b[:D], b[D:2 * D], b[2 * D:], x["L2_attn_out_b"])
    rel = x["L2_attn_rel_pos_emb"][np.clip(np.arange(SHIFTS) - (T - 1), -MAX_REL, MAX_REL) + MAX_REL]
    blocks = np.zeros((C, HC, SHIFTS), np.float32)
    for i in range(HC):
        blocks[i * HD:(i + 1) * HD, i] = rel.T
    k["rel_blocks"] = blocks.reshape(C, -1)
    k["ta_w"] = chunks(x["L3_attn_w_qkv"].T)

    k["sm_slots"] = chunks(x["L0_ffn_slot_params"].reshape(D, SLOTS))
    k["sm_scale"] = np.broadcast_to(x["L0_ffn_scale"].reshape(1, 1), (C, 1))
    k["sm_down"] = chunks(x["L0_ffn_W_down"].transpose(1, 0, 2).reshape(D, SN * SH))
    k["sm_bdown"] = x["L0_ffn_b_down"].reshape(2, C).T
    k["sm_up"] = chunks(x["L0_ffn_W_up"].reshape(SN * SH, D))
    k["sm_bup"] = np.tile(np.repeat(x["L0_ffn_b_up"], SP, 0), (4, 1))

    def units(gate, up, down, M):
        e, inner = gate.shape[0], gate.shape[2]
        n = inner // M
        gu = np.stack([gate.reshape(e, D, n, M), up.reshape(e, D, n, M)], 3).transpose(0, 2, 1, 3, 4).reshape(e * n, D, 2 * M)
        dn = np.zeros((e * n, 128, D), np.float32)
        dn[:, :M] = down.reshape(e * n, M, D)
        return np.concatenate([gu[:, :128], np.concatenate([gu[:, 128:]] * 2, 1), dn], 2)

    def ffn(layer, parts):
        k[f"ffn{layer}_w"] = np.concatenate([units(*q, FFN[layer][3]) for q in parts], 0)
    ffn(1, [(x["L1_ffn_s1"][None], x["L1_ffn_s3"][None], x["L1_ffn_s2"][None]),
            (x["L1_ffn_w1"], x["L1_ffn_w3"], x["L1_ffn_w2"])])
    gu = x["L2_ffn_Wgu"]
    I2 = gu.shape[2] // 2
    ffn(2, [(gu[:, :, :I2], gu[:, :, I2:], x["L2_ffn_Wd"])])
    k["ffn2_ubias"] = x["L2_ffn_bgu"].reshape(8, 2, 2, C).transpose(3, 0, 2, 1).reshape(C, 16, 2)
    k["ffn2_dbias"] = x["L2_ffn_bd"]
    t = lambda a: a.transpose(0, 2, 1)
    ffn(3, [(x["L3_ffn_sw1"].T[None], x["L3_ffn_sw3"].T[None], x["L3_ffn_sw2"].T[None]),
            (t(x["L3_ffn_w1"]), t(x["L3_ffn_w3"]), t(x["L3_ffn_w2"]))])
    k["rt1_w"], k["rt2_w"], k["rt3_w"] = chunks(x["L1_ffn_Wr"]), chunks(x["L2_ffn_Wr"]), chunks(x["L3_ffn_gate_w"].T)
    k["rt2_b"] = np.tile(x["L2_ffn_br"], (PT, 1))
    return k


LAST = 8


def kernel(**inputs):
    import concourse.bacc as _bacc
    from concourse.bass_utils import run_bass_kernel_spmd as _run
    nc = _bacc.Bacc("TRN2", target_bir_lowering=False, num_devices=1)
    arrays = {**layouts({n: np.asarray(a) for n, a in inputs.items()}), **shape_constants()}
    arrays = {f"in_{n}": np.ascontiguousarray(a) for n, a in arrays.items()}
    I = {n[3:]: nc.dram_tensor(n, a.shape, F32, kind="ExternalInput").ap() for n, a in arrays.items()}
    I["rel_scratch"] = nc.dram_tensor("rel_scratch", (N, H * SHIFTS), F32, kind="Internal").ap()
    for layer in (1, 2, 3):
        I[f"comb_scratch{layer}"] = nc.dram_tensor(f"comb_scratch{layer}", (FFN[layer][1], N), F32, kind="Internal").ap()
    out = nc.dram_tensor("out", (N, D), F32, kind="ExternalOutput").ap()
    tower(nc, I, out, LAST)
    got = _run(nc, [arrays], core_ids=[0]).results[0]["out"]
    return got.reshape(B, T, D)
```

```python
from contextlib import ExitStack

import numpy as np
import concourse.bass as bass
from concourse import mybir

F32 = mybir.dt.float32
BF16 = mybir.dt.bfloat16
F16 = mybir.dt.float16
ACT = mybir.ActivationFunctionType
ALU = mybir.AluOpType
AX = mybir.AxisListType

B, T, D, H = 16, 37, 192, 12
HD = D // H
N = B * T
NP, PT = B // 2, 2 * T
C = D // 2
HC = H // 2
HALF = N // 2
G, GH = 4, 3
GK, GD = GH * T, GH * HD
SECOND = 64
SR = SECOND + T
BANK = 512
SPLIT = 256.0
LN_EPS = 1e-5
L2_EPS = 1e-6
TERNARY_EPS = 1e-5
NEG = -1e30
SCALE = HD ** -0.5
MAX_REL = 16
SHIFTS = 2 * T - 1
SN, SP, SH = 8, 4, 24
SLOTS = SN * SP
CAPACITY = -(-N * 2 * 5 // (8 * 4))

FFN = {1: (6, 8, 6, 128, 1), 2: (0, 8, 2, 96, 2), 3: (8, 16, 4, 128, 1)}


SEMAPHORES = []


def alloc(nc, ctx):
    def sb(name, shape, dt=F32):
        return ctx.enter_context(nc.sbuf_tensor(name, shape, dt))

    def ps(name, shape, dt=F32):
        return ctx.enter_context(nc.psum_tensor(name, shape, dt))

    def sem(name):
        SEMAPHORES.append(nc.alloc_semaphore(name))
        return SEMAPHORES[-1]
    return sb, ps, sem


def attention_names(layer):
    kinds = ("q", "qs", "k", "ks") if layer == 1 else ("q", "k")
    return [f"att{layer}_w{n}" for n in kinds + ("v",)] + [f"att{layer}_{n}" for n in ("bias", "wp", "bv", "bp")]


FIRST_LOADS = attention_names(0)
LATER_LOADS = (["sm_slots", "sm_scale", "sm_down", "sm_bdown", "sm_up", "sm_bup", "sm_own_expert", "sm_own_image",
                "sm_own_image4"] + attention_names(1) + ["rope", "rt1_w", "order8", "later"] +
               attention_names(2) + ["rel_blocks", "rt2_w", "rt2_b", "ffn2_ubias", "ffn2_dbias", "ta_w", "rt3_w", "order16"])


def load_ahead(sp, I, held, names, loaded):
    for name in names:
        dst = held[name]
        sp.dma_start(dst[tuple(slice(None) for _ in dst.shape)], I[name]).then_inc(loaded, 16)


def reset_semaphores(nc):
    nc.clear_and_free_semaphores(SEMAPHORES)
    nc.all_engine_barrier()
    SEMAPHORES.clear()


def patch_embedding(nc, I, h, held, const, raw):
    with ExitStack() as ctx:
        sb, ps, sem = alloc(nc, ctx)
        KC = I["patches"].shape[1]
        x = sb("tok_x", [128, KC, N])
        w = sb("tok_w", [128, KC, D])
        pos = sb("tok_pos", [PT, D])
        first = sb("tok_first", [PT, D])
        acc = ps("tok_acc", [PT, NP, BANK])
        loaded = [sem(f"tok_loaded{k}") for k in range(KC)]
        small = sem("tok_small_loaded")
        ahead = sem("tok_ahead_loaded")
        const_loaded = sem("const_loaded")
        made = sem("const_made")
        summed = sem("tok_const_summed")
        product = sem("tok_product_ready")
        done = sem("tok_done")
        with nc.Block() as block:
            @block.sync
            def _(sp):
                for k in range(KC):
                    sp.dma_start(w[:, k, :], I["tok_w"][:, k, :]).then_inc(loaded[k], 16)
                    sp.dma_start(x[:, k, :], I["patches"][:, k, :]).then_inc(loaded[k], 16)
                sp.dma_start(pos[:, :], I["tok_pos"]).then_inc(small, 16)
                sp.dma_start(first[:, :], I["tok_first"]).then_inc(small, 16)
                for name, dst in (("ident", const["ident"]), ("own_head", const["own_head"]), ("own_key", const["own_key"]),
                                  ("copy_keys", raw["copy_keys"]), ("place", raw["place"]), ("causal", raw["causal"])):
                    sp.dma_start(dst[tuple(slice(None) for _ in dst.shape)], I[name]).then_inc(const_loaded, 16)
                load_ahead(sp, I, held, FIRST_LOADS, ahead)
                sp.wait_ge(ahead, 16 * len(FIRST_LOADS))

            @block.tensor
            def _(pe):
                for k in range(KC):
                    pe.wait_ge(loaded[k], 32)
                    for j in range(NP):
                        mm = pe.matmul(acc[:, j, 0:D], lhsT=x[:, k, j * PT:(j + 1) * PT], rhs=w[:, k, :],
                                       start=(k == 0), stop=(k == KC - 1))
                        if k == KC - 1:
                            mm.then_inc(product, 1)

            @block.gpsimd
            def _(pool):
                pool.memset(const["ones"][:, :], 1.0).then_inc(made, 1)
                pool.memset(const["power"][:, 0, :], -0.5).then_inc(made, 1)
                pool.memset(const["power"][:, 1, :], 0.5).then_inc(made, 1)
                pool.memset(const["half"][:, :, :], 0.5).then_inc(made, 1)
                pool.wait_ge(const_loaded, 16 * 6)
                pool.tensor_copy(const["identb"][:, :], const["ident"][:, :]).then_inc(made, 1)
                pool.tensor_copy(const["copy_keys"][:, :, :], raw["copy_keys"][:, :, :]).then_inc(made, 1)
                pool.tensor_copy(const["place"][:, :, :], raw["place"][:, :, :]).then_inc(made, 1)
                pool.tensor_copy(const["causal"][:, :], raw["causal"][:, :]).then_inc(made, 1)

            @block.vector
            def _(dve):
                dve.wait_ge(small, 32)
                dve.tensor_tensor(pos[:, :], pos[:, :], first[:, :], ALU.add).then_inc(summed, 1)
                dve.wait_ge(summed, 1)
                for j in range(NP):
                    dve.wait_ge(product, j + 1)
                    dve.tensor_tensor(h[:, j, :], acc[:, j, 0:D], pos[:, :], ALU.add).then_inc(done, 1)


def to_feature_major(nc, src, dst, ident, tag):
    with ExitStack() as ctx:
        sb, ps, sem = alloc(nc, ctx)
        tp = ps(tag + "_tp", [C, 4, BANK])
        ready = sem(tag + "_tp_ready")
        copied = sem(tag + "_tp_copied")
        with nc.Block() as block:
            @block.tensor
            def _(pe):
                for half in range(2):
                    turn_half(pe, src, tp, half, ident, ready)

            @block.scalar
            def _(act):
                for half in range(2):
                    keep_half(act, tp, dst, half, ready, copied)


def turn_half(pe, src, tp, half, ident, ready):
    for c in range(2):
        for q in range(NP // 2):
            mm = pe.transpose(tp[:, 2 * half + c, q * PT:(q + 1) * PT],
                              src[:, half * (NP // 2) + q, c * C:(c + 1) * C], ident[0:PT, 0:PT])
        mm.then_inc(ready, 1)


def keep_half(act, tp, dst, half, ready, copied):
    for c in range(2):
        act.wait_ge(ready, 2 * half + c + 1)
        act.activation(dst[:, c, half * HALF:(half + 1) * HALF], tp[:, 2 * half + c, 0:HALF], ACT.Copy).then_inc(copied, 1)


class Norm:
    def __init__(self, nc, ctx, tag):
        sb, ps, sem = alloc(nc, ctx)
        self.stats = sb(tag + "_stats", [PT, NP, 6])
        self.mean_var = sb(tag + "_mean_var", [PT, NP, 2])
        self.rstd = sb(tag + "_rstd", [PT, NP])
        self.stats_ready = sem(tag + "_stats_ready")
        self.aggregated = sem(tag + "_aggregated")
        self.eps_added = sem(tag + "_eps_added")
        self.root_ready = sem(tag + "_root_ready")
        self.normalised = sem(tag + "_normalised")


def pair_stats(dve, h, n, j, added, count):
    dve.wait_ge(added, count)
    dve.bn_stats(n.stats[:, bass.ds(j, 1), :].rearrange("p a s -> p (a s)"),
                 h[:, bass.ds(j, 1), :].rearrange("p a d -> p (a d)")).then_inc(n.stats_ready, 1)


def aggregate(dve, n, half):
    for j in range(half * (NP // 2), (half + 1) * (NP // 2)):
        dve.wait_ge(n.stats_ready, j + 1)
        dve.bn_aggr(n.mean_var[:, j, :], n.stats[:, j, :]).then_inc(n.aggregated, 1)


def norm_on_dve(dve, h, n):
    aggregate(dve, n, 1)
    for j in range(NP):
        if j % (NP // 2) == 0:
            dve.wait_ge(n.root_ready, j // (NP // 2) + 1)
        dve.tensor_scalar(h[:, j, :], h[:, j, :], n.mean_var[:, j, 0:1], n.rstd[:, j:j + 1],
                          ALU.subtract, ALU.mult).then_inc(n.normalised, 1)


def roots_on_pool(pool, n, power, half):
    pairs = slice(half * (NP // 2), (half + 1) * (NP // 2))
    pool.wait_ge(n.aggregated, (half + 1) * (NP // 2))
    pool.tensor_scalar(n.rstd[:, pairs], n.mean_var[:, pairs, 1], LN_EPS, None, ALU.add).then_inc(n.eps_added, 1)
    pool.wait_ge(n.eps_added, half + 1)
    pool.tensor_tensor(n.rstd[:, pairs], n.rstd[:, pairs], power[:, 0, pairs], ALU.pow).then_inc(n.root_ready, 1)


def layer_norm(nc, h, n, tag, unit=None, power=None):
    with ExitStack() as ctx:
        sb, ps, sem = alloc(nc, ctx)
        sq = sb(tag + "_squares", [PT, NP, D])
        length = sb(tag + "_length", [PT, NP])
        summed = sem(tag + "_squares_summed")
        rooted = sem(tag + "_length_ready")
        with nc.Block() as block:
            @block.vector
            def _(dve):
                norm_on_dve(dve, h, n)
                if unit is not None:
                    dve.wait_ge(rooted, 1)
                    dve.tensor_scalar(length[:, :], length[:, :], L2_EPS, None, ALU.add).then_inc(rooted, 1)
                    dve.wait_ge(rooted, 2)
                    dve.reciprocal(length[:, :], length[:, :]).then_inc(rooted, 1)
                    dve.wait_ge(rooted, 3)
                    dve.tensor_tensor(unit[:, :, :], h[:, :, :],
                                      length[:, :].unsqueeze(2).to_broadcast([PT, NP, D]), ALU.mult).then_inc(rooted, 1)

            @block.scalar
            def _(act):
                if unit is not None:
                    for j in range(NP):
                        act.wait_ge(n.normalised, j + 1)
                        act.activation(sq[:, j, :], h[:, j, :], ACT.Square, accum_out=length[:, j:j + 1]).then_inc(summed, 1)

            @block.gpsimd
            def _(pool):
                roots_on_pool(pool, n, power, 1)
                if unit is not None:
                    pool.wait_ge(summed, NP)
                    pool.tensor_tensor(length[:, :], length[:, :], power[:, 1, :], ALU.pow).then_inc(rooted, 1)


def norm_to_feature_major(nc, h, n, dst, const, tag, split=None):
    ident = const["ident"]
    with ExitStack() as ctx:
        sb, ps, sem = alloc(nc, ctx)
        tp = ps(tag + "_tp", [C, 4, BANK])
        ready = sem(tag + "_tp_ready")
        copied = sem(tag + "_tp_copied")
        rest = D - 128
        if split:
            wide = ps(tag + "_wide", [128, 4, BANK])
            twice = sb(tag + "_twice", [PT, NP, 2, rest])
            doubled = sem(tag + "_doubled")
            w_ready = sem(tag + "_wide_ready")
            w_high = sem(tag + "_high_ready")
            w_low = sem(tag + "_low_ready")
        with nc.Block() as block:
            @block.tensor
            def _(pe):
                for half in range(2):
                    pe.wait_ge(n.normalised, (half + 1) * (NP // 2))
                    turn_half(pe, h, tp, half, ident, ready)
                    if split:
                        for q in range(NP // 2):
                            pe.transpose(wide[:, 2 * half, q * PT:(q + 1) * PT], h[:, half * (NP // 2) + q, 0:128],
                                         ident[0:PT, 0:PT])
                        pe.wait_ge(doubled, half + 1)
                        for q in range(NP // 2):
                            mm = pe.transpose(wide[:, 2 * half + 1, q * PT:(q + 1) * PT],
                                              twice[:, half * (NP // 2) + q, :, :].rearrange("p a f -> p (a f)"),
                                              ident[0:PT, 0:PT])
                        mm.then_inc(w_ready, 1)

            @block.scalar
            def _(act):
                for half in range(2):
                    cols = slice(half * HALF, (half + 1) * HALF)
                    pairs = slice(half * (NP // 2), (half + 1) * (NP // 2))
                    if split:
                        act.wait_ge(n.normalised, (half + 1) * (NP // 2))
                        act.activation(twice[:, pairs, :, :],
                                       h[:, pairs, 128:D].unsqueeze(2).to_broadcast([PT, NP // 2, 2, rest]),
                                       ACT.Copy).then_inc(doubled, 1)
                    keep_half(act, tp, dst, half, ready, copied)
                    if split:
                        act.wait_ge(w_ready, half + 1)
                        act.activation(split[0][:, cols], wide[:, 2 * half, 0:HALF], ACT.Copy, scale=SPLIT).then_inc(w_high, 1)
                        act.activation(split[1][0:rest, cols], wide[0:rest, 2 * half + 1, 0:HALF], ACT.Copy,
                                       scale=SPLIT).then_inc(w_high, 1)
                        act.activation(split[3][rest:128, cols], wide[rest:128, 2 * half + 1, 0:HALF], ACT.Copy,
                                       scale=SPLIT).then_inc(w_high, 1)

            @block.gpsimd
            def _(pool):
                roots_on_pool(pool, n, const["power"], 1)

            @block.vector
            def _(dve):
                norm_on_dve(dve, h, n)
                if split:
                    for half in range(2):
                        cols = slice(half * HALF, (half + 1) * HALF)
                        dve.wait_ge(w_high, 3 * half + 3)
                        dve.scalar_tensor_tensor(split[2][:, cols], wide[:, 2 * half, 0:HALF], SPLIT, split[0][:, cols],
                                                 ALU.mult, ALU.subtract).then_inc(w_low, 1)
                        dve.scalar_tensor_tensor(split[1][rest:128, cols], wide[rest:128, 2 * half + 1, 0:HALF], SPLIT,
                                                 split[3][rest:128, cols], ALU.mult, ALU.subtract).then_inc(w_low, 1)


def attention(nc, I, layer, h, hT, const, held, norm):
    rope, rel = layer == 1, layer == 2
    p = f"att{layer}"
    ident = const["ident"]
    kinds = ["q", "qs", "k", "ks"] if rope else ["q", "k"]
    with ExitStack() as ctx:
        sb, ps, sem = alloc(nc, ctx)
        w = {n: held[f"{p}_w{n}"] for n in kinds + ["v"]}
        wp, bias, bv, bp = (held[f"{p}_{n}"] for n in ("wp", "bias", "bv", "bp"))
        x_stage = sb(p + "_x_stage", [C, 2, 2, 2, GH, T])
        x_staged = sem(p + "_x_staged")
        qT = sb(p + "_qT", [C, 2, N])
        kT = sb(p + "_kT", [C, 2, N])
        if rope:
            table = held["rope"]
            turned = sb(p + "_turned", [C, 2, HALF])
            straight = sb(p + "_straight", [C, 2, HALF])
        if rel:
            rbd = held["rel_blocks"]
            biases = sb(p + "_score_bias", [SR, 2, H * T])
            grid = sb(p + "_rel_grid", [PT, 4, 2 * HC * SHIFTS])
            grid_dram = I["rel_scratch"]
        biased = sem(p + "_score_bias_ready")
        grid_copied = sem(p + "_grid_copied")
        grid_stored = [sem(f"{p}_grid_stored{i}") for i in range(4)]

        def stage_x(act, j, k):
            for c in range(2):
                act.activation(x_stage[:, k, c, :, :, :],
                               hT[:, c, bass.ds(j * PT, PT)].rearrange("p (b t) -> p b t", b=2)
                               .unsqueeze(2).to_broadcast([C, 2, GH, T]), ACT.Copy).then_inc(x_staged, 1)

        with ExitStack() as pre:
            _, pps, psem = alloc(nc, pre)
            acc = pps(p + "_acc", [128, 8, BANK])
            product = psem(p + "_product_ready")
            taken = psem(p + "_product_taken")
            gridded = psem(p + "_grid_ready")
            bias_taken = psem(p + "_output_bias_ready")
            kept = psem(p + "_residual_ready")
            KN = len(kinds)
            if rel:
                tw = held["ta_w"][:, :, :].rearrange("p c n -> p (c n)")
                below = pre.enter_context(nc.sbuf_tensor("ta_w_below", [C, 2 * 3 * D], F32))
                tsum = pre.enter_context(nc.sbuf_tensor("ta_w_sum", [C, 1], F32))
                tlim = pre.enter_context(nc.sbuf_tensor("ta_w_limits", [128, 2], F32))
                tstep = psem("ta_weight_step")
                tsummed = psem("ta_weight_sum_ready")
                ttaken = psem("ta_weight_sum_taken")
            with nc.Block() as block:
                @block.sync
                def _(sp):
                    if rel:
                        for j in range(NP):
                            sp.wait_ge(grid_copied, 2 * j + 2)
                            sp.dma_start(grid_dram[j * PT:(j + 1) * PT, :], grid[:, j % 4, :]).then_inc(grid_stored[j % 4], 16)

                @block.gpsimd
                def _(pool):
                    if rel:
                        pool.memset(biases[:, :, :], 0.0).then_inc(biased, 1)
                    pool.wait_ge(bias_taken, 1)
                    pool.tensor_tensor(h[:, :, :], h[:, :, :], bp[:, :].unsqueeze(1).to_broadcast([PT, NP, D]),
                                       ALU.add).then_inc(kept, 1)

                @block.tensor
                def _(pe):
                    for g in range(G):
                        mm = pe.matmul(acc[0:PT, 0, 0:D], lhsT=bv[:, g, :], rhs=wp[:, g, :],
                                       start=(g == 0), stop=(g == G - 1))
                    mm.then_inc(product, 1)
                    for s in range(4):
                        co, half = s // 2, s % 2
                        for m, name in enumerate(kinds):
                            n = 1 + s * KN + m
                            if n == 8:
                                pe.wait_ge(bias_taken, 1)
                                if rel:
                                    pe.wait_ge(tstep, 1)
                                    pe.matmul(acc[:, 0, 0:1], lhsT=const["ones"][0:C, :], rhs=tsum[:, :],
                                              start=True, stop=True).then_inc(tsummed, 1)
                                    pe.wait_ge(ttaken, 1)
                            elif n > 8:
                                pe.wait_ge(taken, n - 8)
                            for ci in range(2):
                                mm = pe.matmul(acc[0:C, n % 8, 0:HALF], lhsT=w[name][:, ci, co * C:(co + 1) * C],
                                               rhs=hT[:, ci, half * HALF:(half + 1) * HALF],
                                               start=(ci == 0), stop=(ci == 1))
                            mm.then_inc(product, 1)
                    if rel:
                        pe.wait_ge(taken, 4 * KN)
                        for j in range(NP):
                            for ci in range(2):
                                s = 2 * j + ci
                                bank = 1 + s % 6
                                if s >= 6:
                                    pe.wait_ge(grid_copied, s - 5)
                                pe.matmul(acc[0:PT, bank, 0:HC * SHIFTS], lhsT=qT[:, ci, j * PT:(j + 1) * PT],
                                          rhs=rbd[:, :], start=True, stop=True).then_inc(gridded, 1)

                @block.scalar
                def _(act):
                    for j in range(2):
                        stage_x(act, j, j)
                    if not rope:
                        for s in range(4):
                            co, half = s // 2, s % 2
                            for m, name in enumerate(kinds):
                                n = 1 + s * KN + m
                                act.wait_ge(product, n + 1)
                                dst = qT if name == "q" else kT
                                act.activation(dst[:, co, half * HALF:(half + 1) * HALF],
                                               acc[0:C, n % 8, 0:HALF], ACT.Identity,
                                               bias=bias[:, co, m:m + 1]).then_inc(taken, 1)
                    if rel:
                        for s in range(2 * NP):
                            j, ci = s // 2, s % 2
                            act.wait_ge(gridded, s + 1)
                            if j >= 4:
                                act.wait_ge(grid_stored[j % 4], 16)
                            act.activation(grid[:, j % 4, ci * HC * SHIFTS:(ci + 1) * HC * SHIFTS],
                                           acc[0:PT, 1 + s % 6, 0:HC * SHIFTS], ACT.Copy).then_inc(grid_copied, 1)

                @block.vector
                def _(dve):
                    dve.wait_ge(product, 1)
                    dve.tensor_tensor(bp[:, :], bp[:, :], acc[0:PT, 0, 0:D], ALU.add).then_inc(bias_taken, 1)
                    if rel:
                        ws = const["ta_ws"]
                        dve.tensor_reduce(tsum[:, :], tw, AX.X, ALU.add, apply_absolute_value=True).then_inc(tstep, 1)
                        dve.wait_ge(tsummed, 1)
                        dve.tensor_scalar(ws[:, :], acc[:, 0, 0:1], 1.0 / (D * 3 * D), TERNARY_EPS, ALU.mult, ALU.add).then_inc(ttaken, 1)
                        dve.wait_ge(ttaken, 1)
                        dve.tensor_scalar(tlim[:, 0:1], ws[:, :], 0.5, None, ALU.mult).then_inc(tstep, 1)
                        dve.tensor_scalar(tlim[:, 1:2], ws[:, :], -0.5, None, ALU.mult).then_inc(tstep, 1)
                        dve.wait_ge(tstep, 3)
                        dve.tensor_scalar(below[:, :], tw, tlim[0:C, 1:2], None, ALU.is_lt).then_inc(tstep, 1)
                        dve.wait_ge(tstep, 4)
                        dve.scalar_tensor_tensor(tw, tw, tlim[0:C, 0:1], below[:, :], ALU.is_gt, ALU.subtract).then_inc(tstep, 1)
                    if rope:
                        for s in range(4):
                            co, half = s // 2, s % 2
                            for m in range(2):
                                dst = (qT, kT)[m]
                                for t in range(2):
                                    n = 1 + s * KN + 2 * m + t
                                    dve.wait_ge(product, n + 1)
                                    src = acc[0:C, n % 8, 0:HALF].rearrange("p (b t) -> p b t", t=T)
                                    out = (straight, turned)[t][:, m, :].rearrange("p (b t) -> p b t", t=T)
                                    dve.scalar_tensor_tensor(out, src, bias[:, co, 2 * m + t:2 * m + t + 1],
                                                             table[:, t, :].unsqueeze(1).to_broadcast([C, B // 2, T]),
                                                             ALU.add, ALU.mult).then_inc(taken, 1)
                                dve.wait_ge(taken, s * KN + 2 * m + 2)
                                dve.tensor_tensor(dst[:, co, half * HALF:(half + 1) * HALF], straight[:, m, :],
                                                  turned[:, m, :], ALU.add)

        with ExitStack() as main:
            msb, mps, msem = alloc(nc, main)
            q_stage = msb(p + "_q_stage", [C, 2, 2, PT])
            k_blocks = msb(p + "_k_blocks", [C, 2, 2, 2, HC, T])
            probs = msb(p + "_probs", [SR, 2, H * T])
            probsT = msb(p + "_probsT", [GK, 2, G, SR])
            v_blocks = msb(p + "_v_blocks", [GK, 2, 2, D])
            oT = msb(p + "_oT", [GD, 2, G, PT])
            peak = msb(p + "_peak", [SR, 2, H])
            total = msb(p + "_total", [SR, 2, H])
            s_ps = mps(p + "_s", [128, 2, BANK])
            t_ps = mps(p + "_t", [128, 2, BANK])
            v_ps = mps(p + "_v", [128, 2, BANK])
            oy_ps = mps(p + "_oy", [128, 2, BANK])
            staged = msem(p + "_keys_staged")
            staged_second = msem(p + "_second_pairs_keys_staged")
            q_staged = msem(p + "_queries_staged")
            values = msem(p + "_values_ready")
            scores = msem(p + "_scores_ready")
            peaked = msem(p + "_peak_ready")
            shifted = msem(p + "_shifted")
            exped = msem(p + "_exponentials_ready")
            totaled = msem(p + "_totals_ready")
            inverted = msem(p + "_inverted")
            weighted = msem(p + "_probs_ready")
            v_ready = msem(p + "_v_blocks_ready")
            turned_s = msem(p + "_probsT_ready")
            pT_copied = msem(p + "_probsT_copied")
            o_ready = msem(p + "_outputs_ready")
            o_copied = msem(p + "_outputs_copied")
            y_ready = msem(p + "_projected")
            added = msem(p + "_added")
            ahead = msem(p + "_ahead_loaded")
            rel_loaded = [msem(f"{p}_rel_loaded{k}") for k in range(2)]

            def y_of(k):
                return oy_ps[0:PT, k, G * PT:G * PT + D]

            def stage_k(engine, j, k, done):
                for c in range(2):
                    engine.tensor_tensor(k_blocks[:, k, c, :, :, :],
                                         kT[:, c, bass.ds(j * PT, PT)].rearrange("p (b t) -> p b t", b=2)
                                         .unsqueeze(2).to_broadcast([C, 2, HC, T]),
                                         const["own_head"][:, :].unsqueeze(1).unsqueeze(3)
                                         .to_broadcast([C, 2, HC, T]), ALU.mult).then_inc(done, 1)

            with nc.Block() as block:
                @block.sync
                def _(sp):
                    if layer == 0:
                        load_ahead(sp, I, held, LATER_LOADS, ahead)
                        sp.wait_ge(ahead, 16 * len(LATER_LOADS))
                    if rel:
                        for i in range(4):
                            sp.wait_ge(grid_stored[i], 32)

                        def rel_pair(i, k, later):
                            if later:
                                sp.wait_ge(scores, 2 * i + k - 1)
                            for img in range(2):
                                src = bass.AP(grid_dram.tensor, (2 * i + k) * (PT * H * SHIFTS) + img * T * H * SHIFTS + T - 1,
                                              [[H * SHIFTS - 1, T], [SHIFTS, H], [1, T]])
                                dst = biases[img * SECOND:img * SECOND + T, k, :].rearrange("p (h t) -> p h t", h=H)
                                sp.dma_start(dst, src).then_inc(rel_loaded[k], 16)
                        for k in range(2):
                            rel_pair(0, k, False)
                        with sp.Fori(1, NP // 2) as i:
                            for k in range(2):
                                rel_pair(i, k, True)

                @block.gpsimd
                def _(pool):
                    stage_k(pool, 0, 0, staged)
                    with pool.Fori(1, NP // 2) as i:
                        for k in range(2):
                            j = 2 * i + k
                            pool.wait_ge(scores, j - 1)
                            stage_k(pool, j, k, staged)
                    roots_on_pool(pool, norm, const["power"], 0)

                @block.tensor
                def _(pe):
                    def value(i, k, later):
                        j = 2 * i + k
                        pe.wait_ge(x_staged, 2 * j + 2)
                        if later:
                            pe.wait_ge(v_ready, j - 1)
                        for img in range(2):
                            for c in range(2):
                                mm = pe.matmul(v_ps[0:GK, k, img * D:(img + 1) * D],
                                               lhsT=x_stage[:, k, c, img, :, :].rearrange("p a t -> p (a t)"),
                                               rhs=w["v"][:, c, :], start=(c == 0), stop=(c == 1))
                        mm.then_inc(values, 1)

                    def score(i, k, later):
                        j = 2 * i + k
                        pe.wait_ge(q_staged, j + 1)
                        if later:
                            pe.wait_ge(staged, 2 * j)
                        elif k == 0:
                            pe.wait_ge(staged, 2)
                        else:
                            pe.wait_ge(staged_second, 2)
                        if later:
                            pe.wait_ge(shifted, j - 1)
                        if rel:
                            pe.wait_ge(rel_loaded[k], 32 * i + 32)
                            pe.matmul(s_ps[0:SR, k, 0:H * T], lhsT=ident[0:SR, 0:SR], rhs=biases[:, k, :],
                                      start=True, stop=False, skip_group_check=True)
                        else:
                            pe.matmul(s_ps[0:SR, k, 0:H * T], lhsT=const["identb"][0:SR, 0:SR], rhs=const["causal"][:, :],
                                      start=True, stop=False, skip_group_check=True)
                        for c in range(2):
                            for img in range(2):
                                mm = pe.matmul(s_ps[img * SECOND:img * SECOND + T, k, c * HC * T:(c + 1) * HC * T],
                                               lhsT=q_stage[:, k, c, img * T:(img + 1) * T],
                                               rhs=k_blocks[:, k, c, img, :, :].rearrange("p a t -> p (a t)"),
                                               start=False, stop=True, skip_group_check=True)
                        mm.then_inc(scores, 1)

                    def body(i, later, more):
                        for k in range(2):
                            t = 2 * i + k
                            if not later and k == 0:
                                for m in range(2):
                                    value(i + 1, m, True)
                            pe.wait_ge(weighted, t + 1)
                            if later:
                                pe.wait_ge(pT_copied, t - 1)
                            for g in range(G):
                                mm = pe.transpose(t_ps[0:GK, k, g * SR:(g + 1) * SR],
                                                  probs[:, k, g * GK:(g + 1) * GK], ident[0:SR, 0:SR])
                            mm.then_inc(turned_s, 1)
                            if more:
                                score(i + 1, k, True)
                            pe.wait_ge(pT_copied, t + 1)
                            pe.wait_ge(v_ready, t + 1)
                            if later:
                                pe.wait_ge(added, t - 1)
                            for img in range(2):
                                for g in range(G):
                                    mm = pe.matmul(oy_ps[0:GD, k, g * PT + img * T:g * PT + (img + 1) * T],
                                                   lhsT=v_blocks[:, k, img, g * GD:(g + 1) * GD],
                                                   rhs=probsT[:, k, g, img * SECOND:img * SECOND + T],
                                                   start=True, stop=True)
                            mm.then_inc(o_ready, 1)
                            if more and later:
                                value(i + 1, k, True)
                            pe.wait_ge(o_copied, t + 1)
                            for g in range(G):
                                mm = pe.matmul(y_of(k), lhsT=oT[:, k, g, :], rhs=wp[:, g, :],
                                               start=(g == 0), stop=(g == G - 1))
                            mm.then_inc(y_ready, 1)
                    for k in range(2):
                        value(0, k, False)
                    for k in range(2):
                        score(0, k, False)
                    body(0, False, True)
                    with pe.Fori(1, NP // 2 - 1) as i:
                        body(i, True, True)
                    body(NP // 2 - 1, True, False)

                @block.scalar
                def _(act):
                    def stage_q(j, k):
                        act.activation(q_stage[:, k, :, :], qT[:, :, bass.ds(j * PT, PT)], ACT.Copy).then_inc(q_staged, 1)

                    def exponentials(t, k):
                        act.wait_ge(shifted, t + 1)
                        act.activation(probs[:, k, :], probs[:, k, :], ACT.Exp, scale=SCALE).then_inc(exped, 1)

                    def body(i, later, left):
                        for k in range(2):
                            t = 2 * i + k
                            act.wait_ge(turned_s, t + 1)
                            if later:
                                act.wait_ge(o_ready, t - 1)
                            act.activation(probsT[:, k, :, :].rearrange("p g s -> p (g s)"), t_ps[0:GK, k, 0:G * SR],
                                           ACT.Copy).then_inc(pT_copied, 1)
                            if left or k == 0:
                                exponentials(t + 1, 1 - k)
                            act.wait_ge(o_ready, t + 1)
                            if later:
                                act.wait_ge(y_ready, t - 1)
                            act.activation(oT[:, k, :, :].rearrange("p g s -> p (g s)"), oy_ps[0:GD, k, 0:G * PT],
                                           ACT.Copy).then_inc(o_copied, 1)
                            if left >= 2 + k and (later or k == 1):
                                act.wait_ge(values, t + 2)
                                stage_x(act, t + 3, 1 - k)
                            if left >= 2 + k:
                                act.wait_ge(scores, t + 2)
                                stage_q(t + 3, 1 - k)
                    stage_q(0, 0)
                    stage_q(1, 1)
                    for k in range(2):
                        act.wait_ge(values, k + 1)
                        stage_x(act, 2 + k, k)
                    exponentials(0, 0)
                    act.wait_ge(scores, 1)
                    stage_q(2, 0)
                    body(0, False, NP - 2)
                    with act.Fori(1, NP // 2 - 2) as i:
                        body(i, True, 4)
                    body(NP // 2 - 2, True, 2)
                    body(NP // 2 - 1, True, 0)

                @block.vector
                def _(dve):
                    def heads(t):
                        return t.rearrange("p (h t) -> p h t", h=H)

                    def shift(n, k, later):
                        dve.wait_ge(scores, n + 1)
                        dve.tensor_reduce(peak[:, k, :], heads(s_ps[0:SR, k, 0:H * T]), AX.X, ALU.max).then_inc(peaked, 1)
                        dve.wait_ge(peaked, n + 1)
                        if later:
                            dve.wait_ge(turned_s, n - 1)
                        dve.tensor_tensor(heads(probs[:, k, :]), heads(s_ps[0:SR, k, 0:H * T]),
                                          peak[:, k, :].unsqueeze(2).to_broadcast([SR, H, T]),
                                          ALU.subtract).then_inc(shifted, 1)

                    def value_blocks(n, k, later):
                        dve.wait_ge(values, n + 1)
                        if later:
                            dve.wait_ge(o_ready, n - 1)
                        dve.tensor_tensor(v_blocks[:, k, :, :],
                                          v_ps[0:GK, k, 0:2 * D].rearrange("p (b f) -> p b f", b=2),
                                          const["own_key"][:, :].unsqueeze(1).to_broadcast([GK, 2, D]),
                                          ALU.mult).then_inc(v_ready, 1)

                    def add(t, k):
                        dve.wait_ge(y_ready, t + 1)
                        hj = h[:, bass.ds(t, 1), :].rearrange("p a d -> p (a d)")
                        dve.tensor_tensor(hj, hj, y_of(k), ALU.add).then_inc(added, 1)
                        pair_stats(dve, h, norm, t, added, t + 1)

                    def body(i, later, more):
                        for k in range(2):
                            t = 2 * i + k
                            dve.wait_ge(exped, t + 1)
                            dve.tensor_reduce(total[:, k, :], heads(probs[:, k, :]), AX.X, ALU.add).then_inc(totaled, 1)
                            dve.wait_ge(totaled, t + 1)
                            dve.reciprocal(total[:, k, :], total[:, k, :]).then_inc(inverted, 1)
                            dve.wait_ge(inverted, t + 1)
                            dve.tensor_tensor(heads(probs[:, k, :]), heads(probs[:, k, :]),
                                              total[:, k, :].unsqueeze(2).to_broadcast([SR, H, T]),
                                              ALU.mult).then_inc(weighted, 1)
                            if more or k == 0:
                                shift(t + 1, 1 - k, later or k == 1)
                                if later or k == 1:
                                    value_blocks(t + 1, 1 - k, True)
                            if later or k == 1:
                                add(t - 1, 1 - k)
                    stage_k(dve, 1, 1, staged_second)
                    for k in range(2):
                        value_blocks(k, k, False)
                    shift(0, 0, False)
                    body(0, False, True)
                    with dve.Fori(1, NP // 2 - 1) as i:
                        body(i, True, True)
                    body(NP // 2 - 1, True, False)
                    aggregate(dve, norm, 0)
                    add(NP - 1, 1)


def soft_mixture(nc, h, unit, unitT, const, held, norm):
    ident = const["ident"]
    with ExitStack() as ctx:
        sb, ps, sem = alloc(nc, ctx)
        slots, scale, down, bdown, up, bup, own_expert, own_image, own_image4 = (
            held["sm_" + n] for n in ("slots", "scale", "down", "bdown", "up", "bup", "own_expert", "own_image", "own_image4"))
        squares = sb("sm_squares", [C, 2, SLOTS])
        length = sb("sm_length", [C, 2, SP])
        logitsT = sb("sm_logitsT", [SLOTS, N])
        dispT = sb("sm_dispT", [SLOTS, N])
        comb = sb("sm_comb", [PT, NP, SLOTS])
        peak = sb("sm_peak", [SLOTS, B])
        total = sb("sm_total", [SLOTS, B])
        cpeak = sb("sm_cpeak", [PT, NP])
        ctotal = sb("sm_ctotal", [PT, NP])
        dispatch = sb("sm_dispatch", [PT, NP, 2, SLOTS])
        combine = sb("sm_combine", [PT, NP, 4, SLOTS])
        combineT = sb("sm_combineT", [128, NP, PT])
        slotT = sb("sm_slotT", [C, 2, B * SLOTS])
        hidden = sb("sm_hidden", [C, 2, B * SLOTS])
        masked = sb("sm_masked", [C, 2, B * SLOTS])
        out = sb("sm_out", [128, 4, D])
        l_ps = ps("sm_l_ps", [128, 2, BANK])
        t_ps = ps("sm_t_ps", [128, 2, BANK])
        c_ps = ps("sm_c_ps", [128, 2, BANK])
        y_ps = ps("sm_y_ps", [128, 2, BANK])
        slots_ready = sem("sm_slots_step")
        rooted = sem("sm_slot_lengths_ready")
        logits = sem("sm_logits_ready")
        kept = sem("sm_logits_kept")
        step = sem("sm_vector_step")
        exped = sem("sm_exponentials_ready")
        shifted = sem("sm_shifted")
        turned = sem("sm_transposed")
        disp = sem("sm_dispT_ready")
        dready = sem("sm_dispatch_ready")
        cready = sem("sm_combine_ready")
        slotted = sem("sm_slot_inputs_ready")
        slots_kept = sem("sm_slot_inputs_kept")
        hid = sem("sm_hidden_product_ready")
        gelued = sem("sm_gelu_ready")
        mready = sem("sm_masked_ready")
        oready = sem("sm_out_product_ready")
        okept = sem("sm_out_kept")
        cturned = sem("sm_combine_transposed")
        ckept = sem("sm_combineT_kept")
        yready = sem("sm_result_ready")
        added = sem("sm_added")

        with nc.Block() as block:
            @block.gpsimd
            def _(pool):
                pool.wait_ge(slots_ready, 2)
                pool.tensor_tensor(length[:, :, :], length[:, :, :],
                                   const["half"][:, :, :], ALU.pow).then_inc(rooted, 1)
                roots_on_pool(pool, norm, const["power"], 0)

            @block.tensor
            def _(pe):
                pe.wait_ge(slots_ready, 6)
                for half in range(2):
                    for c in range(2):
                        mm = pe.matmul(l_ps[0:SLOTS, half, 0:HALF], lhsT=slots[:, c, :],
                                       rhs=unitT[:, c, half * HALF:(half + 1) * HALF], start=(c == 0), stop=(c == 1))
                    mm.then_inc(logits, 1)
                pe.wait_ge(kept, 2)
                for j in range(NP):
                    mm = pe.transpose(t_ps[0:PT, 0, j * SLOTS:(j + 1) * SLOTS], logitsT[:, j * PT:(j + 1) * PT],
                                      ident[0:SLOTS, 0:SLOTS])
                mm.then_inc(turned, 1)
                pe.wait_ge(disp, 1)
                for j in range(NP):
                    mm = pe.transpose(t_ps[0:PT, 1, j * SLOTS:(j + 1) * SLOTS], dispT[:, j * PT:(j + 1) * PT],
                                      ident[0:SLOTS, 0:SLOTS])
                mm.then_inc(turned, 1)
                pe.wait_ge(dready, 1)
                for c in range(2):
                    for j in range(NP):
                        mm = pe.matmul(l_ps[0:C, c, j * 2 * SLOTS:(j + 1) * 2 * SLOTS], lhsT=unit[:, j, c * C:(c + 1) * C],
                                       rhs=dispatch[:, j, :, :].rearrange("p b s -> p (b s)"), start=True, stop=True)
                    mm.then_inc(slotted, 1)
                pe.wait_ge(cready, 2)
                for j in range(NP):
                    mm = pe.transpose(c_ps[:, j // 4, (j % 4) * PT:(j % 4 + 1) * PT],
                                      combine[:, j, :, :].rearrange("p b s -> p (b s)"), ident[0:PT, 0:PT])
                mm.then_inc(cturned, 1)
                pe.wait_ge(slots_kept, 2)
                for e in range(2):
                    for c in range(2):
                        mm = pe.matmul(l_ps[0:C, e, :], lhsT=down[:, c, e * C:(e + 1) * C], rhs=slotT[:, c, :],
                                       start=(c == 0), stop=(c == 1))
                    mm.then_inc(hid, 1)
                pe.wait_ge(mready, 2)
                for q in range(4):
                    for e in range(2):
                        mm = pe.matmul(t_ps[:, q // 2, (q % 2) * D:(q % 2 + 1) * D], lhsT=masked[:, e, q * 128:(q + 1) * 128],
                                       rhs=up[:, e, :], start=(e == 0), stop=(e == 1))
                mm.then_inc(oready, 1)
                pe.wait_ge(okept, 2)
                pe.wait_ge(ckept, 2)
                for j in range(NP):
                    if j >= 2:
                        pe.wait_ge(added, j - 1)
                    pe.matmul(y_ps[0:PT, j % 2, 0:D], lhsT=combineT[:, j, :], rhs=out[:, j // 2, :],
                              start=True, stop=True).then_inc(yready, 1)

            @block.scalar
            def _(act):
                act.wait_ge(shifted, 1)
                act.activation(dispT[:, :], dispT[:, :], ACT.Exp).then_inc(exped, 1)
                act.wait_ge(shifted, 2)
                act.activation(comb[:, :, :], comb[:, :, :], ACT.Exp).then_inc(exped, 1)
                for c in range(2):
                    act.wait_ge(slotted, c + 1)
                    act.activation(slotT[:, c, :], l_ps[0:C, c, :], ACT.Copy).then_inc(slots_kept, 1)
                act.wait_ge(cturned, 1)
                for g in range(2):
                    act.activation(combineT[:, 4 * g:4 * g + 4, :].rearrange("p j t -> p (j t)"), c_ps[:, g, 0:4 * PT],
                                   ACT.Copy).then_inc(ckept, 1)
                for e in range(2):
                    act.wait_ge(hid, e + 1)
                    act.activation(hidden[:, e, :], l_ps[0:C, e, :], ACT.Gelu, bias=bdown[:, e:e + 1]).then_inc(gelued, 1)

            @block.vector
            def _(dve):
                dve.tensor_tensor(squares[:, :, :], slots[:, :, :], slots[:, :, :], ALU.mult).then_inc(slots_ready, 1)
                dve.wait_ge(slots_ready, 1)
                dve.tensor_reduce(length[:, :, :], squares[:, :, :].rearrange("p c (n s) -> p c s n", n=SN), AX.X,
                                  ALU.add).then_inc(slots_ready, 1)
                dve.wait_ge(rooted, 1)
                dve.tensor_scalar(length[:, :, :], length[:, :, :], L2_EPS, None, ALU.add).then_inc(slots_ready, 1)
                dve.wait_ge(slots_ready, 3)
                dve.reciprocal(length[:, :, :], length[:, :, :]).then_inc(slots_ready, 1)
                dve.wait_ge(slots_ready, 4)
                dve.tensor_scalar(length[:, :, :], length[:, :, :], scale[:, 0:1], None, ALU.mult).then_inc(slots_ready, 1)
                dve.wait_ge(slots_ready, 5)
                dve.tensor_tensor(slots[:, :, :].rearrange("p c (n s) -> p c n s", n=SN),
                                  slots[:, :, :].rearrange("p c (n s) -> p c n s", n=SN),
                                  length[:, :, :].unsqueeze(2).to_broadcast([C, 2, SN, SP]), ALU.mult).then_inc(slots_ready, 1)
                for half in range(2):
                    dve.wait_ge(logits, half + 1)
                    dve.tensor_copy(logitsT[:, half * HALF:(half + 1) * HALF], l_ps[0:SLOTS, half, 0:HALF]).then_inc(kept, 1)
                dve.wait_ge(kept, 2)
                by_image = logitsT[:, :].rearrange("p (b t) -> p b t", t=T)
                disp_by_image = dispT[:, :].rearrange("p (b t) -> p b t", t=T)
                dve.tensor_reduce(peak[:, :], by_image, AX.X, ALU.max).then_inc(step, 1)
                dve.wait_ge(step, 1)
                dve.tensor_tensor(disp_by_image, by_image, peak[:, :].unsqueeze(2).to_broadcast([SLOTS, B, T]),
                                  ALU.subtract).then_inc(shifted, 1)
                dve.wait_ge(turned, 1)
                tok = t_ps[0:PT, 0, 0:NP * SLOTS].rearrange("p (j s) -> p j s", s=SLOTS)
                dve.tensor_reduce(cpeak[:, :], tok, AX.X, ALU.max).then_inc(step, 1)
                dve.wait_ge(step, 2)
                dve.tensor_tensor(comb[:, :, :], tok, cpeak[:, :].unsqueeze(2).to_broadcast([PT, NP, SLOTS]),
                                  ALU.subtract).then_inc(shifted, 1)
                dve.wait_ge(exped, 1)
                dve.tensor_reduce(total[:, :], disp_by_image, AX.X, ALU.add).then_inc(step, 1)
                dve.wait_ge(step, 3)
                dve.reciprocal(total[:, :], total[:, :]).then_inc(step, 1)
                dve.wait_ge(step, 4)
                dve.tensor_tensor(disp_by_image, disp_by_image, total[:, :].unsqueeze(2).to_broadcast([SLOTS, B, T]),
                                  ALU.mult).then_inc(disp, 1)
                dve.wait_ge(exped, 2)
                dve.tensor_reduce(ctotal[:, :], comb[:, :, :], AX.X, ALU.add).then_inc(step, 1)
                dve.wait_ge(step, 5)
                dve.reciprocal(ctotal[:, :], ctotal[:, :]).then_inc(step, 1)
                dve.wait_ge(step, 6)
                dve.tensor_tensor(comb[:, :, :], comb[:, :, :], ctotal[:, :].unsqueeze(2).to_broadcast([PT, NP, SLOTS]),
                                  ALU.mult).then_inc(step, 1)
                dve.wait_ge(turned, 2)
                dve.tensor_tensor(dispatch[:, :, :, :],
                                  t_ps[0:PT, 1, 0:NP * SLOTS].rearrange("p (j s) -> p j s", s=SLOTS)
                                  .unsqueeze(2).to_broadcast([PT, NP, 2, SLOTS]),
                                  own_image[:, :].unsqueeze(1).unsqueeze(3).to_broadcast([PT, NP, 2, SLOTS]),
                                  ALU.mult).then_inc(dready, 1)
                dve.wait_ge(step, 7)
                for par in range(2):
                    dve.tensor_tensor(combine[:, par:NP:2, :, :],
                                      comb[:, par:NP:2, :].unsqueeze(2).to_broadcast([PT, NP // 2, 4, SLOTS]),
                                      own_image4[:, par, :].unsqueeze(1).unsqueeze(3).to_broadcast([PT, NP // 2, 4, SLOTS]),
                                      ALU.mult).then_inc(cready, 1)
                for e in range(2):
                    dve.wait_ge(gelued, e + 1)
                    dve.tensor_tensor(masked[:, e, :].rearrange("p (b s) -> p b s", s=SLOTS),
                                      hidden[:, e, :].rearrange("p (b s) -> p b s", s=SLOTS),
                                      own_expert[:, e, :].unsqueeze(1).to_broadcast([C, B, SLOTS]), ALU.mult).then_inc(mready, 1)
                dve.wait_ge(oready, 1)
                for g in range(2):
                    dve.tensor_tensor(out[:, 2 * g:2 * g + 2, :], t_ps[:, g, 0:2 * D].rearrange("p (q d) -> p q d", q=2),
                                      bup[:, :].unsqueeze(1).to_broadcast([128, 2, D]), ALU.add).then_inc(okept, 1)
                for j in range(NP):
                    dve.wait_ge(yready, j + 1)
                    dve.tensor_tensor(h[:, j, :], h[:, j, :], y_ps[0:PT, j % 2, 0:D], ALU.add).then_inc(added, 1)
                    pair_stats(dve, h, norm, j, added, j + 1)
                    if j == NP // 2 - 1:
                        aggregate(dve, norm, 0)


class Units:
    def __init__(self, nc, ctx, layer):
        sb, ps, sem = alloc(nc, ctx)
        shared, E, upe, M, per_body = FFN[layer]
        self.ring = upe * per_body
        shape = [128, self.ring, 4 * M + D]
        self.w = sb(f"ffn{layer}_w", shape)
        self.high = sb(f"ffn{layer}_w_high", shape, F16)
        self.low = sb(f"ffn{layer}_w_low", shape, F16)
        self.loaded = [sem(f"ffn{layer}_unit_loaded{k}") for k in range(self.ring)]
        self.high_ready = sem(f"ffn{layer}_w_high_ready")
        self.low_ready = sem(f"ffn{layer}_w_low_ready")


AHEAD = 2


def load_unit(sp, I, layer, units, i, k):
    sp.dma_start(units.w[:, k, :], I[f"ffn{layer}_w"][bass.ds(i * units.ring + k, 1), :, :].rearrange("a p m -> p (a m)")
                 ).then_inc(units.loaded[k], 16)


def split_high(act, units, k):
    act.activation(units.high[:, k, :], units.w[:, k, :], ACT.Copy, scale=SPLIT).then_inc(units.high_ready, 1)


def split_low(dve, units, k):
    dve.scalar_tensor_tensor(units.low[:, k, :], units.w[:, k, :], SPLIT, units.high[:, k, :],
                             ALU.mult, ALU.subtract).then_inc(units.low_ready, 1)


def router(nc, I, layer, hT, comb, comb_dram, units, const, held):
    shared, E, upe, M, per_body = FFN[layer]
    p = f"rt{layer}"
    ident = const["ident"]
    with ExitStack() as ctx:
        sb, ps, sem = alloc(nc, ctx)
        w, order = held[p + "_w"], held[f"order{E}"]
        score = sb(p + "_score", [PT, NP, E])
        rest = sb(p + "_rest", [PT, NP, E])
        place = sb(p + "_place", [PT, NP, E])
        hot = [sb(f"{p}_hot{r}", [PT, NP, E]) for r in range(2)]
        best = [sb(f"{p}_best{r}", [PT, NP]) for r in range(2)]
        at = sb(p + "_at", [PT, NP])
        total = sb(p + "_total", [PT, NP])
        combT = sb(p + "_combT", [E, N])
        l_ps = ps(p + "_l_ps", [128, BANK])
        t_ps = ps(p + "_t_ps", [128, 2, BANK])
        logits = sem(p + "_logits_ready")
        step = sem(p + "_vector_step")
        for_exp = sem(p + "_exponents_ready")
        exped = sem(p + "_exponentials_ready")
        combined = sem(p + "_comb_ready")
        turned = sem(p + "_combT_ready")
        kept = sem(p + "_combT_kept")
        stored = sem(p + "_comb_stored")
        wide = [PT, NP, E]
        with nc.Block() as block:
            @block.sync
            def _(sp):
                for k in range(units.ring):
                    load_unit(sp, I, layer, units, 0, k)
                sp.wait_ge(kept, 2)
                sp.dma_start(comb_dram, combT[:, :]).then_inc(stored, 16)
                sp.wait_ge(stored, 16)

            @block.tensor
            def _(pe):
                for j in range(NP):
                    for c in range(2):
                        mm = pe.matmul(l_ps[0:PT, j * E:(j + 1) * E], lhsT=hT[:, c, j * PT:(j + 1) * PT], rhs=w[:, c, :],
                                       start=(c == 0), stop=(c == 1))
                mm.then_inc(logits, 1)
                pe.wait_ge(combined, 1)
                for half in range(2):
                    for q in range(NP // 2):
                        mm = pe.transpose(t_ps[0:E, half, q * PT:(q + 1) * PT], comb[:, half * (NP // 2) + q, :], ident[0:PT, 0:PT])
                    mm.then_inc(turned, 1)

            @block.scalar
            def _(act):
                for k in range(AHEAD):
                    act.wait_ge(units.loaded[k], 16)
                    split_high(act, units, k)
                act.wait_ge(for_exp, 1)
                if layer == 2:
                    act.activation(at[:, :], at[:, :], ACT.Exp).then_inc(exped, 1)
                else:
                    act.activation(score[:, :, :], score[:, :, :], ACT.Exp).then_inc(exped, 1)
                for half in range(2):
                    act.wait_ge(turned, half + 1)
                    act.activation(combT[:, half * HALF:(half + 1) * HALF], t_ps[0:E, half, 0:HALF], ACT.Copy).then_inc(kept, 1)

            @block.vector
            def _(dve):
                count = [0]

                def chain(ins):
                    count[0] += 1
                    ins.then_inc(step, 1)
                    dve.wait_ge(step, count[0])

                def over(t):
                    return t[:, :].unsqueeze(2).to_broadcast(wide)

                dve.wait_ge(logits, 1)
                l3 = l_ps[0:PT, 0:NP * E].rearrange("p (j e) -> p j e", e=E)
                if layer == 2:
                    chain(dve.tensor_tensor(score[:, :, :], l3, held["rt2_b"][:, :].unsqueeze(1).to_broadcast(wide), ALU.add))
                else:
                    chain(dve.tensor_reduce(total[:, :], l3, AX.X, ALU.max))
                    dve.tensor_tensor(score[:, :, :], l3, over(total), ALU.subtract).then_inc(for_exp, 1)
                    dve.wait_ge(exped, 1)
                    chain(dve.tensor_reduce(total[:, :], score[:, :, :], AX.X, ALU.add))
                    chain(dve.reciprocal(total[:, :], total[:, :]))
                    chain(dve.tensor_tensor(score[:, :, :], score[:, :, :], over(total), ALU.mult))
                for r in range(2):
                    src = score if r == 0 else rest
                    chain(dve.tensor_reduce(best[r][:, :], src[:, :, :], AX.X, ALU.max))
                    chain(dve.tensor_tensor(place[:, :, :], src[:, :, :], over(best[r]), ALU.is_lt))
                    chain(dve.scalar_tensor_tensor(place[:, :, :], place[:, :, :], float(4 * E),
                                                   order[:, :].unsqueeze(1).to_broadcast(wide), ALU.mult, ALU.add))
                    chain(dve.tensor_reduce(at[:, :], place[:, :, :], AX.X, ALU.min))
                    chain(dve.tensor_tensor(hot[r][:, :, :], place[:, :, :], over(at), ALU.is_equal))
                    if r == 0:
                        chain(dve.scalar_tensor_tensor(rest[:, :, :], hot[0][:, :, :], NEG, score[:, :, :], ALU.mult, ALU.add))
                if layer == 1:
                    chain(dve.tensor_tensor(total[:, :], best[0][:, :], best[1][:, :], ALU.add))
                    chain(dve.tensor_scalar(total[:, :], total[:, :], 1e-9, None, ALU.max))
                    chain(dve.reciprocal(total[:, :], total[:, :]))
                    for r in range(2):
                        chain(dve.tensor_tensor(best[r][:, :], best[r][:, :], total[:, :], ALU.mult))
                if layer == 2:
                    chain(dve.tensor_tensor(total[:, :], best[1][:, :], best[0][:, :], ALU.subtract))
                    dve.tensor_copy(at[:, :], total[:, :]).then_inc(for_exp, 1)
                    dve.wait_ge(exped, 1)
                    chain(dve.tensor_scalar(total[:, :], at[:, :], 1.0, None, ALU.add))
                    chain(dve.reciprocal(best[0][:, :], total[:, :]))
                    chain(dve.tensor_tensor(best[1][:, :], best[0][:, :], at[:, :], ALU.mult))
                for r in range(2):
                    chain(dve.tensor_tensor(hot[r][:, :, :], hot[r][:, :, :], over(best[r]), ALU.mult))
                dve.tensor_tensor(comb[:, :, :], hot[0][:, :, :], hot[1][:, :, :], ALU.add).then_inc(combined, 1)
                for k in range(AHEAD):
                    dve.wait_ge(units.high_ready, k + 1)
                    split_low(dve, units, k)


def capacity(nc, comb, comb_dram, rows, held):
    E = FFN[1][1]
    PER = 3 * NP - 1
    with ExitStack() as ctx:
        sb, ps, sem = alloc(nc, ctx)
        before = sb("cap_before", [PT, 2, NP, N], BF16)
        tied = sb("cap_tied", [PT, 2, NP, PT], BF16)
        later = held["later"]
        ones = sb("cap_ones", [PT, 128], BF16)
        rank = ps("cap_rank", [128, 4, BANK])
        ones_ready = sem("cap_ones_ready")
        loaded = [sem(f"cap_row_loaded{k}") for k in range(2)]
        compared = sem("cap_compared")
        ranked = sem("cap_ranked")
        masked = sem("cap_masked")

        with nc.Block() as block:
            @block.sync
            def _(sp):
                def body(i, again):
                    for k in range(2):
                        if again:
                            sp.wait_ge(loaded[k], 16 * i)
                        src = bass.AP(comb_dram.tensor, (2 * i + k) * N, [[0, 128], [1, N]])
                        sp.dma_start(rows[:, bass.ds(1 + 2 * i + k, 1), :].rearrange("p a n -> p (a n)"),
                                     src).then_inc(loaded[k], 16)
                body(0, False)
                with sp.Fori(1, E // 2) as i:
                    body(i, True)

            @block.gpsimd
            def _(pool):
                pool.memset(ones[:, :], 1.0).then_inc(ones_ready, 1)
                pool.memset(rows[:, 0:1, :], 1.0).then_inc(ones_ready, 1)

            @block.vector
            def _(dve):
                def mask(e, k):
                    row = rows[:, bass.ds(1 + e, 1), :].rearrange("p a n -> p (a n)")
                    dve.wait_ge(ranked, e + 1)
                    for half in range(2):
                        cols = slice(half * HALF, (half + 1) * HALF)
                        dve.scalar_tensor_tensor(row[:, cols], rank[:, 2 * k + half, 0:HALF], float(CAPACITY),
                                                 row[:, cols], ALU.is_lt, ALU.mult).then_inc(masked, 1)

                def body(i, again):
                    for k in range(2):
                        e = 2 * i + k
                        row = rows[0:PT, bass.ds(1 + e, 1), :].rearrange("p a n -> p (a n)")
                        dve.wait_ge(loaded[k], 16 * i + 16)
                        if again:
                            dve.wait_ge(ranked, e - 1)
                        for j in range(NP):
                            own = comb[:, j, bass.ds(e, 1)]
                            end = (j + 1) * PT
                            dve.tensor_scalar(before[:, k, j, 0:end], row[:, 0:end], own, None, ALU.is_lt).then_inc(compared, 1)
                            if end < N:
                                dve.tensor_scalar(before[:, k, j, end:N], row[:, end:N], own, None, ALU.is_le).then_inc(compared, 1)
                            dve.scalar_tensor_tensor(tied[:, k, j, :], row[:, end - PT:end], own, later[:, :],
                                                     ALU.is_equal, ALU.mult).then_inc(compared, 1)
                        if again or k == 1:
                            mask(2 * i + k - 1, 1 - k)
                body(0, False)
                with dve.Fori(1, E // 2) as i:
                    body(i, True)
                mask(E - 1, 1)

            @block.tensor
            def _(pe):
                pe.wait_ge(ones_ready, 1)

                def body(i, again):
                    for k in range(2):
                        e = 2 * i + k
                        if again:
                            pe.wait_ge(masked, 2 * (e - 1))
                        for half in range(2):
                            for j in range(NP):
                                if half == 0:
                                    pe.wait_ge(compared, PER * e + min(3 * j + 3, PER))
                                pe.matmul(rank[:, 2 * k + half, 0:HALF], lhsT=ones[:, :],
                                          rhs=before[:, k, j, half * HALF:(half + 1) * HALF],
                                          start=(j == 0), stop=False, skip_group_check=True)
                            for q in range(NP // 2):
                                mm = pe.matmul(rank[:, 2 * k + half, q * PT:(q + 1) * PT], lhsT=ones[:, :],
                                               rhs=tied[:, k, half * (NP // 2) + q, :],
                                               start=False, stop=True, skip_group_check=True)
                        mm.then_inc(ranked, 1)
                body(0, False)
                with pe.Fori(1, E // 2) as i:
                    body(i, True)


def experts(nc, I, layer, h, split, weights_dram, ring_of_units, held, const, norm, rows=None):
    shared, E, upe, M, per_body = FFN[layer]
    p = f"ffn{layer}"
    ring = upe * per_body
    units = shared + E * upe
    bodies = units // ring
    plain = shared // upe
    S = 2 * ring
    rest = D - 128
    WG, WR, WD = 0, 2 * M, 4 * M
    WEND = WD + D
    ALPHA, LIMIT = 1.702, 7.0
    GU = SPLIT * SPLIT
    clamped = layer == 2
    lag = 3
    ident = const["ident"]
    with ExitStack() as ctx:
        sb, ps, sem = alloc(nc, ctx)
        w_high, w_low = ring_of_units.high, ring_of_units.low
        w_high_ready, w_low_ready = ring_of_units.high_ready, ring_of_units.low_ready
        given = rows is not None
        if not given:
            rows = sb(p + "_rows", [128, plain + E, N])
        silu = sb(p + "_silu", [M, 2, HALF])
        up = sb(p + "_up", [M, 2, HALF])
        inner = sb(p + "_inner", [M, 4, HALF])
        high = sb(p + "_inner_high", [M, 4, HALF], F16)
        low = sb(p + "_inner_low", [M, 4, HALF], F16)
        yT = sb(p + "_yT", [128, 3, HALF])
        gu_ps = ps(p + "_gu_ps", [128, 4, BANK])
        y_ps = ps(p + "_y_ps", [128, 3, BANK])
        rows_loaded = sem(p + "_rows_loaded")
        rows_set = sem(p + "_rows_set")
        gu = sem(p + "_gate_up_ready")
        taken = sem(p + "_gate_up_taken")
        silued = sem(p + "_silu_ready")
        product = sem(p + "_product_ready")
        ready = sem(p + "_inner_ready")
        high_ready = sem(p + "_inner_high_ready")
        low_ready = sem(p + "_inner_low_ready")
        downed = sem(p + "_down_done")
        kept = sem(p + "_yT_kept")
        turned = sem(p + "_y_ready")
        added = sem(p + "_added")
        if clamped:
            gate = sb(p + "_gate", [M, 2, HALF])
            ubias, dbias = held["ffn2_ubias"], held["ffn2_dbias"]
            combT = sb(p + "_combT", [E, N])
            small = sem(p + "_small_loaded")
            first_rows_loaded = sem(p + "_first_rows_loaded")
            scaled = sem(p + "_biases_scaled")
            gated = sem(p + "_gate_clamped")
            upped = sem(p + "_up_clamped")
        with nc.Block() as block:
            @block.sync
            def _(sp):
                if clamped:
                    sp.dma_start(combT[:, :], weights_dram).then_inc(small, 16)
                    sp.dma_start(rows[:, 0:per_body, :].rearrange("p e n -> p (e n)"),
                                 bass.AP(weights_dram.tensor, 0, [[0, 128], [1, per_body * N]])).then_inc(first_rows_loaded, 16)
                    sp.dma_start(rows[:, per_body:, :].rearrange("p e n -> p (e n)"),
                                 bass.AP(weights_dram.tensor, per_body * N, [[0, 128], [1, (E - per_body) * N]])
                                 ).then_inc(rows_loaded, 16)
                if not clamped and not given:
                    sp.dma_start(rows[:, plain:, :].rearrange("p e n -> p (e n)"),
                                 bass.AP(weights_dram.tensor, 0, [[0, 128], [1, E * N]])).then_inc(rows_loaded, 16)
                with sp.Fori(1, bodies) as i:
                    for k in range(ring):
                        sp.wait_ge(w_low_ready, (i - 1) * ring + k + 1)
                        load_unit(sp, I, layer, ring_of_units, i, k)

            @block.gpsimd
            def _(pool):
                if plain and not given:
                    pool.memset(rows[:, 0:plain, :], 1.0).then_inc(rows_set, 1)
                if clamped:
                    pool.tensor_scalar(ubias[:, :, :], ubias[:, :, :], GU, None, ALU.mult).then_inc(scaled, 1)
                    pool.tensor_scalar(dbias[:, :], dbias[:, :], SPLIT, None, ALU.mult).then_inc(scaled, 1)

                def keep_low(i, n):
                    pool.wait_ge(high_ready, i * S + n + 1)
                    pool.tensor_tensor(low[:, n % 4, :], inner[:, n % 4, :], high[:, n % 4, :],
                                       ALU.subtract).then_inc(low_ready, 1)

                with pool.Fori(0, bodies) as i:
                    for n in range(S):
                        keep_low(i, n)
                roots_on_pool(pool, norm, const["power"], 0)

            @block.tensor
            def _(pe):
                def gate_up(i, n):
                    k, half = n // 2, n % 2
                    cols = slice(half * HALF, (half + 1) * HALF)
                    for m in range(2):
                        out = gu_ps[0:M, 2 * half + m, 0:HALF]
                        first, second = slice(WG + m * M, WG + (m + 1) * M), slice(WR + m * M, WR + (m + 1) * M)
                        pe.matmul(out, lhsT=w_high[:, k, first], rhs=split[0][:, cols], start=True, stop=False)
                        pe.matmul(out, lhsT=w_high[:, k, first], rhs=split[2][:, cols], start=False, stop=False)
                        pe.matmul(out, lhsT=w_low[:, k, first], rhs=split[0][:, cols], start=False, stop=False)
                        pe.matmul(out, lhsT=w_high[:, k, second], rhs=split[1][:, cols], start=False, stop=False)
                    for m in range(2):
                        rows_of = slice(m * rest, (m + 1) * rest)
                        mm = pe.matmul(gu_ps[0:M, 2 * half + m, 0:HALF], lhsT=w_low[rows_of, k, WR + m * M:WR + (m + 1) * M],
                                       rhs=split[3 if m else 1][rows_of, cols], start=False, stop=True)
                    mm.then_inc(gu, 1)

                def down(i, n, start=False, stop=False):
                    k, half = n // 2, n % 2
                    pe.wait_ge(low_ready, i * S + n + 1)
                    def add(out, cols, m):
                        pe.matmul(out, lhsT=w_high[0:M, k, cols], rhs=high[:, m, :], start=start, stop=False, skip_group_check=True)
                        pe.matmul(out, lhsT=w_high[0:M, k, cols], rhs=low[:, m, :], start=False, stop=False, skip_group_check=True)
                        return pe.matmul(out, lhsT=w_low[0:M, k, cols], rhs=high[:, m, :], start=False, stop=stop, skip_group_check=True)
                    mm = add(y_ps[:, half, 0:HALF], slice(WD, WD + 128), n % 4)
                    if half:
                        for part in range(3):
                            for both in range(2):
                                m = (n - 1 + both) % 4
                                mm = pe.matmul(y_ps[both * rest:(both + 1) * rest, 2, 0:HALF],
                                               lhsT=(w_low if part == 2 else w_high)[0:M, k, WD + 128:WEND],
                                               rhs=(low if part == 1 else high)[:, m, :], start=start and part == 0,
                                               stop=stop and part == 2, skip_group_check=True)
                    mm.then_inc(downed, 1)

                def body(i, again):
                    for n in range(S):
                        if n % 2 == 0:
                            pe.wait_ge(w_low_ready, i * ring + n // 2 + 1)
                        if again or n >= 2:
                            pe.wait_ge(taken, i * S + n - 1)
                        gate_up(i, n)
                        if clamped and not again and n == 1:
                            pe.wait_ge(scaled, 2)
                            pe.wait_ge(small, 16)
                            for half in range(2):
                                cols = slice(half * HALF, (half + 1) * HALF)
                                pe.matmul(y_ps[:, half, 0:HALF], lhsT=dbias[:, 0:128], rhs=combT[:, cols],
                                          start=True, stop=False, skip_group_check=True)
                                pe.matmul(y_ps[half * rest:(half + 1) * rest, 2, 0:HALF], lhsT=dbias[:, 128:D],
                                          rhs=combT[:, cols], start=True, stop=False, skip_group_check=True)
                        if n >= lag:
                            down(i, n - lag, start=not again and not clamped and n < lag + 2)
                        elif again:
                            down(i - 1, S + n - lag)
                body(0, False)
                with pe.Fori(1, bodies) as i:
                    body(i, True)
                for n in range(S - lag, S):
                    down(bodies - 1, n, stop=n >= S - 2)
                for j in range(NP):
                    half, q = j // (NP // 2), j % (NP // 2)
                    if q == 0:
                        pe.wait_ge(kept, half + 2)
                    out = gu_ps[0:PT, j // 2, (j % 2) * D:(j % 2 + 1) * D]
                    part = slice(half * rest, (half + 1) * rest)
                    pe.transpose(out[:, 0:128], yT[:, half, q * PT:(q + 1) * PT], ident[:, :])
                    mm = pe.transpose(out[:, 128:D], yT[part, 2, q * PT:(q + 1) * PT], ident[part, part])
                    mm.then_inc(turned, 1)

            @block.scalar
            def _(act):
                def split_unit(i, k, again):
                    act.wait_ge(ring_of_units.loaded[k], 16 * i + 16)
                    if again:
                        act.wait_ge(downed, (i - 1) * S + 2 * k + 2)
                    split_high(act, ring_of_units, k)

                def keep_high(i, n, again):
                    act.wait_ge(ready, i * S + n + 1)
                    if again or n >= 4:
                        act.wait_ge(downed, i * S + n - 3 + (n % 2 == 0))
                    act.activation(high[:, n % 4, :], inner[:, n % 4, :], ACT.Copy).then_inc(high_ready, 1)

                def body(i, again, more):
                    for n in range(S):
                        k, half = n // 2, n % 2
                        s = i * S + n
                        if clamped:
                            act.wait_ge(gated, s + 1)
                            act.activation(silu[:, half, :], gate[:, half, :], ACT.Silu, scale=ALPHA / GU).then_inc(silued, 1)
                        else:
                            act.wait_ge(gu, s + 1)
                            act.activation(silu[:, half, :], gu_ps[0:M, 2 * half, 0:HALF], ACT.Silu,
                                           scale=1.0 / GU).then_inc(silued, 1)
                        if n:
                            keep_high(i, n - 1, again)
                        elif again:
                            keep_high(i - 1, S - 1, True)
                        if half == 0:
                            if k + AHEAD < ring:
                                split_unit(i, k + AHEAD, again)
                            elif more:
                                split_unit(i + 1, k + AHEAD - ring, True)
                body(0, False, True)
                with act.Fori(1, bodies - 1) as i:
                    body(i, True, True)
                body(bodies - 1, True, False)
                keep_high(bodies - 1, S - 1, True)
                act.wait_ge(downed, bodies * S)
                for bank in (2, 0, 1):
                    act.activation(yT[:, bank, :], y_ps[:, bank, 0:HALF], ACT.Copy, scale=1.0 / SPLIT).then_inc(kept, 1)

            @block.vector
            def _(dve):
                def split_unit(i, k, again):
                    dve.wait_ge(w_high_ready, i * ring + k + 1)
                    split_low(dve, ring_of_units, k)

                def take_gate(i, n, again):
                    k, half = n // 2, n % 2
                    s = i * S + n
                    u = bass.ds(i * ring + k, 1)
                    dve.wait_ge(gu, s + 1)
                    if again or n >= 2:
                        dve.wait_ge(silued, s - 1)
                    dve.tensor_scalar(gate[:, half, :], gu_ps[0:M, 2 * half, 0:HALF], ubias[:, u, 0], LIMIT * GU,
                                      ALU.add, ALU.min).then_inc(gated, 1)

                def take_up(i, n, again):
                    k, half = n // 2, n % 2
                    u = bass.ds(i * ring + k, 1)
                    if again or n >= 2:
                        dve.wait_ge(ready, i * S + n - 1)
                    dve.tensor_scalar(up[:, half, :], gu_ps[0:M, 2 * half + 1, 0:HALF], ubias[:, u, 1], LIMIT * GU,
                                      ALU.add, ALU.min).then_inc(taken, 1)

                def body(i, again, more):
                    for n in range(S):
                        k, half = n // 2, n % 2
                        s = i * S + n
                        cols = slice(half * HALF, (half + 1) * HALF)
                        if clamped:
                            after = (i, n + 1, again) if n + 1 < S else (i + 1, 0, True)
                            dve.wait_ge(taken, s + 1)
                            dve.tensor_scalar(up[:, half, :], up[:, half, :], -LIMIT * GU, GU, ALU.max, ALU.add).then_inc(upped, 1)
                            if more or n + 1 < S:
                                take_gate(*after)
                            dve.wait_ge(silued, s + 1)
                            dve.wait_ge(upped, s + 1)
                            dve.scalar_tensor_tensor(up[:, half, :], silu[:, half, :], 1.0 / (ALPHA * GU), up[:, half, :],
                                                     ALU.mult, ALU.mult).then_inc(product, 1)
                            if more or n + 1 < S:
                                take_up(*after)
                            dve.wait_ge(product, s + 1)
                        else:
                            dve.wait_ge(gu, s + 1)
                            dve.wait_ge(silued, s + 1)
                            dve.scalar_tensor_tensor(up[:, half, :], gu_ps[0:M, 2 * half + 1, 0:HALF], 1.0 / GU, silu[:, half, :],
                                                     ALU.mult, ALU.mult).then_inc(taken, 1)
                            dve.wait_ge(taken, s + 1)
                        row = rows[0:M, bass.ds(i * per_body + k // upe, 1), cols].rearrange("p a n -> p (a n)")
                        if again or n >= 4:
                            dve.wait_ge(low_ready, s - 3)
                        dve.tensor_tensor(inner[:, n % 4, :], up[:, half, :], row, ALU.mult).then_inc(ready, 1)
                        if half == 0:
                            if k + AHEAD < ring:
                                split_unit(i, k + AHEAD, again)
                            elif more:
                                split_unit(i + 1, k + AHEAD - ring, True)
                if plain and not given:
                    dve.wait_ge(rows_set, 1)
                if clamped:
                    dve.wait_ge(scaled, 2)
                if clamped:
                    take_gate(0, 0, False)
                    take_up(0, 0, False)
                    dve.wait_ge(first_rows_loaded, 16)
                body(0, False, True)
                if not given:
                    dve.wait_ge(rows_loaded, 16)
                with dve.Fori(1, bodies - 1) as i:
                    body(i, True, True)
                body(bodies - 1, True, False)
                for q in range(NP // 2):
                    dve.wait_ge(turned, 2 * q + 2)
                    dve.tensor_tensor(h[:, 2 * q:2 * q + 2, :], h[:, 2 * q:2 * q + 2, :],
                                      gu_ps[0:PT, q, 0:2 * D].rearrange("p (a d) -> p a d", a=2), ALU.add).then_inc(added, 1)
                    for j in (2 * q, 2 * q + 1):
                        pair_stats(dve, h, norm, j, added, q + 1)
                    if q == NP // 4 - 1:
                        aggregate(dve, norm, 0)


def ternary_attention(nc, h, hT, const, held, norm):
    identb = const["identb"]
    with ExitStack() as ctx:
        sb, ps, sem = alloc(nc, ctx)
        W3 = 3 * D
        qT = sb("ta_qT", [C, 2, N], BF16)
        kT = sb("ta_kT", [C, 2, N], BF16)
        tern = sb("ta_tern", [PT, NP, W3], BF16)
        means = sb("ta_means", [128, 3])
        limit = sb("ta_limit", [128, 1])
        out_scale = sb("ta_out_scale", [128, 1])
        ones = const["ones"]

        with ExitStack() as pre:
            psb, pps, psem = alloc(nc, pre)
            wt, ws = held["ta_w"], const["ta_ws"]
            qkv = psb("ta_qkv", [PT, NP, W3])
            lower = psb("ta_lower", [PT, NP, D], BF16)
            norm1 = psb("ta_norm1", [PT, NP, 3 * H])
            inverse = psb("ta_inverse", [PT, NP, 3 * H])
            sums = psb("ta_sums", [PT, NP, 3])
            lims = psb("ta_lims", [128, 2, 3])
            acc = pps("ta_acc", [128, 4, BANK])
            stat = pps("ta_stat", [128, BANK])
            trans = pps("ta_trans", [128, 2, 2 * BANK], BF16)
            stat_ready = psem("ta_mean_sums_ready")
            projected = psem("ta_projected")
            copied = psem("ta_projection_copied")
            normed = psem("ta_norm_step")
            length_ready = psem("ta_head_lengths_ready")
            inverted = psem("ta_inverse_lengths_ready")
            divided_by_pool = psem("ta_divided_by_pool")
            divided_by_dve = psem("ta_divided_by_dve")
            mstep = psem("ta_mean_step")
            tready = psem("ta_ternary_ready")
            turned = psem("ta_transposed")
            tcopied = psem("ta_transposed_copied")
            ON_POOL = NP // 2 + 1

            def divide(engine, j, done):
                heads = qkv[:, j, :].rearrange("p (h d) -> p h d", d=HD)
                engine.tensor_tensor(heads, heads, inverse[:, j, :].unsqueeze(2).to_broadcast([PT, 3 * H, HD]),
                                     ALU.mult).then_inc(done, 1)

            with nc.Block() as block:
                @block.gpsimd
                def _(pool):
                    for j in range(ON_POOL):
                        pool.wait_ge(inverted, j // (NP // 2) + 1)
                        divide(pool, j, divided_by_pool)

                @block.tensor
                def _(pe):
                    for j in range(NP):
                        if j >= 2:
                            pe.wait_ge(copied, 2 * (j - 1))
                        for part in range(2):
                            for c in range(2):
                                mm = pe.matmul(acc[0:PT, 2 * (j % 2) + part, 0:W3 // 2], lhsT=hT[:, c, j * PT:(j + 1) * PT],
                                               rhs=wt[:, c, part * (W3 // 2):(part + 1) * (W3 // 2)],
                                               start=(c == 0), stop=(c == 1))
                            mm.then_inc(projected, 1)
                    pe.wait_ge(normed, 6)
                    pe.matmul(stat[:, 0:3 * NP], lhsT=ones[0:PT, :], rhs=sums[:, :, :].rearrange("p j a -> p (j a)"),
                              start=True, stop=True).then_inc(stat_ready, 1)
                    for a in range(2):
                        pe.wait_ge(tready, a + 1)
                        for c in range(2):
                            if a:
                                pe.wait_ge(tcopied, c + 1)
                            for j in range(NP):
                                mm = pe.transpose(trans[0:C, c, j * PT:(j + 1) * PT],
                                                  tern[:, j, a * D + c * C:a * D + (c + 1) * C], identb[0:PT, 0:PT])
                            mm.then_inc(turned, 1)

                @block.scalar
                def _(act):
                    for j in range(NP):
                        for part in range(2):
                            act.wait_ge(projected, 2 * j + part + 1)
                            act.activation(qkv[:, j, part * (W3 // 2):(part + 1) * (W3 // 2)],
                                           acc[0:PT, 2 * (j % 2) + part, 0:W3 // 2], ACT.Copy,
                                           scale=ws[0:PT, 0:1]).then_inc(copied, 1)
                    for a in range(2):
                        for c in range(2):
                            act.wait_ge(turned, 2 * a + c + 1)
                            act.activation((qT, kT)[a][:, c, :], trans[0:C, c, 0:N], ACT.Copy).then_inc(tcopied, 1)

                @block.vector
                def _(dve):
                    for half in range(2):
                        pairs = slice(half * (NP // 2), (half + 1) * (NP // 2))
                        for j in range(half * (NP // 2), (half + 1) * (NP // 2)):
                            dve.wait_ge(copied, 2 * j + 2)
                            dve.tensor_reduce(norm1[:, j, :], qkv[:, j, :].rearrange("p (h d) -> p h d", d=HD), AX.X, ALU.add,
                                              apply_absolute_value=True).then_inc(length_ready, 1)
                        dve.wait_ge(length_ready, (half + 1) * (NP // 2))
                        dve.tensor_scalar(inverse[:, pairs, :], norm1[:, pairs, :], TERNARY_EPS, None, ALU.add).then_inc(normed, 1)
                        dve.wait_ge(normed, 3 * half + 1)
                        dve.reciprocal(inverse[:, pairs, :], inverse[:, pairs, :]).then_inc(inverted, 1)
                        dve.wait_ge(inverted, half + 1)
                        dve.tensor_tensor(norm1[:, pairs, :], norm1[:, pairs, :], inverse[:, pairs, :], ALU.mult).then_inc(normed, 1)
                        dve.wait_ge(normed, 3 * half + 2)
                        dve.tensor_reduce(sums[:, pairs, :], norm1[:, pairs, :].rearrange("p j (a h) -> p j a h", a=3),
                                          AX.X, ALU.add).then_inc(normed, 1)
                    for j in range(ON_POOL, NP):
                        divide(dve, j, divided_by_dve)
                    dve.wait_ge(stat_ready, 1)
                    dve.tensor_reduce(means[:, :], stat[:, 0:3 * NP].rearrange("p (j a) -> p a j", a=3), AX.X,
                                      ALU.add).then_inc(mstep, 1)
                    dve.wait_ge(mstep, 1)
                    dve.tensor_scalar(means[:, :], means[:, :], 1.0 / (N * D), TERNARY_EPS, ALU.mult, ALU.add).then_inc(mstep, 1)
                    dve.wait_ge(mstep, 2)
                    dve.tensor_scalar(lims[:, 0, :], means[:, :], 0.5, None, ALU.mult).then_inc(mstep, 1)
                    dve.tensor_scalar(lims[:, 1, :], means[:, :], -0.5, None, ALU.mult).then_inc(mstep, 1)
                    dve.wait_ge(mstep, 4)
                    dve.wait_ge(divided_by_dve, NP - ON_POOL)
                    dve.wait_ge(divided_by_pool, ON_POOL)
                    for a in range(3):
                        part = qkv[:, :, a * D:(a + 1) * D]
                        if a:
                            dve.wait_ge(tready, a)
                        dve.tensor_scalar(lower[:, :, :], part, lims[0:PT, 1, a:a + 1], None, ALU.is_lt).then_inc(mstep, 1)
                        dve.wait_ge(mstep, 5 + a)
                        dve.scalar_tensor_tensor(tern[:, :, a * D:(a + 1) * D], part, lims[0:PT, 0, a:a + 1],
                                                 lower[:, :, :], ALU.is_gt, ALU.subtract).then_inc(tready, 1)

        with ExitStack() as main:
            msb, mps, msem = alloc(nc, main)
            q_stage = msb("ta_q_stage", [C, 2, 2, PT], BF16)
            k_blocks = msb("ta_k_blocks", [C, 2, 2, 2, HC, T], BF16)
            dots = msb("ta_dots", [SR, NP, H * T], BF16)
            dsum = msb("ta_dsum", [SR, NP])
            dtot = msb("ta_dtot", [SR, 1])
            mean = msb("ta_mean", [128, 1])
            unit = msb("ta_unit", [128, 1])
            score_s = msb("ta_score_s", [128, 1])
            nlimit = msb("ta_nlimit", [128, 1])
            inv = msb("ta_inv", [128, 1])
            lower = msb("ta_dots_lower", [SR, 2, H * T], BF16)
            probs = msb("ta_probs", [SR, 2, H * T], BF16)
            probsT = msb("ta_probsT", [GK, 2, G, SR], BF16)
            v_blocks = msb("ta_v_blocks", [GK, 2, 2, D], BF16)
            oT = msb("ta_oT", [GD, 2, G, PT], BF16)
            s_ps = mps("ta_s", [128, 2, BANK])
            staged = msem("ta_keys_staged_by_pool")
            staged_too = msem("ta_keys_staged_by_dve")
            q_staged = msem("ta_queries_staged")
            cleared = msem("ta_banks_cleared")
            scores = msem("ta_scores_ready")
            dotted = msem("ta_dots_kept")
            sstep = msem("ta_scalar_step")
            total = msem("ta_total_ready")

            def stage_k(engine, j, k, c, done):
                engine.tensor_tensor(k_blocks[:, k, c, :, :, :],
                                     kT[:, c, bass.ds(j * PT, PT)].rearrange("p (b t) -> p b t", b=2)
                                     .unsqueeze(2).to_broadcast([C, 2, HC, T]),
                                     const["own_head"][:, :].unsqueeze(1).unsqueeze(3)
                                     .to_broadcast([C, 2, HC, T]), ALU.mult).then_inc(done, 1)

            with nc.Block() as block:
                @block.gpsimd
                def _(pool):
                    def body(i, later):
                        for k in range(2):
                            j = 2 * i + k
                            if later:
                                pool.wait_ge(scores, j - 1)
                            stage_k(pool, j, k, 0, staged)
                    body(0, False)
                    with pool.Fori(1, NP // 2) as i:
                        body(i, True)

                @block.scalar
                def _(act):
                    def body(i, later):
                        for k in range(2):
                            j = 2 * i + k
                            if later:
                                act.wait_ge(scores, j - 1)
                            act.activation(q_stage[:, k, :, :], qT[:, :, bass.ds(j * PT, PT)], ACT.Copy).then_inc(q_staged, 1)
                    body(0, False)
                    with act.Fori(1, NP // 2) as i:
                        body(i, True)

                @block.tensor
                def _(pe):
                    pe.wait_ge(cleared, 1)

                    def body(i, later):
                        for k in range(2):
                            j = 2 * i + k
                            pe.wait_ge(q_staged, j + 1)
                            pe.wait_ge(staged, j + 1)
                            pe.wait_ge(staged_too, j + 1)
                            if later:
                                pe.wait_ge(dotted, j - 1)
                            for c in range(2):
                                for img in range(2):
                                    mm = pe.matmul(s_ps[img * SECOND:img * SECOND + T, k, c * HC * T:(c + 1) * HC * T],
                                                   lhsT=q_stage[:, k, c, img * T:(img + 1) * T],
                                                   rhs=k_blocks[:, k, c, img, :, :].rearrange("p a t -> p (a t)"),
                                                   start=True, stop=True)
                            mm.then_inc(scores, 1)
                    body(0, False)
                    with pe.Fori(1, NP // 2) as i:
                        body(i, True)
                    pe.wait_ge(sstep, 1)
                    pe.matmul(s_ps[:, 0, 0:1], lhsT=ones[0:SR, :], rhs=dtot[:, :], start=True, stop=True).then_inc(total, 1)

                @block.vector
                def _(dve):
                    dve.memset(s_ps[:, :, :], 0.0).then_inc(cleared, 1)

                    def body(i, later, more):
                        for k in range(2):
                            j = 2 * i + k
                            if more or k == 0:
                                if later or k == 1:
                                    dve.wait_ge(scores, j)
                                stage_k(dve, j + 1, 1 - k, 1, staged_too)
                            dve.wait_ge(scores, j + 1)
                            dve.tensor_reduce(dsum[:, bass.ds(j, 1)], s_ps[0:SR, k, 0:H * T], AX.X, ALU.add,
                                              apply_absolute_value=True)
                            dve.tensor_copy(dots[:, bass.ds(j, 1), :].rearrange("p a n -> p (a n)"),
                                            s_ps[0:SR, k, 0:H * T]).then_inc(dotted, 1)
                    stage_k(dve, 0, 0, 1, staged_too)
                    body(0, False, True)
                    with dve.Fori(1, NP // 2 - 1) as i:
                        body(i, True, True)
                    body(NP // 2 - 1, True, False)
                    dve.wait_ge(dotted, NP)
                    dve.tensor_reduce(dtot[:, :], dsum[:, :], AX.X, ALU.add).then_inc(sstep, 1)
                    dve.wait_ge(total, 1)
                    dve.tensor_scalar(mean[:, :], s_ps[:, 0, 0:1], 1.0 / (B * H * T * T), None, ALU.mult).then_inc(sstep, 1)
                    dve.scalar_tensor_tensor(unit[:, :], means[:, 0:1], SCALE, means[:, 1:2], ALU.mult, ALU.mult).then_inc(sstep, 1)
                    dve.wait_ge(sstep, 3)
                    dve.tensor_tensor(score_s[:, :], mean[:, :], unit[:, :], ALU.mult).then_inc(sstep, 1)
                    dve.wait_ge(sstep, 4)
                    dve.tensor_scalar(score_s[:, :], score_s[:, :], TERNARY_EPS, None, ALU.add).then_inc(sstep, 1)
                    dve.reciprocal(inv[:, :], unit[:, :]).then_inc(sstep, 1)
                    dve.wait_ge(sstep, 6)
                    dve.scalar_tensor_tensor(limit[:, :], score_s[:, :], 0.5, inv[:, :], ALU.mult, ALU.mult).then_inc(sstep, 1)
                    dve.tensor_tensor(out_scale[:, :], score_s[:, :], means[:, 2:3], ALU.mult).then_inc(sstep, 1)
                    dve.wait_ge(sstep, 8)
                    dve.tensor_scalar(nlimit[:, :], limit[:, :], -1.0, None, ALU.mult).then_inc(sstep, 1)

            t_ps = mps("ta_t", [128, 2, 2 * BANK], BF16)
            v_ps = mps("ta_v", [128, 2, BANK])
            oy_ps = mps("ta_oy", [128, 2, BANK])
            under = msem("ta_under")
            rounded = msem("ta_rounded")
            values = msem("ta_values_ready")
            v_ready = msem("ta_v_blocks_ready")
            turned_s = msem("ta_roundedT_ready")
            pT_copied = msem("ta_roundedT_copied")
            o_ready = msem("ta_outputs_ready")
            o_copied = msem("ta_outputs_copied")
            y_ready = msem("ta_token_major_ready")
            added = msem("ta_added")

            def y_of(k):
                return oy_ps[0:PT, k, G * PT:G * PT + D]

            with nc.Block() as block:
                @block.gpsimd
                def _(pool):
                    roots_on_pool(pool, norm, const["power"], 0)

                @block.tensor
                def _(pe):
                    def value(i, k, later):
                        j = 2 * i + k
                        if later:
                            pe.wait_ge(v_ready, j - 1)
                        for img in range(2):
                            mm = pe.matmul(v_ps[0:GK, k, img * D:(img + 1) * D], lhsT=const["copy_keys"][:, img, :],
                                           rhs=tern[:, bass.ds(j, 1), 2 * D:3 * D].rearrange("p a d -> p (a d)"),
                                           start=True, stop=True)
                        mm.then_inc(values, 1)

                    def body(i, later, more):
                        for k in range(2):
                            t = 2 * i + k
                            pe.wait_ge(rounded, t + 1)
                            if later:
                                pe.wait_ge(pT_copied, t - 1)
                            for g in range(G):
                                mm = pe.transpose(t_ps[0:GK, k, g * 128:g * 128 + SR],
                                                  probs[:, k, g * GK:(g + 1) * GK], identb[0:SR, 0:SR])
                            mm.then_inc(turned_s, 1)
                            if more:
                                value(i + 1, k, True)
                            pe.wait_ge(pT_copied, t + 1)
                            pe.wait_ge(v_ready, t + 1)
                            if later:
                                pe.wait_ge(added, t - 1)
                            for img in range(2):
                                for g in range(G):
                                    mm = pe.matmul(oy_ps[0:GD, k, g * PT + img * T:g * PT + (img + 1) * T],
                                                   lhsT=v_blocks[:, k, img, g * GD:(g + 1) * GD],
                                                   rhs=probsT[:, k, g, img * SECOND:img * SECOND + T],
                                                   start=True, stop=True)
                            mm.then_inc(o_ready, 1)
                            pe.wait_ge(o_copied, t + 1)
                            for g in range(G):
                                mm = pe.matmul(y_of(k), lhsT=oT[:, k, g, :], rhs=const["place"][:, g, :],
                                               start=(g == 0), stop=(g == G - 1))
                            mm.then_inc(y_ready, 1)
                    for k in range(2):
                        value(0, k, False)
                    body(0, False, True)
                    with pe.Fori(1, NP // 2 - 1) as i:
                        body(i, True, True)
                    body(NP // 2 - 1, True, False)

                @block.scalar
                def _(act):
                    def body(i, later):
                        for k in range(2):
                            t = 2 * i + k
                            act.wait_ge(turned_s, t + 1)
                            if later:
                                act.wait_ge(o_ready, t - 1)
                            act.activation(probsT[:, k, :, :],
                                           t_ps[0:GK, k, 0:G * 128].rearrange("p (g s) -> p g s", g=G)[:, :, 0:SR],
                                           ACT.Copy).then_inc(pT_copied, 1)
                            act.wait_ge(o_ready, t + 1)
                            if later:
                                act.wait_ge(y_ready, t - 1)
                            act.activation(oT[:, k, :, :].rearrange("p g s -> p (g s)"), oy_ps[0:GD, k, 0:G * PT],
                                           ACT.Copy).then_inc(o_copied, 1)
                    body(0, False)
                    with act.Fori(1, NP // 2) as i:
                        body(i, True)

                @block.vector
                def _(dve):
                    def round_scores(n, k, later):
                        dn = dots[:, bass.ds(n, 1), :].rearrange("p a n -> p (a n)")
                        if later:
                            dve.wait_ge(rounded, n - 1)
                        dve.tensor_scalar(lower[:, k, :], dn, nlimit[0:SR, 0:1], None, ALU.is_lt).then_inc(under, 1)
                        dve.wait_ge(under, n + 1)
                        if later:
                            dve.wait_ge(turned_s, n - 1)
                        dve.scalar_tensor_tensor(probs[:, k, :], dn, limit[0:SR, 0:1], lower[:, k, :],
                                                 ALU.is_gt, ALU.subtract).then_inc(rounded, 1)

                    def value_blocks(n, k, later):
                        dve.wait_ge(values, n + 1)
                        if later:
                            dve.wait_ge(o_ready, n - 1)
                        dve.tensor_tensor(v_blocks[:, k, :, :],
                                          v_ps[0:GK, k, 0:2 * D].rearrange("p (b f) -> p b f", b=2),
                                          const["own_key"][:, :].unsqueeze(1).to_broadcast([GK, 2, D]),
                                          ALU.mult).then_inc(v_ready, 1)

                    def add(t, k):
                        dve.wait_ge(y_ready, t + 1)
                        hj = h[:, bass.ds(t, 1), :].rearrange("p a d -> p (a d)")
                        dve.scalar_tensor_tensor(hj, y_of(k), out_scale[0:PT, 0:1], hj,
                                                 ALU.mult, ALU.add).then_inc(added, 1)
                        pair_stats(dve, h, norm, t, added, t + 1)

                    def body(i, later, more):
                        for k in range(2):
                            t = 2 * i + k
                            if more or k == 0:
                                round_scores(t + 1, 1 - k, later or k == 1)
                                value_blocks(t + 1, 1 - k, later or k == 1)
                            if later or k == 1:
                                add(t - 1, 1 - k)
                    round_scores(0, 0, False)
                    value_blocks(0, 0, False)
                    body(0, False, True)
                    with dve.Fori(1, NP // 2 - 1) as i:
                        body(i, True, True)
                    body(NP // 2 - 1, True, False)
                    aggregate(dve, norm, 0)
                    add(NP - 1, 1)


def tower(nc, I, out, last=8):
    SEMAPHORES.clear()
    with ExitStack() as ctx:
        sb, ps, sem = alloc(nc, ctx)
        h = sb("h", [PT, NP, D])
        hT = sb("hT", [C, 2, N])
        split = [sb(f"split{i}", [128, N], F16) for i in range(4)]
        const = {"ident": sb("ident", [128, 128]), "identb": sb("identb", [128, 128], BF16),
                 "ones": sb("ones", [128, 128]), "power": sb("power", [PT, 2, NP]),
                 "half": sb("half", [C, 2, SP]), "own_head": sb("own_head", [C, HC]),
                 "own_key": sb("own_key", [GK, D]), "copy_keys": sb("copy_keys", [PT, 2, GK], BF16),
                 "place": sb("place", [GD, G, D], BF16), "causal": sb("causal", [SR, H * T], BF16),
                 "ta_ws": sb("ta_ws", [128, 1])}
        raw = {"copy_keys": sb("copy_keys_f", [PT, 2, GK]), "place": sb("place_f", [GD, G, D]),
               "causal": sb("causal_f", [SR, H * T])}
        held = {name: sb("held_" + name, list(I[name].shape)) for name in FIRST_LOADS + LATER_LOADS}
        def store():
            stored = sem("h_stored")
            with nc.Block() as block:
                @block.sync
                def _(sp):
                    sp.dma_start(out.rearrange("(j p) d -> p j d", p=PT), h[:, :, :]).then_inc(stored, 16)
                    sp.wait_ge(stored, 16)

        patch_embedding(nc, I, h, held, const, raw)
        if last == 0:
            return store()
        to_feature_major(nc, h, hT, const["ident"], "tr0")
        n = 0
        for layer in range(4):
            reset_semaphores(nc)
            n += 1
            with ExitStack() as around:
                norm = Norm(nc, around, f"ln{n}")
                unit = around.enter_context(nc.sbuf_tensor("unit", [PT, NP, D], F32)) if layer == 0 else None
                if layer < 3:
                    attention(nc, I, layer, h, hT, const, held, norm)
                else:
                    ternary_attention(nc, h, hT, const, held, norm)
                if layer == 0:
                    layer_norm(nc, h, norm, f"ln{n}", unit, const["power"])
                else:
                    norm_to_feature_major(nc, h, norm, hT, const, f"ln{n}", split)
                if last == n:
                    return store()
                n += 1
                norm = Norm(nc, around, f"ln{n}")
                if layer == 0:
                    to_feature_major(nc, unit, hT, const["ident"], f"tr{n}")
                    soft_mixture(nc, h, unit, hT, const, held, norm)
                else:
                    units = Units(nc, around, layer)
                    rows = (around.enter_context(nc.sbuf_tensor("cap_rows", [128, 1 + FFN[1][1], N], F32))
                            if layer == 1 else None)
                    with nc.sbuf_tensor(f"comb{layer}", [PT, NP, FFN[layer][1]], F32) as comb:
                        router(nc, I, layer, hT, comb, I[f"comb_scratch{layer}"], units, const, held)
                        if layer == 1:
                            capacity(nc, comb, I["comb_scratch1"], rows, held)
                    experts(nc, I, layer, h, split, I[f"comb_scratch{layer}"], units, held, const, norm, rows)
                if layer < 3:
                    norm_to_feature_major(nc, h, norm, hT, const, f"ln{n}")
                else:
                    layer_norm(nc, h, norm, f"ln{n}", None, const["power"])
                if last == n:
                    return store()


def shape_constants():
    f = lambda *s: np.zeros(s, np.float32)
    k = {}
    k["ident"] = np.eye(128, dtype=np.float32)
    own_head = f(C, HC)
    own_head[np.arange(C), np.arange(C) // HD] = 1
    k["own_head"] = own_head
    row, col = np.arange(GK)[:, None] // T, (np.arange(D)[None, :] // HD) % GH
    k["own_key"] = (row == col).astype(np.float32)
    rep = f(PT, 2, GK)
    for img in range(2):
        for a in range(GH):
            rep[img * T + np.arange(T), img, a * T + np.arange(T)] = 1
    k["copy_keys"] = rep
    place = f(GD, G, D)
    for g in range(G):
        place[np.arange(GD), g, g * GD + np.arange(GD)] = 1
    k["place"] = place
    causal = f(SR, H, T)
    for img in range(2):
        causal[img * SECOND:img * SECOND + T] = np.where(np.arange(T)[None, :] > np.arange(T)[:, None], NEG, 0)[:, None, :]
    k["causal"] = causal.reshape(SR, H * T)
    angle = (np.arange(T, dtype=np.float32)[None, :] *
             (1.0 / 10000.0 ** (2.0 * np.arange(HD // 2, dtype=np.float32) / HD)).astype(np.float32)[:, None])
    rope = f(C, 2, T)
    d = np.arange(C) % HD
    rope[:, 0] = np.cos(angle)[d // 2]
    rope[:, 1] = np.sin(angle)[d // 2] * np.where(d % 2, 1, -1)[:, None]
    k["rope"] = rope
    own = f(C, 2, SN, SP)
    for e in range(2):
        own[np.arange(C), e, e * 4 + np.arange(C) // SH] = 1
    k["sm_own_expert"] = own.reshape(C, 2, SLOTS)
    k["sm_own_image"] = (np.arange(PT)[:, None] // T == np.arange(2)).astype(np.float32)
    k["sm_own_image4"] = (2 * np.arange(2)[None, :, None] + (np.arange(PT) // T)[:, None, None] ==
                          np.arange(4)).astype(np.float32)
    for E in (8, 16):
        k[f"order{E}"] = np.tile(np.arange(E, dtype=np.float32), (PT, 1))
    k["later"] = (np.arange(PT)[None, :] > np.arange(PT)[:, None]).astype(np.float32)
    return k


def chunks(a, n=2):
    return a.reshape(n, a.shape[0] // n, a.shape[1]).transpose(1, 0, 2)


def swapped(a):
    return a.reshape(a.shape[:-1] + (-1, 2))[..., ::-1].reshape(a.shape)


def layouts(x):
    P = 16
    k = {}
    gh = 96 // P
    pt = x["x"].reshape(B, 3, gh, P, gh, P).transpose(0, 2, 4, 1, 3, 5).reshape(B, gh * gh, 3 * P * P)
    pt = np.concatenate([np.zeros((B, 1, 3 * P * P), np.float32), pt], 1).reshape(N, -1)
    k["patches"] = chunks(pt.T, 6)
    k["tok_w"] = chunks(x["L0_tok_W"].T, 6)
    k["tok_pos"] = np.tile(x["L0_tok_pos_emb"][0], (2, 1))
    first = np.concatenate([x["L0_tok_cls_tok"][0], np.broadcast_to(x["L0_tok_b"], (T - 1, D))], 0)
    k["tok_first"] = np.tile(first, (2, 1))

    def att(p, wq, wk, wv, wp, bq, bk, bv, bp, rope=False):
        k[p + "_wq"], k[p + "_wk"], k[p + "_wv"] = chunks(wq), chunks(wk), chunks(wv)
        bs = [bq, bk]
        if rope:
            k[p + "_wqs"], k[p + "_wks"] = chunks(swapped(wq)), chunks(swapped(wk))
            bs = [bq, swapped(bq), bk, swapped(bk)]
        k[p + "_bias"] = np.stack([b.reshape(2, C).T for b in bs], 2)
        k[p + "_wp"] = chunks(wp, G)
        k[p + "_bv"] = np.broadcast_to(bv.reshape(G, GD).T[:, :, None], (GD, G, PT))
        k[p + "_bp"] = np.tile(bp, (PT, 1))
    w, b = x["L0_attn_W_attn"], x["L0_attn_b_attn"]
    att("att0", w[:, :D], w[:, D:2 * D], w[:, 2 * D:], x["L0_attn_W_proj"], b[:D], b[D:2 * D], b[2 * D:], x["L0_attn_b_proj"])
    att("att1", x["L1_attn_Wq"].T, x["L1_attn_Wk"].T, x["L1_attn_Wv"].T, x["L1_attn_Wp"].T,
        x["L1_attn_bq"], x["L1_attn_bk"], x["L1_attn_bv"], x["L1_attn_bp"], rope=True)
    w, b = x["L2_attn_qkv_w"].T, x["L2_attn_qkv_b"]
    att("att2", w[:, :D], w[:, D:2 * D], w[:, 2 * D:], x["L2_attn_out_w"].T, b[:D], b[D:2 * D], b[2 * D:], x["L2_attn_out_b"])
    rel = x["L2_attn_rel_pos_emb"][np.clip(np.arange(SHIFTS) - (T - 1), -MAX_REL, MAX_REL) + MAX_REL]
    blocks = np.zeros((C, HC, SHIFTS), np.float32)
    for i in range(HC):
        blocks[i * HD:(i + 1) * HD, i] = rel.T
    k["rel_blocks"] = blocks.reshape(C, -1)
    k["ta_w"] = chunks(x["L3_attn_w_qkv"].T)

    k["sm_slots"] = chunks(x["L0_ffn_slot_params"].reshape(D, SLOTS))
    k["sm_scale"] = np.broadcast_to(x["L0_ffn_scale"].reshape(1, 1), (C, 1))
    k["sm_down"] = chunks(x["L0_ffn_W_down"].transpose(1, 0, 2).reshape(D, SN * SH))
    k["sm_bdown"] = x["L0_ffn_b_down"].reshape(2, C).T
    k["sm_up"] = chunks(x["L0_ffn_W_up"].reshape(SN * SH, D))
    k["sm_bup"] = np.tile(np.repeat(x["L0_ffn_b_up"], SP, 0), (4, 1))

    def units(gate, up, down, M):
        e, inner = gate.shape[0], gate.shape[2]
        n = inner // M
        gu = np.stack([gate.reshape(e, D, n, M), up.reshape(e, D, n, M)], 3).transpose(0, 2, 1, 3, 4).reshape(e * n, D, 2 * M)
        dn = np.zeros((e * n, 128, D), np.float32)
        dn[:, :M] = down.reshape(e * n, M, D)
        return np.concatenate([gu[:, :128], np.concatenate([gu[:, 128:]] * 2, 1), dn], 2)

    def ffn(layer, parts):
        k[f"ffn{layer}_w"] = np.concatenate([units(*q, FFN[layer][3]) for q in parts], 0)
    ffn(1, [(x["L1_ffn_s1"][None], x["L1_ffn_s3"][None], x["L1_ffn_s2"][None]),
            (x["L1_ffn_w1"], x["L1_ffn_w3"], x["L1_ffn_w2"])])
    gu = x["L2_ffn_Wgu"]
    I2 = gu.shape[2] // 2
    ffn(2, [(gu[:, :, :I2], gu[:, :, I2:], x["L2_ffn_Wd"])])
    k["ffn2_ubias"] = x["L2_ffn_bgu"].reshape(8, 2, 2, C).transpose(3, 0, 2, 1).reshape(C, 16, 2)
    k["ffn2_dbias"] = x["L2_ffn_bd"]
    t = lambda a: a.transpose(0, 2, 1)
    ffn(3, [(x["L3_ffn_sw1"].T[None], x["L3_ffn_sw3"].T[None], x["L3_ffn_sw2"].T[None]),
            (t(x["L3_ffn_w1"]), t(x["L3_ffn_w3"]), t(x["L3_ffn_w2"]))])
    k["rt1_w"], k["rt2_w"], k["rt3_w"] = chunks(x["L1_ffn_Wr"]), chunks(x["L2_ffn_Wr"]), chunks(x["L3_ffn_gate_w"].T)
    k["rt2_b"] = np.tile(x["L2_ffn_br"], (PT, 1))
    return k


LAST = 8


def kernel(**inputs):
    import concourse.bacc as _bacc
    from concourse.bass_utils import run_bass_kernel_spmd as _run
    nc = _bacc.Bacc("TRN2", target_bir_lowering=False, num_devices=1)
    arrays = {**layouts({n: np.asarray(a) for n, a in inputs.items()}), **shape_constants()}
    arrays = {f"in_{n}": np.ascontiguousarray(a) for n, a in arrays.items()}
    I = {n[3:]: nc.dram_tensor(n, a.shape, F32, kind="ExternalInput").ap() for n, a in arrays.items()}
    I["rel_scratch"] = nc.dram_tensor("rel_scratch", (N, H * SHIFTS), F32, kind="Internal").ap()
    for layer in (1, 2, 3):
        I[f"comb_scratch{layer}"] = nc.dram_tensor(f"comb_scratch{layer}", (FFN[layer][1], N), F32, kind="Internal").ap()
    out = nc.dram_tensor("out", (N, D), F32, kind="ExternalOutput").ap()
    tower(nc, I, out, LAST)
    got = _run(nc, [arrays], core_ids=[0]).results[0]["out"]
    return got.reshape(B, T, D)
```
